# Optimizing a Trainium2 kernel written in Bass

```python
import numpy as np
import jax
import jax.numpy as jnp

def _softmax(x, axis=-1):
    return jax.nn.softmax(x, axis=axis)

def _gelu(x):
    return jax.nn.gelu(x, approximate=True)

def _silu(x):
    return jax.nn.silu(x)

def _sigmoid(x):
    return jax.nn.sigmoid(x)

def _layernorm(x, axis=-1, eps=1e-05):
    m = jnp.mean(x, axis=axis, keepdims=True)
    v = jnp.var(x, axis=axis, keepdims=True)
    return (x - m) / jnp.sqrt(v + eps)

def _scatter_add(tgt, idx, src, axis=0):
    return tgt.at[idx].add(src)

def _segment_sum(src, seg, n):
    return jax.ops.segment_sum(src, seg, n)
kernel_name = 'mk_hybrid_d1_jaxref_r8_cb97f6'

def setup_inputs(seed: int=0):
    np.random.seed(seed)
    _w = jnp.asarray

    def _L0_attn_a_setup():
        import jax, jax.numpy as jnp
        import numpy as np
        N_HEAD = 16

        def _rope_cos_sin(T, D):
            half = D // 2
            i = jnp.arange(half, dtype=jnp.float32)
            alpha = 1.0 / 10000.0 ** (2.0 * i / D)
            ang = jnp.arange(T, dtype=jnp.float32)[:, None] * alpha
            return (jnp.cos(ang), jnp.sin(ang))

        def _apply_rope(t, cos, sin):
            half = t.shape[-1] // 2
            xr, xi = (t[..., :half], t[..., half:])
            return jnp.concatenate([xr * cos - xi * sin, xr * sin + xi * cos], axis=-1)
        key = jax.random.key(seed)
        ks = jax.random.split(key, 5)
        B, T, C = (4, 256, 128)
        s = 0.02
        x = jax.random.normal(ks[0], (B, T, C), jnp.float32)
        wq = jax.random.normal(ks[1], (C, C), jnp.float32) * s
        wk = jax.random.normal(ks[2], (C, C), jnp.float32) * s
        wv = jax.random.normal(ks[3], (C, C), jnp.float32) * s
        wp = jax.random.normal(ks[4], (C, C), jnp.float32) * s
        zb = jnp.zeros((C,), jnp.float32)
        return {'x': x, 'wq': wq, 'bq': zb, 'wk': wk, 'bk': zb, 'wv': wv, 'bv': zb, 'wp': wp, 'bp': zb}
    _L0_attn_a_in = _L0_attn_a_setup()

    def _L0_attn_b_setup():
        import jax, jax.numpy as jnp
        import numpy as np
        N_HEAD = 16
        MAX_WAVELENGTH = 1250
        ROPE_PCT = 1.0

        def apply_p_rope(inputs, positions, head_dim, max_wavelength=MAX_WAVELENGTH, rope_percentage=ROPE_PCT):
            rope_angles = int(rope_percentage * head_dim // 2)
            nope_angles = head_dim // 2 - rope_angles
            fraction = 2.0 * jnp.arange(0, rope_angles) / head_dim
            timescale = max_wavelength ** fraction
            timescale = jnp.pad(timescale, (0, nope_angles), mode='constant', constant_values=(0, jnp.inf))
            sinusoid_inp = positions[..., None] / timescale[None, :]
            sin = jnp.sin(sinusoid_inp)
            cos = jnp.cos(sinusoid_inp)
            first_half, second_half = jnp.split(inputs, 2, axis=-1)
            first_part = first_half * cos - second_half * sin
            second_part = second_half * cos + first_half * sin
            return jnp.concatenate([first_part, second_part], axis=-1).astype(inputs.dtype)
        key = jax.random.key(seed)
        ks = jax.random.split(key, 4)
        B, T, C = (2, 256, 128)
        x = jax.random.normal(ks[0], (B, T, C), dtype=jnp.float32)
        W_attn = jax.random.normal(ks[1], (C, 3 * C), dtype=jnp.float32) * 0.02
        b_attn = jnp.zeros((3 * C,), dtype=jnp.float32)
        W_proj = jax.random.normal(ks[2], (C, C), dtype=jnp.float32) * 0.02
        b_proj = jnp.zeros((C,), dtype=jnp.float32)
        return {'x': x, 'W_attn': W_attn, 'b_attn': b_attn, 'W_proj': W_proj, 'b_proj': b_proj}
    _L0_attn_b_in = _L0_attn_b_setup()

    def _L0_ffn_setup():
        import jax, jax.numpy as jnp
        import numpy as np
        B, T, D = (4, 256, 128)
        H, DH, E, SEL = (8, 64, 5, 2)

        def _topk_mask(logits, k):
            _, idx = jax.lax.top_k(logits, k)
            return jnp.sum(jax.nn.one_hot(idx, logits.shape[-1], dtype=logits.dtype), axis=-2)
        key = jax.random.key(seed)
        ks = jax.random.split(key, 7)
        s = 0.02
        x = jax.random.normal(ks[0], (B, T, D), dtype=jnp.float32)
        Wq = jax.random.normal(ks[1], (D, H * DH), dtype=jnp.float32) * s
        Wk = jax.random.normal(ks[2], (D, H * DH), dtype=jnp.float32) * s
        Ws = jax.random.normal(ks[3], (D, H * E), dtype=jnp.float32) * s
        Wd = jax.random.normal(ks[4], (D, H * E), dtype=jnp.float32) * s
        Wv = jax.random.normal(ks[5], (E, D, DH), dtype=jnp.float32) * s
        Wo = jax.random.normal(ks[6], (E, DH, D), dtype=jnp.float32) * s
        return {'x': x, 'Wq': Wq, 'Wk': Wk, 'Ws': Ws, 'Wd': Wd, 'Wv': Wv, 'Wo': Wo}
    _L0_ffn_in = _L0_ffn_setup()
    _d = {'L0_attn_a_x': _L0_attn_a_in['x'], 'L0_attn_a_wq': _L0_attn_a_in['wq'], 'L0_attn_a_bq': _L0_attn_a_in['bq'], 'L0_attn_a_wk': _L0_attn_a_in['wk'], 'L0_attn_a_bk': _L0_attn_a_in['bk'], 'L0_attn_a_wv': _L0_attn_a_in['wv'], 'L0_attn_a_bv': _L0_attn_a_in['bv'], 'L0_attn_a_wp': _L0_attn_a_in['wp'], 'L0_attn_a_bp': _L0_attn_a_in['bp'], 'L0_attn_b_W_attn': _L0_attn_b_in['W_attn'], 'L0_attn_b_b_attn': _L0_attn_b_in['b_attn'], 'L0_attn_b_W_proj': _L0_attn_b_in['W_proj'], 'L0_attn_b_b_proj': _L0_attn_b_in['b_proj'], 'L0_ffn_Wq': _L0_ffn_in['Wq'], 'L0_ffn_Wk': _L0_ffn_in['Wk'], 'L0_ffn_Ws': _L0_ffn_in['Ws'], 'L0_ffn_Wd': _L0_ffn_in['Wd'], 'L0_ffn_Wv': _L0_ffn_in['Wv'], 'L0_ffn_Wo': _L0_ffn_in['Wo']}
    _x0 = _d['L0_attn_a_x']
    _d['L0_attn_a_x'] = jax.random.normal(jax.random.fold_in(jax.random.key(seed), 1), (8, 512, 128), dtype=_x0.dtype)
    del _x0
    return _d

def reference(L0_attn_a_x, L0_attn_a_wq, L0_attn_a_bq, L0_attn_a_wk, L0_attn_a_bk, L0_attn_a_wv, L0_attn_a_bv, L0_attn_a_wp, L0_attn_a_bp, L0_attn_b_W_attn, L0_attn_b_b_attn, L0_attn_b_W_proj, L0_attn_b_b_proj, L0_ffn_Wq, L0_ffn_Wk, L0_ffn_Ws, L0_ffn_Wd, L0_ffn_Wv, L0_ffn_Wo):

    def _L0_attn_a_ref(x, wq, bq, wk, bk, wv, bv, wp, bp):
        import jax, jax.numpy as jnp
        import numpy as np
        N_HEAD = 16

        def _rope_cos_sin(T, D):
            half = D // 2
            i = jnp.arange(half, dtype=jnp.float32)
            alpha = 1.0 / 10000.0 ** (2.0 * i / D)
            ang = jnp.arange(T, dtype=jnp.float32)[:, None] * alpha
            return (jnp.cos(ang), jnp.sin(ang))

        def _apply_rope(t, cos, sin):
            half = t.shape[-1] // 2
            xr, xi = (t[..., :half], t[..., half:])
            return jnp.concatenate([xr * cos - xi * sin, xr * sin + xi * cos], axis=-1)
        B, T, C = x.shape
        H = N_HEAD
        D = C // H

        def heads(w, b):
            return (x @ w.T + b).reshape(B, T, H, D).transpose(0, 2, 1, 3)
        q, k, v = (heads(wq, bq), heads(wk, bk), heads(wv, bv))
        cos, sin = _rope_cos_sin(T, D)
        q = _apply_rope(q, cos, sin)
        k = _apply_rope(k, cos, sin)
        scale = 1.0 / np.sqrt(D).astype(np.float32)
        att = jnp.einsum('bhtd,bhsd->bhts', q, k) * scale
        causal = jnp.tril(jnp.ones((T, T), bool))
        att = jnp.where(causal, att, jnp.float32(-jnp.inf))
        att = jax.nn.softmax(att, axis=-1)
        y = jnp.einsum('bhts,bhsd->bhtd', att, v)
        y = y.transpose(0, 2, 1, 3).reshape(B, T, C)
        return y @ wp.T + bp

    def _L0_attn_b_ref(x, W_attn, b_attn, W_proj, b_proj):
        import jax, jax.numpy as jnp
        import numpy as np
        N_HEAD = 16
        MAX_WAVELENGTH = 1250
        ROPE_PCT = 1.0

        def apply_p_rope(inputs, positions, head_dim, max_wavelength=MAX_WAVELENGTH, rope_percentage=ROPE_PCT):
            rope_angles = int(rope_percentage * head_dim // 2)
            nope_angles = head_dim // 2 - rope_angles
            fraction = 2.0 * jnp.arange(0, rope_angles) / head_dim
            timescale = max_wavelength ** fraction
            timescale = jnp.pad(timescale, (0, nope_angles), mode='constant', constant_values=(0, jnp.inf))
            sinusoid_inp = positions[..., None] / timescale[None, :]
            sin = jnp.sin(sinusoid_inp)
            cos = jnp.cos(sinusoid_inp)
            first_half, second_half = jnp.split(inputs, 2, axis=-1)
            first_part = first_half * cos - second_half * sin
            second_part = second_half * cos + first_half * sin
            return jnp.concatenate([first_part, second_part], axis=-1).astype(inputs.dtype)
        B, T, C = x.shape
        H = N_HEAD
        D = C // H
        qkv = x @ W_attn + b_attn
        q, k, v = jnp.split(qkv, 3, axis=-1)

        def split_heads(t):
            return t.reshape(B, T, H, D).transpose(0, 2, 1, 3)
        q, k, v = (split_heads(q), split_heads(k), split_heads(v))
        positions = jnp.arange(T, dtype=q.dtype)
        q = apply_p_rope(q, positions, D)
        k = apply_p_rope(k, positions, D)
        scale = jnp.sqrt(D).astype(k.dtype)
        attn = jnp.einsum('bhqd,bhkd->bhqk', q, k) / scale
        causal_mask = jnp.tril(jnp.ones((T, T))).astype(bool)
        attn = jnp.where(causal_mask, attn, jnp.finfo(attn.dtype).min)
        attn = jax.nn.softmax(attn, axis=-1)
        y = jnp.einsum('bhqk,bhkd->bhqd', attn, v)
        y = y.transpose(0, 2, 1, 3).reshape(B, T, C)
        return y @ W_proj + b_proj

    def _L0_ffn_ref(x, Wq, Wk, Ws, Wd, Wv, Wo):
        import jax, jax.numpy as jnp
        import numpy as np
        B, T, D = (4, 256, 128)
        H, DH, E, SEL = (8, 64, 5, 2)

        def _topk_mask(logits, k):
            _, idx = jax.lax.top_k(logits, k)
            return jnp.sum(jax.nn.one_hot(idx, logits.shape[-1], dtype=logits.dtype), axis=-2)
        e, d, dh = Wv.shape
        h = Wq.shape[1] // dh
        b, t, _ = x.shape
        scale = dh ** (-0.5)
        q = (x @ Wq).reshape(b, t, h, dh).transpose(0, 2, 1, 3)
        k = (x @ Wk).reshape(b, t, h, dh).transpose(0, 2, 1, 3)
        gl_v = (x @ Ws).reshape(b, t, h, e)
        wv = _topk_mask(gl_v, SEL) * jax.nn.sigmoid(gl_v)
        xv = jnp.einsum('btd,edk->btek', x, Wv)
        v = jnp.einsum('bthe,btek->bhtk', wv, xv)
        scores = jnp.einsum('bhid,bhjd->bhij', q * scale, k)
        probs = jax.nn.softmax(scores, axis=-1)
        attn = jnp.einsum('bhij,bhjd->bihd', probs, v)
        gl_o = (x @ Wd).reshape(b, t, h, e)
        mask_o = _topk_mask(gl_o, SEL)
        out = jnp.einsum('bthe,bthk,ekd->btd', mask_o, attn, Wo)
        return out
    x = L0_attn_a_x
    x = x + _L0_attn_a_ref(_layernorm(x, axis=-1), L0_attn_a_wq, L0_attn_a_bq, L0_attn_a_wk, L0_attn_a_bk, L0_attn_a_wv, L0_attn_a_bv, L0_attn_a_wp, L0_attn_a_bp)
    x = x + _L0_ffn_ref(_layernorm(x, axis=-1), L0_ffn_Wq, L0_ffn_Wk, L0_ffn_Ws, L0_ffn_Wd, L0_ffn_Wv, L0_ffn_Wo)
    x = x + _L0_attn_b_ref(_layernorm(x, axis=-1), L0_attn_b_W_attn, L0_attn_b_b_attn, L0_attn_b_W_proj, L0_attn_b_b_proj)
    x = x + _L0_ffn_ref(_layernorm(x, axis=-1), L0_ffn_Wq, L0_ffn_Wk, L0_ffn_Ws, L0_ffn_Wd, L0_ffn_Wv, L0_ffn_Wo)
    return x

_drawn_inputs = setup_inputs


def setup_inputs(seed=0):
    import zlib

    import numpy as np

    out = dict(_drawn_inputs(seed))
    spreads = {'L0_attn_a_bq': (0.0, 0.8),
     'L0_attn_a_bk': (0.0, 0.8),
     'L0_attn_a_bv': (0.0, 0.297),
     'L0_attn_a_bp': (0.0, 0.1),
     'L0_attn_b_b_attn': (0.0, 0.367),
     'L0_attn_b_b_proj': (0.0, 0.1)}
    factors = {'L0_attn_a_wq': 8.0,
     'L0_attn_a_wk': 8.0,
     'L0_attn_a_wv': 8.0,
     'L0_attn_b_W_attn': 6.586,
     'L0_ffn_Wq': 8.0,
     'L0_ffn_Wk': 8.0,
     'L0_ffn_Ws': 4.055,
     'L0_ffn_Wd': 3.093}
    for name, (base, spread) in spreads.items():
        noise = np.random.default_rng([zlib.crc32(name.encode()), seed]).standard_normal(out[name].shape)
        drawn = base * np.exp(spread * noise) if base else spread * noise
        out[name] = jnp.asarray(drawn.astype(out[name].dtype))
    for name, factor in factors.items():
        out[name] = (out[name] * factor).astype(out[name].dtype)
    return out
```

```python
import numpy as np
import concourse.bass as bass
from concourse import mybir
from contextlib import ExitStack



def attention_and_mixture(nc, x, wa, ba, va, tab, wqk, wgv, wo, ident_in, mask_in, out):
    F32, BF = mybir.dt.float32, mybir.dt.bfloat16
    ALU, ACT, AX = mybir.AluOpType, mybir.ActivationFunctionType, mybir.AxisListType

    B, T, C = x.shape
    P = 128
    NT = T // P
    ROUNDS = wa.shape[0]
    UNITS = ROUNDS * B
    EPS = 1e-5
    HA, DA = 16, C // 16
    GA = 4
    SA = HA // GA
    SCALE_A = float(1.0 / np.sqrt(np.float32(DA)))
    SPLITS_Q = (0, 1, 0, 1, 2, 0)
    SPLITS_K = (0, 0, 1, 1, 0, 2)
    NSP = len(SPLITS_Q)
    ROWS_P1 = 96
    ROWS_P2 = ROWS_P1 + 2
    HF, DF, E = 8, 64, wo.shape[0] // 64
    GF = 2
    SF = HF // GF
    SCALE_F = float(DF) ** -0.5
    PAIRS = HF // 2
    NG = 2 * HF * E
    NX = E * DF
    ZCH = [(0, 128), (128, 256), (256, NX)]

    BANKS_A1 = []
    BANKS_A2 = []
    for pair in range(GA // 2):
        h0, h1 = 2 * pair, 2 * pair + 1
        for h in (h0, h1):
            BANKS_A1 += [[(h, 3, 0)], [(h, 2, 0), (h, 0, 384)]]
            BANKS_A2 += [[(h, 0, 0)], [(h, 1, 0), (h, 3, 384)]]
        BANKS_A1.append([(h0, 1, 0), (h1, 1, 256)])
        BANKS_A2.append([(h0, 2, 0), (h1, 2, 256)])
    NA_B = len(BANKS_A1)
    NF_B = GF * NT

    ctx = ExitStack()
    with ctx:
        def sb(name, shape, dt=F32):
            return ctx.enter_context(nc.sbuf_tensor(name, shape, dt))

        def pb(name, dt=F32):
            return ctx.enter_context(nc.psum_tensor(name, [P, 512], dt))

        waits_passed = {e: ctx.enter_context(nc.semaphore(f"waits_passed_{n}")) for n, e in
                        (("sp", nc.sync), ("pool", nc.gpsimd), ("dve", nc.vector), ("pe", nc.tensor))}

        def apart(eng):
            eng.sem_inc(waits_passed[eng], 1)

        class Signal:

            def __init__(self, name, per, unit=1):
                self.sem = ctx.enter_context(nc.semaphore(name))
                self.per, self.unit = per, unit

                self.first = per * unit

            def at(self, k, n):
                assert -self.per < n <= self.per
                return k * self.first + (self.per + n) * self.unit

        ident = sb("ident", [P, P])
        identb = sb("identb", [P, P], BF)
        maskf = sb("maskf", [P, P])
        maskb = sb("maskb", [P, P], BF)
        wa_s = sb("wa_s", [P, 6, C])
        ba_s = sb("ba_s", [P, 4])
        va_s = sb("va_s", [P, 2, C])
        tab_s = sb("tab_s", [P, 2, T])
        xa = sb("xa", [P, NT, C])
        xb = sb("xb", [P, NT, C])
        xn = sb("xn", [P, NT, C])
        xnT = sb("xnT", [C, T])
        stats = sb("stats", [P, NT, 6])
        mv = sb("mv", [P, NT, 2])
        rstd = sb("rstd", [P, NT])
        var_eps = sb("var_eps", [P, NT])
        minus_half = sb("minus_half", [P, NT])
        rot = sb("rot", [P, T])
        rot2 = sb("rot2", [P, T])
        parts = sb("parts", [P, 3, T], BF)
        Qs = sb("Qs", [ROWS_P2, HA, T], BF)
        Ks = sb("Ks", [ROWS_P2, HA, T], BF)
        Vs = sb("Vs", [P, NT, HA, DA + 1])
        nmaxA = sb("nmaxA", [P, HA, NT])
        nmb = sb("nmb", [P, 2, GA, NT], BF)
        mrowA = sb("mrowA", [2 * GA * NT, P], BF)
        PT = sb("PT", [P, 2, NA_B, 512])
        ySB = sb("ySB", [P, T])
        recA = sb("recA", [P, NT, GA])
        yN = sb("yN", [P, NT, C])
        yT = sb("yT", [C, T])
        res = sb("res", [P, NT, C])
        wqk_s = sb("wqk_s", [P, 2 * HF * DF])
        wgv_s = sb("wgv_s", [P, NG + NX])
        wo_s = sb("wo_s", [P, 3, C])
        stage = sb("stage", [P, 2, 2, T])
        Qb = sb("Qb", [P, PAIRS, T], BF)
        Kb = sb("Kb", [P, PAIRS, T], BF)
        QF = sb("QF", [DF + 1, HF, T])
        KF = sb("KF", [DF + 1, HF, T])
        gate = sb("gate", [P, NT, 2 * HF, E])
        xv = sb("xv", [P, NT, NX])
        cmp_ = sb("cmp", [P, NT * 2 * HF, E, E], BF)
        pick = sb("pick", [P, NT, 2 * HF, E])
        wv_s = sb("wv_s", [P, NT, HF, E])
        Vf = sb("Vf", [P, NT, HF, DF])
        nmaxF = sb("nmaxF", [P, HF, NT])
        mrowF = sb("mrowF", [GF * NT, P])
        ksum = sb("ksum", [P, GF, T])
        ones = sb("ones", [P, 32])
        dSB = sb("dSB", [2 * 32, T])
        recF = sb("recF", [P, NT, GF])
        wz = sb("wz", [P, NT, GF, E])
        Z = sb("Z", [P, NT, E, DF])
        ztmp = sb("ztmp", [P, NT, E, DF])
        vtmp = ztmp[:, :, :, :].rearrange("p t e d -> p (t e d)")[:, 0:2 * HF * DF].rearrange(
            "p (j h d) -> p j h d", j=2, h=HF)
        ZT = sb("ZT", [P, 3, T])

        S1 = [pb("S1a"), pb("S1b")]
        S2 = [pb("S2a"), pb("S2b"), pb("S2c")]
        Y = pb("Y")
        M0, M1 = pb("M0"), pb("M1")

        M0_USES = ["A xnT", "A qp", "A kp"] + [f"A rows{g}" for g in range(SA)] + ["A yNT", "F xnT"] \
            + [f"F k{p}" for p in range(PAIRS)] + ["F gate1", "F gate3", "F rows0", "F rows1"]
        for g in range(SF):
            M0_USES += [f"F rows{g + 2}"] if g + 2 < SF else []
            M0_USES += [f"F den{g - 1}", f"F denT{g - 1}"] if g else []
        M0_USES += [f"F den{SF - 1}", f"F denT{SF - 1}"]
        M0_USES += ["F ZT0", "F ZT2"]
        M1_USES = ["A q", "A k", "A v"] + [f"A YT{g}" for g in range(SA)] + ["A out"] \
            + [f"F q{p}" for p in range(PAIRS)] + ["F gate0", "F gate2"] + [f"F YT{g}" for g in range(SF)] \
            + ["F ZT1", "F out"]

        N1 = SA * NA_B + SF * NF_B
        m0_filled = Signal("m0_filled", len(M0_USES))
        m0_drained = Signal("m0_drained", len(M0_USES))
        m1_filled = Signal("m1_filled", len(M1_USES))
        m1_drained = Signal("m1_drained", len(M1_USES))
        s1_filled = Signal("s1_filled", N1)
        s1_drained = Signal("s1_drained", N1)
        s2_filled = Signal("s2_filled", N1)
        exps_done = Signal("exps_done", N1)
        y_filled = Signal("y_filled", SA + SF)
        y_copied = Signal("y_copied", SA + SF)
        NSET = 6
        consts_loaded = Signal("consts_loaded", NSET, 16)
        x_copied = Signal("x_copied", B, 16)
        consts_cast = Signal("consts_cast", 2)
        dve_init = Signal("dve_init", 9)
        x_loaded = Signal("x_loaded", 2, 16)
        x_stored = Signal("x_stored", 2, 16)
        wa_loaded = Signal("wa_loaded", 4, 16)
        scattered = Signal("scattered", 2 * NSP, 16)
        rows_in = Signal("rows_in", 2 * SA + SF, 16)
        qf_in = Signal("qf_in", 2 * 4, 16)
        res_ready = Signal("res_ready", 2)
        var_ready = Signal("var_ready", 2)
        rstd_ready = Signal("rstd_ready", 2)
        xn_ready = Signal("xn_ready", 2)
        rot_ready = Signal("rot_ready", 2)
        part0_ready = Signal("part0_ready", 2)
        rest1_ready = Signal("rest1_ready", 2)
        part1_ready = Signal("part1_ready", 2)
        part2_ready = Signal("part2_ready", 2)
        nmb_ready = Signal("nmb_ready", SA)
        masked = Signal("masked", SA * NA_B)
        cast_done = Signal("cast_done", 2 * PAIRS)
        sig_e = Signal("sig_e", 1)
        v_mult = Signal("v_mult", NT * E)
        v_acc = Signal("v_acc", NT * (E - 1))
        ksum_done = Signal("ksum_done", GF * SF)
        z_mult = Signal("z_mult", HF)
        z_acc = Signal("z_acc", HF - 1)
        dve_chain = Signal("dve_chain", 2 * 2 + 1 + 2 * SA + 3 + 3 + 2 * SF)
        pool_chain = Signal("pool_chain", GF * SF * 2)

        def bank(use):
            return M0 if use in M0_USES else M1

        def is_full(use):
            return (m0_filled if use in M0_USES else m1_filled).sem

        def is_free(use):
            return (m0_drained if use in M0_USES else m1_drained).sem

        def filled(k, use):
            uses, signal = (M0_USES, m0_filled) if use in M0_USES else (M1_USES, m1_filled)
            return signal.sem, signal.at(k, uses.index(use) + 1)

        def drained(k, use):
            uses, signal = (M0_USES, m0_drained) if use in M0_USES else (M1_USES, m1_drained)
            return signal.sem, signal.at(k, uses.index(use) + 1)

        def free_for(k, use):
            uses, signal = (M0_USES, m0_drained) if use in M0_USES else (M1_USES, m1_drained)
            return signal.sem, signal.at(k, uses.index(use))

        block = ctx.enter_context(nc.Block())

        @block.sync
        def _(sp):
            for s in (x_loaded, x_stored, wa_loaded, scattered, rows_in, qf_in):
                sp.sem_inc(s.sem, s.first)
            sp.dma_start(ident[:, :], ident_in).then_inc(consts_loaded.sem, 16)
            sp.dma_start(maskf[:, :], mask_in).then_inc(consts_loaded.sem, 16)
            for b in range(B):
                sp.dma_start(out[b], x[b]).then_inc(x_copied.sem, 16)
            sp.dma_start(wqk_s[:, :], wqk).then_inc(consts_loaded.sem, 16)
            sp.dma_start(wgv_s[:, :], wgv).then_inc(consts_loaded.sem, 16)
            sp.dma_start(wo_s[:, 0:2, :], wo[0:256, :].rearrange("(c p) n -> p c n", p=P)).then_inc(consts_loaded.sem, 16)
            sp.dma_start(wo_s[0:NX - 256, 2, :], wo[256:NX, :]).then_inc(consts_loaded.sem, 16)
            sp.wait_ge(x_copied.sem, 16 * B)
            sp.wait_ge(dve_init.sem, dve_init.per)
            with sp.Fori(0, UNITS) as k:
                sp.wait_ge(res_ready.sem, res_ready.at(k, 0))
                apart(sp)
                sp.wait_ge(x_stored.sem, x_stored.at(k, 0))
                apart(sp)
                sp.dma_start(xa[:, :, :], out[k % B].rearrange("(t p) c -> p t c", p=P)).then_inc(x_loaded.sem, 16)
                sp.dma_start(wa_s[:, :, :], wa[k // B]).then_inc(wa_loaded.sem, 16)
                sp.dma_start(ba_s[:, :], ba[k // B]).then_inc(wa_loaded.sem, 16)
                sp.dma_start(va_s[:, :, :], va[k // B]).then_inc(wa_loaded.sem, 16)
                sp.dma_start(tab_s[:, :, :], tab[k // B]).then_inc(wa_loaded.sem, 16)
                for qk, (dst, order) in enumerate(((Qs, SPLITS_Q), (Ks, SPLITS_K))):
                    sp.wait_ge(part2_ready.sem, part2_ready.at(k, qk + 1))
                    apart(sp)
                    for r in range(NSP):
                        sp.dma_start(dst[DA * r:DA * r + DA, :, :], parts[:, order[r], :]).then_inc(scattered.sem, 16)
                    sp.wait_ge(scattered.sem, scattered.at(k, NSP * (qk + 1)))
                    apart(sp)
                for g in range(SA):
                    sp.wait_ge(*drained(k, f"A rows{g}"))
                    apart(sp)
                    for j in range(2):
                        sp.dma_start(Qs[ROWS_P1 + j:ROWS_P1 + j + 1, GA * g:GA * g + GA, :],
                                     mrowA[j * GA * NT:(j + 1) * GA * NT, :]).then_inc(rows_in.sem, 16)
                    sp.wait_ge(rows_in.sem, rows_in.at(k, 2 * g + 2))
                    apart(sp)
                sp.wait_ge(res_ready.sem, res_ready.at(k, 1))
                apart(sp)
                sp.dma_start(out[k % B].rearrange("(t p) c -> p t c", p=P), res[:, :, :]).then_inc(x_stored.sem, 16)
                sp.wait_ge(x_stored.sem, x_stored.at(k, 1))
                apart(sp)
                sp.dma_start(xa[:, :, :], out[k % B].rearrange("(t p) c -> p t c", p=P)).then_inc(x_loaded.sem, 16)
                for half in range(2):
                    sp.wait_ge(*drained(k, f"F q{2 * half + 1}"))
                    apart(sp)
                    sp.wait_ge(*drained(k, f"F k{2 * half + 1}"))
                    apart(sp)
                    for qk, dst in enumerate((QF, KF)):
                        for e in range(2):
                            sp.dma_start(dst[0:DF, 4 * half + e:4 * half + e + 3:2, :],
                                         stage[e * DF:(e + 1) * DF, qk, :, :]).then_inc(qf_in.sem, 16)
                    sp.wait_ge(qf_in.sem, qf_in.at(k, 4 * half + 4))
                    apart(sp)
                for g in range(SF):
                    sp.wait_ge(*drained(k, f"F rows{g}"))
                    apart(sp)
                    sp.dma_start(QF[DF:DF + 1, GF * g:GF * g + GF, :], mrowF[:, :]).then_inc(rows_in.sem, 16)
                    sp.wait_ge(rows_in.sem, rows_in.at(k, 2 * SA + g + 1))
                    apart(sp)
                sp.wait_ge(res_ready.sem, res_ready.at(k, 2))
                apart(sp)
                sp.dma_start(out[k % B].rearrange("(t p) c -> p t c", p=P), res[:, :, :]).then_inc(x_stored.sem, 16)
            sp.wait_ge(x_stored.sem, x_stored.at(UNITS - 1, 2))

        @block.tensor
        def _(pe):
            for s in (m0_filled, m1_filled, s1_filled, s2_filled, y_filled):
                pe.sem_inc(s.sem, s.first)
            pe.wait_ge(consts_loaded.sem, 16 * NSET)
            pe.wait_ge(dve_init.sem, dve_init.per)
            pe.wait_ge(consts_cast.sem, consts_cast.per)
            with pe.Fori(0, UNITS) as k:
                def xn_transposes(use):
                    pe.wait_ge(*free_for(k, use))
                    t = bank(use)
                    for i in range(NT):
                        last = nc.tensor.transpose(t[:, i * P:(i + 1) * P], xn[:, i, :], ident[:, :])
                    last.then_inc(is_full(use), 1)

                pe.wait_ge(xn_ready.sem, xn_ready.at(k, 1))
                xn_transposes("A xnT")
                pe.wait_ge(wa_loaded.sem, wa_loaded.at(k, 4))
                pe.wait_ge(*drained(k, "A xnT"))
                for w, use in enumerate(("A q", "A qp", "A k", "A kp")):
                    pe.wait_ge(*free_for(k, use))
                    t = bank(use)
                    nc.tensor.matmul(t[:, :], wa_s[:, w, :], xnT[:, :], start=True, stop=True).then_inc(is_full(use), 1)
                pe.wait_ge(*free_for(k, "A v"))
                t = bank("A v")
                for i in range(NT):
                    last = nc.tensor.matmul(t[:, i * C:(i + 1) * C], xnT[:, i * P:(i + 1) * P], wa_s[:, 4, :],
                                            start=True, stop=True)
                last.then_inc(is_full("A v"), 1)

                def a_pass1(g, b):
                    n = g * NA_B + b + 1
                    pe.wait_ge(s1_drained.sem, s1_drained.at(k, n - 2))
                    t = S1[(n - 1) % 2]
                    for h, qt, col in BANKS_A1[b]:
                        hh, keys = GA * g + h, (qt + 1) * P
                        nc.tensor.matmul(t[:, col:col + keys], Qs[0:ROWS_P1, hh, qt * P:keys],
                                         Ks[0:ROWS_P1, hh, 0:keys], start=True, stop=False)
                        last = nc.tensor.matmul(t[:, col + qt * P:col + keys], identb[:, :], maskb[:, :],
                                                start=False, stop=True)
                    last.then_inc(s1_filled.sem, 1)

                def a_pass2(g, b):
                    n = g * NA_B + b + 1
                    pe.wait_ge(exps_done.sem, exps_done.at(k, n - 3))
                    for h, kt, col in BANKS_A2[b]:
                        hh = GA * g + h
                        last = nc.tensor.matmul(S2[(n - 1) % 3][:, col:col + T - kt * P],
                                                Ks[0:ROWS_P2, hh, kt * P:kt * P + P], Qs[0:ROWS_P2, hh, kt * P:T],
                                                start=True, stop=True)
                    last.then_inc(s2_filled.sem, 1)

                def a_rows(g):
                    pe.wait_ge(nmb_ready.sem, nmb_ready.at(k, g + 1))
                    pe.wait_ge(*free_for(k, f"A rows{g}"))
                    t = bank(f"A rows{g}")
                    nc.tensor.transpose(t[:, :].bitcast(BF)[0:2 * GA * NT, 0:P],
                                        nmb[:, :, :, :].rearrange("p j h t -> p (j h t)"),
                                        identb[:, :]).then_inc(is_full(f"A rows{g}"), 1)

                def a_values(g, kt):
                    if kt == 0:
                        pe.wait_ge(masked.sem, masked.at(k, NA_B * (g + 1)))
                        pe.wait_ge(y_copied.sem, y_copied.at(k, g))
                    for h in range(GA):
                        b, col = next((b, c) for b in range(NA_B) for hh, t, c in BANKS_A2[b] if (hh, t) == (h, kt))
                        last = nc.tensor.matmul(Y[32 * h:32 * h + DA + 1, kt * P:T], Vs[:, kt, GA * g + h, :],
                                                PT[:, g % 2, b, col:col + T - kt * P],
                                                start=(kt == 0), stop=(kt == NT - 1), tile_position=(0, 32 * h))
                    if kt == NT - 1:
                        last.then_inc(y_filled.sem, 1)

                def y_transposes(use, n):
                    pe.wait_ge(y_copied.sem, y_copied.at(k, n))
                    pe.wait_ge(*free_for(k, use))
                    t = bank(use)
                    for i in range(NT):
                        last = nc.tensor.transpose(t[:, i * P:(i + 1) * P], ySB[:, i * P:(i + 1) * P], ident[:, :])
                    last.then_inc(is_full(use), 1)

                pe.wait_ge(scattered.sem, scattered.at(k, 2 * NSP))
                for b in range(NA_B):
                    a_pass1(0, b)
                for b in range(NA_B):
                    a_pass1(1, b)
                    if b == 4:
                        a_rows(0)
                pe.wait_ge(*drained(k, "A v"))
                for g in range(SA):
                    pe.wait_ge(rows_in.sem, rows_in.at(k, 2 * g + 2))
                    for b in range(NA_B):
                        a_pass2(g, b)
                        if g + 2 < SA:
                            a_pass1(g + 2, b)
                        if b == 3 and g + 1 < SA:
                            a_rows(g + 1)
                        if g and b % 2 == 1 and b < 8:
                            a_values(g - 1, b // 2)
                    if g:
                        y_transposes(f"A YT{g - 1}", g)
                for kt in range(NT):
                    a_values(SA - 1, kt)
                y_transposes(f"A YT{SA - 1}", SA)
                pe.wait_ge(*drained(k, f"A YT{SA - 1}"))
                pe.wait_ge(*free_for(k, "A yNT"))
                t = bank("A yNT")
                for i in range(NT):
                    last = nc.tensor.transpose(t[:, i * P:(i + 1) * P], yN[:, i, :], ident[:, :])
                last.then_inc(is_full("A yNT"), 1)
                pe.wait_ge(*drained(k, "A yNT"))
                pe.wait_ge(*free_for(k, "A out"))
                t = bank("A out")
                for i in range(NT):
                    last = nc.tensor.matmul(t[:, i * C:(i + 1) * C], yT[:, i * P:(i + 1) * P], wa_s[:, 5, :],
                                            start=True, stop=True)
                last.then_inc(is_full("A out"), 1)

                pe.wait_ge(xn_ready.sem, xn_ready.at(k, 2))
                xn_transposes("F xnT")
                pe.wait_ge(*drained(k, "F xnT"))
                for p in range(PAIRS):
                    for j, use in enumerate((f"F q{p}", f"F k{p}")):
                        pe.wait_ge(*free_for(k, use))
                        t = bank(use)
                        w0 = j * HF * DF + p * P
                        nc.tensor.matmul(t[:, :], wqk_s[:, w0:w0 + P], xnT[:, :], start=True,
                                         stop=True).then_inc(is_full(use), 1)
                for i in range(NT):
                    pe.wait_ge(*free_for(k, f"F gate{i}"))
                    t = bank(f"F gate{i}")
                    nc.tensor.matmul(t[:, 0:NG + NX], xnT[:, i * P:(i + 1) * P], wgv_s[:, :],
                                     start=True, stop=True).then_inc(is_full(f"F gate{i}"), 1)

                def f_pass1(g, b):
                    n = SA * NA_B + g * NF_B + b + 1
                    pe.wait_ge(s1_drained.sem, s1_drained.at(k, n - 2))
                    h, qt = divmod(b, NT)
                    lo, pair = DF * h, (GF * g + h) // 2
                    nc.tensor.matmul(S1[(n - 1) % 2][:, :], Qb[lo:lo + DF, pair, qt * P:qt * P + P],
                                     Kb[lo:lo + DF, pair, :], start=True, stop=True).then_inc(s1_filled.sem, 1)

                def f_pass2(g, b):
                    n = SA * NA_B + g * NF_B + b + 1
                    pe.wait_ge(exps_done.sem, exps_done.at(k, n - 3))
                    h, kt = divmod(b, NT)
                    hh = GF * g + h
                    nc.tensor.matmul(S2[(n - 1) % 3][:, :], KF[:, hh, kt * P:kt * P + P], QF[:, hh, :],
                                     start=True, stop=True).then_inc(s2_filled.sem, 1)

                def f_rows(g):
                    pe.wait_ge(s1_drained.sem, s1_drained.at(k, SA * NA_B + NF_B * (g + 1)))
                    pe.wait_ge(*free_for(k, f"F rows{g}"))
                    t = bank(f"F rows{g}")
                    nc.tensor.transpose(t[0:GF * NT, 0:P], nmaxF[:, GF * g:GF * g + GF, :].rearrange("p h t -> p (h t)"),
                                        ident[:, :]).then_inc(is_full(f"F rows{g}"), 1)

                def f_values(g, kt):
                    if kt == 0:
                        pe.wait_ge(exps_done.sem, exps_done.at(k, SA * NA_B + NF_B * (g + 1)))
                        pe.wait_ge(y_copied.sem, y_copied.at(k, SA + g))
                    for h in range(GF):
                        last = nc.tensor.matmul(Y[DF * h:DF * h + DF, :], Vf[:, kt, GF * g + h, :],
                                                PT[:, (SA + g) % 2, NT * h + kt, :],
                                                start=(kt == 0), stop=(kt == NT - 1))
                    if kt == NT - 1:
                        last.then_inc(y_filled.sem, 1)

                def f_tail(g):
                    pe.wait_ge(ksum_done.sem, ksum_done.at(k, GF * (g + 1)))
                    pe.wait_ge(*free_for(k, f"F den{g}"))
                    t = bank(f"F den{g}")
                    for h in range(GF):
                        last = nc.tensor.matmul(t[32 * h:32 * h + 32, :], ones[:, :], ksum[:, h, :], start=True, stop=True)
                    last.then_inc(is_full(f"F den{g}"), 1)
                    y_transposes(f"F YT{g}", SA + g + 1)
                    pe.wait_ge(*drained(k, f"F den{g}"))
                    pe.wait_ge(*free_for(k, f"F denT{g}"))
                    t = bank(f"F denT{g}")
                    apart(pe)
                    for i in range(NT):
                        last = nc.tensor.transpose(t[:, i * P:i * P + 64], dSB[:, i * P:(i + 1) * P], ident[0:64, 0:64])
                    last.then_inc(is_full(f"F denT{g}"), 1)

                pe.wait_ge(cast_done.sem, cast_done.at(k, 2 * PAIRS))
                pe.wait_ge(qf_in.sem, qf_in.at(k, 8))
                for b in range(NF_B):
                    f_pass1(0, b)
                for b in range(NF_B):
                    f_pass1(1, b)
                f_rows(0)
                f_rows(1)
                pe.wait_ge(v_acc.sem, v_acc.at(k, NT * (E - 1)))
                for g in range(SF):
                    pe.wait_ge(rows_in.sem, rows_in.at(k, 2 * SA + g + 1))
                    for b in range(NF_B):
                        f_pass2(g, b)
                        if g + 2 < SF:
                            f_pass1(g + 2, b)
                        if g and b % 2 == 1:
                            f_values(g - 1, b // 2)
                    if g + 2 < SF:
                        f_rows(g + 2)
                    if g:
                        f_tail(g - 1)
                for kt in range(NT):
                    f_values(SF - 1, kt)
                f_tail(SF - 1)
                pe.wait_ge(z_acc.sem, z_acc.at(k, HF - 1))
                for c, (lo, hi) in enumerate(ZCH):
                    pe.wait_ge(*free_for(k, f"F ZT{c}"))
                    t = bank(f"F ZT{c}")
                    apart(pe)
                    for i in range(NT):
                        zi = Z[:, i, :, :].rearrange("p e d -> p (e d)")
                        last = nc.tensor.transpose(t[0:hi - lo, i * P:(i + 1) * P], zi[:, lo:hi], ident[:, :])
                    last.then_inc(is_full(f"F ZT{c}"), 1)
                pe.wait_ge(*drained(k, "F ZT1"))
                pe.wait_ge(*drained(k, "F ZT2"))
                pe.wait_ge(*free_for(k, "F out"))
                t = bank("F out")
                for i in range(NT):
                    for c, (lo, hi) in enumerate(ZCH):
                        last = nc.tensor.matmul(t[:, i * C:(i + 1) * C], ZT[0:hi - lo, c, i * P:(i + 1) * P],
                                                wo_s[0:hi - lo, c, :], start=(c == 0), stop=(c == 2))
                last.then_inc(is_full("F out"), 1)

        @block.scalar
        def _(act):
            for s in (exps_done, y_copied, part0_ready, part1_ready, sig_e):
                act.sem_inc(s.sem, s.first)
            act.wait_ge(consts_loaded.sem, 16 * NSET)
            nc.scalar.activation(identb[:, :], ident[:, :], ACT.Copy).then_inc(consts_cast.sem, 1)
            nc.scalar.activation(maskb[:, :], maskf[:, :], ACT.Copy).then_inc(consts_cast.sem, 1)
            with act.Fori(0, UNITS) as k:
                def exps(n, slot, b, scale):
                    act.wait_ge(s2_filled.sem, s2_filled.at(k, n))
                    nc.scalar.activation(PT[:, slot % 2, b, :], S2[(n - 1) % 3][:, :], ACT.Exp,
                                         scale=scale).then_inc(exps_done.sem, 1)

                def y_copy(n):
                    act.wait_ge(y_filled.sem, y_filled.at(k, n))
                    nc.scalar.activation(ySB[:, :], Y[:, :], ACT.Copy).then_inc(y_copied.sem, 1)

                def a_rows(g):
                    act.wait_ge(*filled(k, f"A rows{g}"))
                    t = bank(f"A rows{g}")
                    act.wait_ge(rows_in.sem, rows_in.at(k, 2 * g if g else 0))
                    nc.scalar.activation(mrowA[:, :], t[:, :].bitcast(BF)[0:2 * GA * NT, 0:P], ACT.Copy).then_inc(is_free(f"A rows{g}"), 1)

                def f_rows(g):
                    act.wait_ge(*filled(k, f"F rows{g}"))
                    t = bank(f"F rows{g}")
                    act.wait_ge(rows_in.sem, rows_in.at(k, 2 * SA + g))
                    nc.scalar.activation(mrowF[:, :], t[0:GF * NT, 0:P], ACT.Copy).then_inc(is_free(f"F rows{g}"), 1)

                act.wait_ge(*filled(k, "A xnT"))
                t = bank("A xnT")
                nc.scalar.activation(xnT[:, :], t[:, :], ACT.Copy).then_inc(is_free("A xnT"), 1)
                for qk in range(2):
                    act.wait_ge(rot_ready.sem, rot_ready.at(k, qk + 1))
                    if qk:
                        act.wait_ge(scattered.sem, scattered.at(k, NSP))
                    nc.scalar.activation(parts[:, 0, :], rot[:, :], ACT.Copy).then_inc(part0_ready.sem, 1)
                    act.wait_ge(rest1_ready.sem, rest1_ready.at(k, qk + 1))
                    nc.scalar.activation(parts[:, 1, :], rot2[:, :], ACT.Copy).then_inc(part1_ready.sem, 1)
                a_rows(0)
                for g in range(SA):
                    if g > 1:
                        act.wait_ge(masked.sem, masked.at(k, NA_B * (g - 1)))
                    act.wait_ge(y_filled.sem, y_filled.at(k, g - 1))
                    for b in range(NA_B):
                        exps(g * NA_B + b + 1, g, b, SCALE_A)
                        if b == 3 and g + 1 < SA:
                            a_rows(g + 1)
                    if g:
                        y_copy(g)
                y_copy(SA)
                act.wait_ge(*filled(k, "A yNT"))
                t = bank("A yNT")
                nc.scalar.activation(yT[:, :], t[:, :], ACT.Copy).then_inc(is_free("A yNT"), 1)
                act.wait_ge(*filled(k, "F xnT"))
                t = bank("F xnT")
                nc.scalar.activation(xnT[:, :], t[:, :], ACT.Copy).then_inc(is_free("F xnT"), 1)
                for p in range(PAIRS):
                    if p == 2:
                        act.wait_ge(qf_in.sem, qf_in.at(k, 4))
                        act.wait_ge(cast_done.sem, cast_done.at(k, 4))
                    for j, use in enumerate((f"F q{p}", f"F k{p}")):
                        act.wait_ge(*filled(k, use))
                        t = bank(use)
                        nc.scalar.activation(stage[:, j, p % 2, :], t[:, :], ACT.Copy).then_inc(is_free(use), 1)
                for i in range(NT):
                    act.wait_ge(*filled(k, f"F gate{i}"))
                    t = bank(f"F gate{i}")
                    nc.scalar.activation(gate[:, i, :, :].rearrange("p g e -> p (g e)"), t[:, 0:NG], ACT.Copy)
                    nc.scalar.activation(xv[:, i, :], t[:, NG:NG + NX], ACT.Copy).then_inc(is_free(f"F gate{i}"), 1)
                act.wait_ge(*drained(k, "F gate3"))
                nc.scalar.activation(wv_s[:, :, :, :].rearrange("p t h e -> p t (h e)"),
                                     gate[:, :, 0:HF, :].rearrange("p t h e -> p t (h e)"),
                                     ACT.Exp, scale=-1.0).then_inc(sig_e.sem, 1)
                f_rows(0)
                f_rows(1)
                for g in range(SF):
                    slot = SA + g
                    act.wait_ge(y_filled.sem, y_filled.at(k, slot - 1))
                    if g > 1:
                        act.wait_ge(ksum_done.sem, ksum_done.at(k, GF * (g - 1)))
                    for b in range(NF_B):
                        exps(SA * NA_B + g * NF_B + b + 1, slot, b, SCALE_F)
                    if g:
                        y_copy(slot)
                    if g + 2 < SF:
                        f_rows(g + 2)
                    if g:
                        act.wait_ge(*filled(k, f"F den{g - 1}"))
                        t = bank(f"F den{g - 1}")
                        nc.scalar.activation(dSB[:, :], t[0:64, :], ACT.Copy).then_inc(is_free(f"F den{g - 1}"), 1)
                y_copy(SA + SF)
                act.wait_ge(*filled(k, f"F den{SF - 1}"))
                t = bank(f"F den{SF - 1}")
                nc.scalar.activation(dSB[:, :], t[0:64, :], ACT.Copy).then_inc(is_free(f"F den{SF - 1}"), 1)
                for c, (lo, hi) in enumerate(ZCH):
                    act.wait_ge(*filled(k, f"F ZT{c}"))
                    t = bank(f"F ZT{c}")
                    nc.scalar.activation(ZT[0:hi - lo, c, :], t[0:hi - lo, :], ACT.Copy).then_inc(is_free(f"F ZT{c}"), 1)

        @block.vector
        def _(dve):
            for s in (m0_drained, m1_drained, s1_drained, res_ready, var_ready, xn_ready, nmb_ready, cast_done,
                      v_mult, z_mult, dve_chain):
                dve.sem_inc(s.sem, s.first)
            nc.vector.memset(Qs[:, :, :], 0.0).then_inc(dve_init.sem, 1)
            nc.vector.memset(Ks[:, :, :], 0.0).then_inc(dve_init.sem, 1)
            nc.vector.memset(Y[:, :], 0.0).then_inc(dve_init.sem, 1)
            nc.vector.memset(Vs[:, :, :, :], 1.0).then_inc(dve_init.sem, 1)
            nc.vector.memset(KF[DF:DF + 1, :, :], 1.0).then_inc(dve_init.sem, 1)
            nc.vector.memset(ones[:, :], 1.0).then_inc(dve_init.sem, 1)
            nc.vector.memset(minus_half[:, :], -0.5).then_inc(dve_init.sem, 1)
            nc.vector.memset(cmp_[:, :, :, :], 0.0).then_inc(dve_init.sem, 1)
            dve.wait_ge(dve_init.sem, 2)
            nc.vector.memset(Ks[ROWS_P1:ROWS_P2, :, :], 1.0).then_inc(dve_init.sem, 1)
            dve.wait_ge(dve_init.sem, dve_init.per)
            with dve.Fori(0, UNITS) as k:
                links = [0]

                def link(ins):
                    links[0] += 1
                    ins.then_inc(dve_chain.sem, 1)
                    dve.wait_ge(dve_chain.sem, dve_chain.at(k, links[0]))

                def normalise(n):
                    dve.wait_ge(x_loaded.sem, x_loaded.at(k, n))
                    for i in range(NT):
                        last = nc.vector.bn_stats(stats[:, i, :], xa[:, i, :])
                    link(last)
                    apart(dve)
                    for i in range(NT):
                        last = nc.vector.bn_aggr(mv[:, i, :], stats[:, i, :])
                    link(last)
                    nc.vector.tensor_scalar(var_eps[:, :], mv[:, :, 1], EPS, None, ALU.add).then_inc(var_ready.sem, 1)
                    dve.wait_ge(rstd_ready.sem, rstd_ready.at(k, n))
                    for i in range(NT):
                        last = nc.vector.tensor_scalar(xn[:, i, :], xa[:, i, :], mv[:, i, 0:1], rstd[:, i:i + 1],
                                                       ALU.subtract, ALU.mult)
                    last.then_inc(xn_ready.sem, 1)

                normalise(1)
                dve.wait_ge(wa_loaded.sem, wa_loaded.at(k, 4))
                dve.wait_ge(x_stored.sem, x_stored.at(k, 0))
                link(nc.vector.tensor_tensor(res[:, :, :], xa[:, :, :],
                                             va_s[:, 1:2, :].broadcast_to([P, NT, C]), ALU.add))
                for qk, (use, use_p) in enumerate((("A q", "A qp"), ("A k", "A kp"))):
                    if qk:
                        dve.wait_ge(part2_ready.sem, part2_ready.at(k, 1))
                    for j, (u, dst) in enumerate(((use, rot), (use_p, rot2))):
                        dve.wait_ge(*filled(k, u))
                        t = bank(u)
                        ins = nc.vector.scalar_tensor_tensor(dst[:, :], t[:, :], ba_s[:, 2 * qk + j:2 * qk + j + 1],
                                                             tab_s[:, j, :], ALU.add, ALU.mult)
                        ins.then_inc(is_free(u), 1)
                dve.wait_ge(*filled(k, "A v"))
                t = bank("A v")
                nc.vector.tensor_tensor(
                    Vs[:, :, :, 0:DA], t[:, :].rearrange("p (t h d) -> p t h d", t=NT, h=HA),
                    va_s[:, 0:1, :].rearrange("p o (h d) -> p o h d", h=HA).broadcast_to([P, NT, HA, DA]),
                    ALU.add).then_inc(is_free("A v"), 1)

                def a_max(g, b):
                    n = g * NA_B + b + 1
                    dve.wait_ge(s1_filled.sem, s1_filled.at(k, n))
                    t = S1[(n - 1) % 2]
                    segs = BANKS_A1[b]
                    h0, qt0, _ = segs[0]
                    if len(segs) == 2 and segs[1][1] == qt0:
                        last = nc.vector.tensor_reduce(nmaxA[:, GA * g + h0:GA * g + h0 + 2, qt0],
                                                       t[:, :].rearrange("p (h k) -> p h k", h=2), AX.X, ALU.max,
                                                       negate=True)
                    else:
                        for h, qt, col in segs:
                            last = nc.vector.tensor_reduce(nmaxA[:, GA * g + h, qt:qt + 1],
                                                           t[:, col:col + (qt + 1) * P], AX.X, ALU.max, negate=True)
                    last.then_inc(s1_drained.sem, 1)

                def a_maxima(g):
                    dve.wait_ge(s1_drained.sem, s1_drained.at(k, NA_B * (g + 1)))
                    if g:
                        dve.wait_ge(*filled(k, f"A rows{g - 1}"))
                    src = nmaxA[:, GA * g:GA * g + GA, :]
                    link(nc.vector.tensor_copy(nmb[:, 0, :, :], src))
                    nc.vector.tensor_tensor(nmb[:, 1, :, :], src, nmb[:, 0, :, :], ALU.subtract).then_inc(nmb_ready.sem, 1)

                def a_norm(g):
                    dve.wait_ge(*filled(k, f"A YT{g}"))
                    t = bank(f"A YT{g}")
                    v = t[:, :].rearrange("p (t h r) -> p t h r", t=NT, h=GA)
                    link(nc.vector.reciprocal(recA[:, :, :], v[:, :, :, DA]))
                    ins = nc.vector.tensor_tensor(
                        yN[:, :, GA * DA * g:GA * DA * (g + 1)].rearrange("p t (h d) -> p t h d", h=GA), v[:, :, :, 0:DA],
                        recA[:, :, :].unsqueeze(3).broadcast_to([P, NT, GA, DA]), ALU.mult)
                    ins.then_inc(is_free(f"A YT{g}"), 1)

                for g in range(2):
                    for b in range(NA_B):
                        a_max(g, b)
                    a_maxima(g)
                for g in range(SA):
                    if g + 2 < SA:
                        for b in range(NA_B):
                            a_max(g + 2, b)
                        a_maxima(g + 2)
                    if g:
                        a_norm(g - 1)
                a_norm(SA - 1)
                dve.wait_ge(*filled(k, "A out"))
                t = bank("A out")
                nc.vector.tensor_tensor(res[:, :, :].rearrange("p t c -> p (t c)"), t[:, :],
                                        res[:, :, :].rearrange("p t c -> p (t c)"), ALU.add).then_inc(res_ready.sem, 1)
                dve.wait_ge(res_ready.sem, res_ready.at(k, 1))
                dve.sem_inc(m1_drained.sem, 1)

                normalise(2)
                for p in range(PAIRS):
                    for j, (use, dst) in enumerate(((f"F q{p}", Qb), (f"F k{p}", Kb))):
                        dve.wait_ge(*drained(k, use))
                        nc.vector.tensor_copy(dst[:, p, :], stage[:, j, p % 2, :]).then_inc(cast_done.sem, 1)
                dve.wait_ge(*drained(k, "F gate2"))
                dve.wait_ge(*drained(k, "F gate3"))
                gl = gate[:, :, :, :].rearrange("p t g e -> p (t g) e")
                n_gl = NT * 2 * HF
                for e in range(E):
                    if e:
                        last = nc.vector.tensor_tensor(cmp_[:, :, 0:e, e], gl[:, :, e:e + 1].broadcast_to([P, n_gl, e]),
                                                       gl[:, :, 0:e], ALU.is_gt)
                    if e < E - 1:
                        last = nc.vector.tensor_tensor(cmp_[:, :, e + 1:E, e],
                                                       gl[:, :, e:e + 1].broadcast_to([P, n_gl, E - 1 - e]),
                                                       gl[:, :, e + 1:E], ALU.is_ge)
                link(last)
                pk = pick[:, :, :, :].rearrange("p t g e -> p (t g) e")
                link(nc.vector.tensor_reduce(pk, cmp_[:, :, :, :], AX.X, ALU.add))
                link(nc.vector.tensor_scalar(pk, pk, 1.5, None, ALU.is_lt))
                dve.wait_ge(sig_e.sem, sig_e.at(k, 1))
                wv2 = wv_s[:, :, :, :].rearrange("p t h e -> p (t h e)")
                link(nc.vector.tensor_scalar(wv2, wv2, 1.0, None, ALU.add))
                link(nc.vector.reciprocal(wv2, wv2))
                link(nc.vector.tensor_tensor(wv_s[:, :, :, :].rearrange("p t h e -> p t (h e)"),
                                             wv_s[:, :, :, :].rearrange("p t h e -> p t (h e)"),
                                             pick[:, :, 0:HF, :].rearrange("p t h e -> p t (h e)"), ALU.mult))
                for i in range(NT):
                    for e in range(E):
                        n = i * (E - 1) + e
                        if e and n > 2:
                            dve.wait_ge(v_acc.sem, v_acc.at(k, n - 2))
                        dst = vtmp[:, n % 2, :, :] if e else Vf[:, i, :, :]
                        nc.vector.tensor_tensor(
                            dst, xv[:, i:i + 1, e * DF:(e + 1) * DF].broadcast_to([P, HF, DF]),
                            wv_s[:, i, :, e:e + 1].broadcast_to([P, HF, DF]), ALU.mult).then_inc(v_mult.sem, 1)

                def f_max(g, b):
                    n = SA * NA_B + g * NF_B + b + 1
                    dve.wait_ge(s1_filled.sem, s1_filled.at(k, n))
                    h, qt = divmod(b, NT)
                    nc.vector.tensor_reduce(nmaxF[:, GF * g + h, qt:qt + 1], S1[(n - 1) % 2][:, :], AX.X, ALU.max,
                                            negate=True).then_inc(s1_drained.sem, 1)

                def f_mix(g):
                    dve.wait_ge(*filled(k, f"F denT{g}"))
                    t = bank(f"F denT{g}")
                    link(nc.vector.reciprocal(recF[:, :, :], t[:, :].rearrange("p (t h r) -> p t h r", t=NT, h=4)[:, :, 0:GF, 0]))
                    dve.sem_inc(m0_drained.sem, 1)
                    link(nc.vector.tensor_tensor(wz[:, :, :, :], pick[:, :, HF + GF * g:HF + GF * g + GF, :],
                                                 recF[:, :, :].unsqueeze(3).broadcast_to([P, NT, GF, E]), ALU.mult))
                    dve.wait_ge(*filled(k, f"F YT{g}"))
                    t = bank(f"F YT{g}")
                    y = t[:, :].rearrange("p (t h d) -> p t h d", t=NT, h=GF)
                    for h in range(GF):
                        hh = GF * g + h
                        if hh > 1:
                            dve.wait_ge(z_acc.sem, z_acc.at(k, hh - 1))
                        dst = ztmp if hh else Z
                        ins = nc.vector.tensor_tensor(dst[:, :, :, :], y[:, :, h:h + 1, :].broadcast_to([P, NT, E, DF]),
                                                      wz[:, :, h, :].unsqueeze(3).broadcast_to([P, NT, E, DF]), ALU.mult)
                        ins.then_inc(z_mult.sem, 1)
                    dve.wait_ge(z_mult.sem, z_mult.at(k, GF * g + GF))
                    dve.sem_inc(m1_drained.sem, 1)

                for g in range(2):
                    for b in range(NF_B):
                        f_max(g, b)
                for g in range(SF):
                    if g + 2 < SF:
                        for b in range(NF_B):
                            f_max(g + 2, b)
                    if g:
                        f_mix(g - 1)
                f_mix(SF - 1)
                dve.wait_ge(*filled(k, "F out"))
                t = bank("F out")
                dve.wait_ge(x_stored.sem, x_stored.at(k, 1))
                nc.vector.tensor_tensor(res[:, :, :].rearrange("p t c -> p (t c)"), t[:, :],
                                        xa[:, :, :].rearrange("p t c -> p (t c)"), ALU.add).then_inc(res_ready.sem, 1)
                dve.wait_ge(res_ready.sem, res_ready.at(k, 2))
                dve.sem_inc(m1_drained.sem, 1)
                assert links[0] == dve_chain.per, links

        @block.gpsimd
        def _(pool):
            for s in (rstd_ready, rot_ready, rest1_ready, part2_ready, masked, v_acc, ksum_done, z_acc, pool_chain):
                pool.sem_inc(s.sem, s.first)
            pool.wait_ge(dve_init.sem, dve_init.per)
            with pool.Fori(0, UNITS) as k:
                links = [0]

                def rstds(n):
                    pool.wait_ge(var_ready.sem, var_ready.at(k, n))
                    nc.gpsimd.tensor_tensor(rstd[:, :], var_eps[:, :], minus_half[:, :], ALU.pow).then_inc(rstd_ready.sem, 1)

                rstds(1)
                for qk in range(2):
                    for j, use in enumerate(("A k", "A kp") if qk else ("A q", "A qp")):
                        pool.wait_ge(*drained(k, use))
                    nc.gpsimd.tensor_tensor(rot[:, :], rot[:, :], rot2[:, :], ALU.add).then_inc(rot_ready.sem, 1)
                    pool.wait_ge(part0_ready.sem, part0_ready.at(k, qk + 1))
                    nc.gpsimd.tensor_tensor(rot2[:, :], rot[:, :], parts[:, 0, :], ALU.subtract).then_inc(rest1_ready.sem, 1)
                    pool.wait_ge(part1_ready.sem, part1_ready.at(k, qk + 1))
                    nc.gpsimd.tensor_tensor(parts[:, 2, :], rot2[:, :], parts[:, 1, :], ALU.subtract).then_inc(part2_ready.sem, 1)
                for g in range(SA):
                    for b in range(NA_B):
                        pool.wait_ge(exps_done.sem, exps_done.at(k, g * NA_B + b + 1))
                        apart(pool)
                        for h, kt, col in BANKS_A2[b]:
                            v = PT[:, g % 2, b, col:col + P]
                            last = nc.gpsimd.affine_select(out=v, in_=v, compare_op=ALU.is_ge, fill=0.0, base=0,
                                                           pattern=[[1, P]], channel_multiplier=-1)
                        last.then_inc(masked.sem, 1)
                rstds(2)
                for i in range(NT):
                    for e in range(1, E):
                        n = i * (E - 1) + e
                        pool.wait_ge(v_mult.sem, v_mult.at(k, i * E + e + 1))
                        if n > 1:
                            pool.wait_ge(v_acc.sem, v_acc.at(k, n - 1))
                        nc.gpsimd.tensor_tensor(Vf[:, i, :, :], Vf[:, i, :, :], vtmp[:, n % 2, :, :],
                                                ALU.add).then_inc(v_acc.sem, 1)

                def f_ksum(g):
                    for h in range(GF):
                        pool.wait_ge(exps_done.sem, exps_done.at(k, SA * NA_B + NF_B * g + NT * (h + 1)))
                        if g:
                            pool.wait_ge(*filled(k, f"F den{g - 1}"))
                        pt = PT[:, (SA + g) % 2, NT * h:NT * h + NT, :]
                        for j in (1, 2, 3):
                            ins = nc.gpsimd.tensor_tensor(ksum[:, h, :], pt[:, 0, :] if j == 1 else ksum[:, h, :],
                                                          pt[:, j, :], ALU.add)
                            if j < 3:
                                links[0] += 1
                                ins.then_inc(pool_chain.sem, 1)
                                pool.wait_ge(pool_chain.sem, pool_chain.at(k, links[0]))
                            else:
                                ins.then_inc(ksum_done.sem, 1)

                def f_mix(g):
                    for h in range(GF):
                        hh = GF * g + h
                        if hh:
                            pool.wait_ge(z_mult.sem, z_mult.at(k, hh + 1))
                            if hh > 1:
                                pool.wait_ge(z_acc.sem, z_acc.at(k, hh - 1))
                            nc.gpsimd.tensor_tensor(Z[:, :, :, :], Z[:, :, :, :], ztmp[:, :, :, :],
                                                    ALU.add).then_inc(z_acc.sem, 1)

                for g in range(SF):
                    f_ksum(g)
                    if g:
                        f_mix(g - 1)
                f_mix(SF - 1)
                assert links[0] == pool_chain.per, links


def kernel(L0_attn_a_x, L0_attn_a_wq, L0_attn_a_bq, L0_attn_a_wk, L0_attn_a_bk, L0_attn_a_wv, L0_attn_a_bv, L0_attn_a_wp,
           L0_attn_a_bp, L0_attn_b_W_attn, L0_attn_b_b_attn, L0_attn_b_W_proj, L0_attn_b_b_proj, L0_ffn_Wq, L0_ffn_Wk,
           L0_ffn_Ws, L0_ffn_Wd, L0_ffn_Wv, L0_ffn_Wo):
    import concourse.bacc as bacc
    from concourse.bass_utils import run_bass_kernel_spmd

    x = np.ascontiguousarray(L0_attn_a_x)
    B, T, C = x.shape
    H, D = 16, C // 16
    plain = [h * D + d for d in range(D) for h in range(H)]
    swapped = [h * D + (d + D // 2) % D for d in range(D) for h in range(H)]

    def layout(wq, wk, wv, wp, bq, bk, bv, bp):
        w = np.stack([wq[:, plain], wq[:, swapped], wk[:, plain], wk[:, swapped], wv, wp], 1)
        b = np.stack([bq[plain], bq[swapped], bk[plain], bk[swapped]], 1)
        v = np.broadcast_to(np.stack([bv, bp]), (C, 2, C))
        return w, b, v

    a = layout(*(np.asarray(w).T for w in (L0_attn_a_wq, L0_attn_a_wk, L0_attn_a_wv, L0_attn_a_wp)),
               *(np.asarray(b) for b in (L0_attn_a_bq, L0_attn_a_bk, L0_attn_a_bv, L0_attn_a_bp)))
    Wb, bb = np.asarray(L0_attn_b_W_attn), np.asarray(L0_attn_b_b_attn)
    b = layout(Wb[:, :C], Wb[:, C:2 * C], Wb[:, 2 * C:], np.asarray(L0_attn_b_W_proj), bb[:C], bb[C:2 * C], bb[2 * C:],
               np.asarray(L0_attn_b_b_proj))

    half = D // 2
    i = np.arange(half, dtype=np.float32)
    f32 = np.float32
    ang_a = np.arange(T, dtype=f32)[None] * (f32(1.0) / f32(10000.0) ** (f32(2.0) * i / f32(D)))[:, None]
    ang_b = np.arange(T, dtype=f32)[None] / (f32(1250.0) ** (f32(2.0) * i / f32(D)))[:, None]
    tabs = []
    for ang in (ang_a, ang_b):
        cos, sin = np.cos(ang), np.sin(ang)
        tabs.append(np.stack([np.repeat(np.concatenate([cos, cos]), H, 0), np.repeat(np.concatenate([-sin, sin]), H, 0)], 1))

    Wv, Wo = np.asarray(L0_ffn_Wv), np.asarray(L0_ffn_Wo)
    E, _, DH = Wv.shape
    HE = L0_ffn_Ws.shape[1]
    arrays = {
        "x": x,
        "wa": np.stack([a[0], b[0]]),
        "ba": np.stack([a[1], b[1]]),
        "va": np.stack([a[2], b[2]]),
        "tab": np.stack(tabs).astype(np.float32),
        "wqk": np.concatenate([np.asarray(L0_ffn_Wq), np.asarray(L0_ffn_Wk)], 1),
        "wgv": np.concatenate([np.asarray(L0_ffn_Ws), np.asarray(L0_ffn_Wd), Wv.transpose(1, 0, 2).reshape(C, E * DH)], 1),
        "wo": Wo.reshape(E * DH, C),
        "ident": np.eye(128, dtype=np.float32),
        "mask": np.triu(np.full((128, 128), -1e30, np.float32), 1),
    }
    arrays = {n: np.ascontiguousarray(v) for n, v in arrays.items()}
    nc = bacc.Bacc("TRN2", target_bir_lowering=False, num_devices=1)
    args = [nc.dram_tensor(f"in_{n}", v.shape, mybir.dt.from_np(v.dtype), kind="ExternalInput").ap()
            for n, v in arrays.items()]
    args.append(nc.dram_tensor("out_x", (B, T, C), mybir.dt.float32, kind="ExternalOutput").ap())
    attention_and_mixture(nc, *args)
    r = run_bass_kernel_spmd(nc, [{f"in_{n}": v for n, v in arrays.items()}], core_ids=[0])
    return r.results[0]["out_x"]
```

```python
import numpy as np
import concourse.bass as bass
from concourse import mybir
from contextlib import ExitStack



def attention_and_mixture(nc, x, wa, wp, ba, bv, bp, tab, wqk, wgv, wo, ident_in, mask_in, out):
    F32, F32R, BF = mybir.dt.float32, mybir.dt.float32r, mybir.dt.bfloat16
    ALU, ACT, AX = mybir.AluOpType, mybir.ActivationFunctionType, mybir.AxisListType

    B, T, C = x.shape
    P = 128
    NT = T // P
    ROUNDS = wa.shape[0]
    UNITS = ROUNDS * B
    HEAD, LAST = 3, UNITS + 3
    EPS = 1e-5
    HA, DA = 16, C // 16
    GA = 4
    SA = HA // GA
    SCALE_A = float(1.0 / np.sqrt(np.float32(DA)))
    SPLITS_Q = (0, 1, 0, 1, 2, 0)
    SPLITS_K = (0, 0, 1, 1, 0, 2)
    NSP = len(SPLITS_Q)
    ROWS_P1 = 96
    ROWS_P2 = ROWS_P1 + 2
    HF, DF, E = 8, 64, wo.shape[0] // 64
    GF = 2
    SF = HF // GF
    SCALE_F = float(DF) ** -0.5
    PAIRS = HF // 2
    NG = 2 * HF * E
    NX = E * DF
    ZCH = [(0, 128), (128, 256), (256, NX)]

    BANKS_A1 = []
    BANKS_A2 = []
    for pair in range(GA // 2):
        h0, h1 = 2 * pair, 2 * pair + 1
        for h in (h0, h1):
            BANKS_A1 += [[(h, 3, 0)], [(h, 2, 0), (h, 0, 384)]]
            BANKS_A2 += [[(h, 0, 0)], [(h, 1, 0), (h, 3, 384)]]
        BANKS_A1.append([(h0, 1, 0), (h1, 1, 256)])
        BANKS_A2.append([(h0, 2, 0), (h1, 2, 256)])
    NA_B = len(BANKS_A1)
    NF_B = GF * NT

    ctx = ExitStack()
    with ctx:
        def sb(name, shape, dt=F32):
            return ctx.enter_context(nc.sbuf_tensor(name, shape, dt))

        def pb(name, dt=F32):
            return ctx.enter_context(nc.psum_tensor(name, [P, 512], dt))

        waits_passed = {e: ctx.enter_context(nc.semaphore(f"waits_passed_{n}")) for n, e in
                        (("sp", nc.sync), ("pool", nc.gpsimd), ("dve", nc.vector), ("pe", nc.tensor))}

        def apart(eng):
            eng.sem_inc(waits_passed[eng], 1)

        class Signal:

            def __init__(self, name, per, unit=1, times=UNITS):
                self.sem = ctx.enter_context(nc.semaphore(name))
                self.per, self.unit, self.times = per, unit, times
                self.first = per * unit

            def at(self, j, n, lag=0):
                value = j * self.first + ((1 - lag) * self.per + n) * self.unit
                return min(max(value, 0), (self.times + 1) * self.first) if isinstance(j, int) else value

        ident = sb("ident", [P, P])
        identb = sb("identb", [P, P], BF)
        maskb = sb("maskb", [P, P], BF)
        wa_s = sb("wa_s", [P, 5, C])
        wp_s = sb("wp_s", [P, C])
        bp_s = sb("bp_s", [P, C])
        ba_s = sb("ba_s", [P, 4])
        bv_s = sb("bv_s", [P, C])
        tab_s = sb("tab_s", [P, 2, T])
        xl = sb("xl", [P, NT, C])
        xr = sb("xr", [P, NT, C])
        xn = sb("xn", [P, NT, C])
        xnT = sb("xnT", [C, T])
        stats = sb("stats", [P, NT, 6])
        mv = sb("mv", [P, NT, 2])
        rstd = sb("rstd", [P, NT])
        var_eps = sb("var_eps", [P, NT])
        minus_half = sb("minus_half", [P, NT])
        parts = sb("parts", [P, 2, 3, T], BF)
        Qs = sb("Qs", [ROWS_P2, HA, T], BF)
        Ks = sb("Ks", [ROWS_P2, HA, T], BF)
        Vs = sb("Vs", [P, NT, HA, DA + 1])
        nmaxA = sb("nmaxA", [P, HA, NT])
        nmb = sb("nmb", [P, 2, GA, NT], BF)
        mrowA = sb("mrowA", [2 * GA * NT, P], BF)
        PT = sb("PT", [P, 2, NA_B, 512])
        ySB = sb("ySB", [P, T])
        recA = sb("recA", [P, NT, GA])
        yN = sb("yN", [P, NT, C])
        yT = sb("yT", [C, T])
        res = sb("res", [P, NT, C])
        wqk_s = sb("wqk_s", [P, 2 * HF * DF])
        wgv_s = sb("wgv_s", [P, NG + NX])
        wo_s = sb("wo_s", [P, 3, C])
        stage = sb("stage", [P, 2, PAIRS, T])
        maskf = stage[:, 0, 0, 0:P]
        Qb = sb("Qb", [P, PAIRS, T], BF)
        Kb = sb("Kb", [P, PAIRS, T], BF)
        XQ = sb("XQ", [P, 2, GF, T], F32R)
        XK = sb("XK", [P, 2, GF, T], F32R)
        QM = sb("QM", [DF + 1, 2, GF, T], F32R)
        KL = sb("KL", [DF + 1, 2, GF, T], F32R)
        gate = sb("gate", [P, NT, 2 * HF, E])
        xv = sb("xv", [P, NT, NX])
        pick = sb("pick", [P, NT, 2 * HF, E])
        wv_s = sb("wv_s", [P, NT, HF, E])
        Vf = sb("Vf", [P, NT, HF, DF])
        nmaxF = sb("nmaxF", [P, HF, NT])
        mrowF = sb("mrowF", [GF * NT, P], F32R)
        rotated = sb("rotated", [P, 2, T])
        rot, rot2 = rotated[:, 0, :], rotated[:, 1, :]
        cmp_ = rotated[:, :, :].rearrange("p a t -> p (a t)").bitcast(BF)[:, 0:NT * 2 * HF * E * E].rearrange(
            "p (g a b) -> p g a b", a=E, b=E)
        ones = sb("ones", [P, 32])
        dSB = sb("dSB", [P, T])
        denF = sb("denF", [P, NT, GF])
        recF = sb("recF", [P, NT, GF])
        wz = sb("wz", [P, NT, GF, E])
        Z = sb("Z", [P, NT, E, DF])
        ztmp = sb("ztmp", [P, 2, NT, E, DF])
        VBUF = 4
        vtmp = ztmp[:, :, :, :, :].rearrange("p b t e d -> p (b t e d)")[:, 0:VBUF * HF * DF].rearrange(
            "p (j h d) -> p j h d", j=VBUF, h=HF)
        ZT = parts[:, :, :, :].rearrange("p q c t -> p (q c t)").bitcast(F32).rearrange("p (c t) -> p c t", c=3)

        S1 = [pb("S1a"), pb("S1b"), pb("S1c")]
        S2 = [pb("S2a"), pb("S2b")]
        Y = pb("Y")
        M0, M1 = pb("M0"), pb("M1")

        M0_USES = ["denT2", "rows1", "den3",
                   "denT3", "rows2", "ZT1", "F out",
                   "rows3", "A xnT", "A qp",
                   "rows4", "A kp",
                   "rows5",
                   "rows6", "A yNT", "den0",
                   "denT0", "rows7", "F xnT", "den1", "F k0",
                   "denT1", "F k1", "rows0", "F k2", "F k3", "F gate1", "den2", "F gate3"]
        M1_USES = ["YT7",
                   "ZT0", "ZT2", "YT0",
                   "A q", "YT1",
                   "A k", "YT2",
                   "YT3",
                   "A v", "A out", "YT4",
                   "F q0", "YT5",
                   "F q1", "F q2", "F q3", "F gate0", "F gate2", "YT6"]

        N_BANKS = [NA_B] * SA + [NF_B] * SF
        NS = SA + SF
        STEPS = NA_B
        V_STEPS = [(s, b) for s, bs in ((2, (0, 2, 4, 8)), (3, (0, 2, 4, 8)), (4, (0, 1, 2, 3, 4, 5, 7)), (5, (0, 1, 3, 4, 5)))
                   for b in bs]
        N1 = sum(N_BANKS)
        AHEAD = 2
        BEFORE2 = [sum(N_BANKS[:s]) for s in range(NS)]
        BEFORE1 = [sum(N_BANKS[i % NS] for i in range(AHEAD, AHEAD + s)) for s in range(NS)]

        m0_filled = Signal("m0_filled", len(M0_USES), times=LAST)
        m0_drained = Signal("m0_drained", len(M0_USES), times=LAST)
        m1_filled = Signal("m1_filled", len(M1_USES), times=LAST)
        m1_drained = Signal("m1_drained", len(M1_USES), times=LAST)
        s1_filled = Signal("s1_filled", N1, times=LAST)
        s1_drained = Signal("s1_drained", N1, times=LAST)
        s2_filled = Signal("s2_filled", N1, times=LAST)
        exps_done = Signal("exps_done", N1, times=LAST)
        y_filled = Signal("y_filled", NS, times=LAST)
        y_copied = Signal("y_copied", NS, times=LAST)
        NSET = 6
        consts_loaded = Signal("consts_loaded", NSET, 16)
        x_copied = Signal("x_copied", B, 16)
        consts_cast = Signal("consts_cast", 2)
        dve_init = Signal("dve_init", 8)
        xlA_loaded = Signal("xlA_loaded", 1, 16)
        xlF_loaded = Signal("xlF_loaded", 1, 16)
        xrA_loaded = Signal("xrA_loaded", 3, 16)
        xrF_loaded = Signal("xrF_loaded", 1, 16)
        resA_stored = Signal("resA_stored", 1, 16)
        resF_stored = Signal("resF_stored", 1, 16)
        wa_loaded = Signal("wa_loaded", 4, 16)
        scattered = Signal("scattered", 2 * NSP, 16)
        rowsA_in = Signal("rowsA_in", 2 * SA, 16)
        rowsF_in = Signal("rowsF_in", SF, 16)
        hi_ready = Signal("hi_ready", 2 * SF)
        low_ready = Signal("low_ready", 2 * SF)
        copies_in = Signal("copies_in", 4 * SF, 16)
        resA_ready = Signal("resA_ready", 1)
        resF_ready = Signal("resF_ready", 1)
        varA_ready = Signal("varA_ready", 1)
        varF_ready = Signal("varF_ready", 1)
        rstdA_ready = Signal("rstdA_ready", 1)
        rstdF_ready = Signal("rstdF_ready", 1)
        xnA_ready = Signal("xnA_ready", 1)
        xnF_ready = Signal("xnF_ready", 1)
        rot_ready = Signal("rot_ready", 2)
        part0_ready = Signal("part0_ready", 2)
        rest1_ready = Signal("rest1_ready", 2)
        part1_ready = Signal("part1_ready", 2)
        part2_ready = Signal("part2_ready", 2)
        nmb_ready = Signal("nmb_ready", SA)
        masked = Signal("masked", SA * NA_B)
        cast_done = Signal("cast_done", 2 * PAIRS)
        sig_e = Signal("sig_e", 1)
        v_mult = Signal("v_mult", NT * E)
        v_acc = Signal("v_acc", NT * (E - 1))
        z_mult = Signal("z_mult", HF)
        z_acc = Signal("z_acc", HF - 1)
        lnA_chain = Signal("lnA_chain", 2)
        lnF_chain = Signal("lnF_chain", 2)
        outA_chain = Signal("outA_chain", 1)
        maxA_chain = Signal("maxA_chain", SA)
        normA_chain = Signal("normA_chain", SA)
        pick_chain = Signal("pick_chain", 6)
        mix_chain = Signal("mix_chain", 2 * SF)

        def bank(use):
            return M0 if use in M0_USES else M1

        def is_full(use):
            return (m0_filled if use in M0_USES else m1_filled).sem

        def is_free(use):
            return (m0_drained if use in M0_USES else m1_drained).sem

        def filled(k, use, lag=0):
            uses, signal = (M0_USES, m0_filled) if use in M0_USES else (M1_USES, m1_filled)
            return signal.sem, signal.at(k, uses.index(use) + 1, lag)

        def drained(k, use, lag=0):
            uses, signal = (M0_USES, m0_drained) if use in M0_USES else (M1_USES, m1_drained)
            return signal.sem, signal.at(k, uses.index(use) + 1, lag)

        def free_for(k, use, lag=0):
            uses, signal = (M0_USES, m0_drained) if use in M0_USES else (M1_USES, m1_drained)
            return signal.sem, signal.at(k, uses.index(use), lag)

        ALL = dict(a=True, f=True, f_end=True, a_prep=True, f_prep=True)

        def parts_of(j):
            return dict(a=0 <= j - 1 < UNITS, f=0 <= j - 2 < UNITS, f_end=0 <= j - 3 < UNITS, a_prep=0 <= j < UNITS,
                        f_prep=0 <= j - 1 < UNITS)

        block = ctx.enter_context(nc.Block())

        @block.sync
        def _(sp):
            for s in (xlA_loaded, xlF_loaded, xrA_loaded, xrF_loaded, resA_stored, resF_stored, wa_loaded, scattered,
                      rowsA_in, rowsF_in, copies_in):
                sp.sem_inc(s.sem, s.first)
            for b in range(B):
                sp.dma_start(out[b], x[b]).then_inc(x_copied.sem, 16)
            sp.dma_start(ident[:, :], ident_in).then_inc(consts_loaded.sem, 16)
            sp.dma_start(maskf, mask_in).then_inc(consts_loaded.sem, 16)
            sp.dma_start(wqk_s[:, :], wqk).then_inc(consts_loaded.sem, 16)
            sp.dma_start(wgv_s[:, :], wgv).then_inc(consts_loaded.sem, 16)
            sp.dma_start(wo_s[:, 0:2, :], wo[0:256, :].rearrange("(c p) n -> p c n", p=P)).then_inc(consts_loaded.sem, 16)
            sp.dma_start(wo_s[0:NX - 256, 2, :], wo[256:NX, :]).then_inc(consts_loaded.sem, 16)
            sp.wait_ge(x_copied.sem, 16 * B)
            sp.wait_ge(dve_init.sem, dve_init.per)

            def stream(u):
                return out[u % B].rearrange("(t p) c -> p t c", p=P)

            def iteration(j, a, f, f_end, a_prep, f_prep):
                def rows(group):
                    sp.wait_ge(*drained(j, f"rows{group}"))
                    apart(sp)
                    if group < SA:
                        for i in range(2):
                            sp.dma_start(Qs[ROWS_P1 + i:ROWS_P1 + i + 1, GA * group:GA * group + GA, :],
                                         mrowA[i * GA * NT:(i + 1) * GA * NT, :]).then_inc(rowsA_in.sem, 16)
                    else:
                        g = group - SA
                        sp.dma_start(QM[DF:DF + 1, g % 2, :, :].bitcast(F32),
                                     mrowF[:, :].bitcast(F32)).then_inc(rowsF_in.sem, 16)

                def copies(g):
                    if not f:
                        return
                    for qk, (src, dst) in enumerate(((XQ, QM), (XK, XK))):
                        sp.wait_ge(hi_ready.sem, hi_ready.at(j, 2 * g + qk + 1, 2))
                        apart(sp)
                        for h in range(GF):
                            own = slice(DF * h, DF * h + DF)
                            to = slice(DF - DF * h, P - DF * h) if qk else slice(0, DF)
                            sp.dma_start(dst[to, g % 2, h, :].bitcast(F32),
                                         src[own, g % 2, h, :].bitcast(F32)).then_inc(copies_in.sem, 16)

                if f_end:
                    sp.wait_ge(resA_ready.sem, resA_ready.at(j, 1, 2))
                    apart(sp)
                    sp.dma_start(xr[:, :, :], stream(j - 3)).then_inc(xrF_loaded.sem, 16)
                if a:
                    rows(1)
                if a_prep:
                    sp.wait_ge(xnF_ready.sem, xnF_ready.at(j, 1, 2))
                    apart(sp)
                    sp.wait_ge(resF_stored.sem, resF_stored.at(j, 1, 4))
                    apart(sp)
                    sp.dma_start(xl[:, :, :], stream(j)).then_inc(xlA_loaded.sem, 16)
                    sp.wait_ge(*drained(j, "A v", 1))
                    apart(sp)
                    for dst, src in ((wa_s, wa), (ba_s, ba), (bv_s, bv), (tab_s, tab)):
                        dst = dst[:, :] if len(dst.shape) == 2 else dst[:, :, :]
                        sp.dma_start(dst, src[j // B]).then_inc(wa_loaded.sem, 16)
                if a:
                    rows(2)
                if f_end:
                    sp.wait_ge(resF_ready.sem, resF_ready.at(j, 1, 3))
                    apart(sp)
                    sp.dma_start(stream(j - 3), res[:, :, :]).then_inc(resF_stored.sem, 16)
                if a:
                    sp.wait_ge(resF_ready.sem, resF_ready.at(j, 1, 3))
                    apart(sp)
                    sp.wait_ge(resA_ready.sem, resA_ready.at(j, 1, 2))
                    apart(sp)
                    sp.dma_start(xr[:, :, :], stream(j - 1)).then_inc(xrA_loaded.sem, 16)
                    sp.dma_start(wp_s[:, :], wp[(j - 1) // B]).then_inc(xrA_loaded.sem, 16)
                    sp.dma_start(bp_s[:, :], bp[(j - 1) // B]).then_inc(xrA_loaded.sem, 16)
                    rows(3)
                copies(0)
                if f:
                    rows(4)
                copies(1)
                if a_prep:
                    sp.wait_ge(s2_filled.sem, s2_filled.at(j, BEFORE2[SA]))
                    apart(sp)
                    for qk, (dst, order) in enumerate(((Qs, SPLITS_Q), (Ks, SPLITS_K))):
                        sp.wait_ge(part2_ready.sem, part2_ready.at(j, qk + 1))
                        apart(sp)
                        for r in range(NSP):
                            sp.dma_start(dst[DA * r:DA * r + DA, :, :],
                                         parts[:, qk, order[r], :]).then_inc(scattered.sem, 16)
                if f:
                    rows(5)
                copies(2)
                if f:
                    rows(6)
                if a:
                    sp.wait_ge(resA_ready.sem, resA_ready.at(j, 1, 1))
                    apart(sp)
                    sp.dma_start(stream(j - 1), res[:, :, :]).then_inc(resA_stored.sem, 16)
                if f_prep:
                    sp.wait_ge(resA_stored.sem, resA_stored.at(j, 1, 1))
                    apart(sp)
                    sp.wait_ge(xnA_ready.sem, xnA_ready.at(j, 1))
                    apart(sp)
                    sp.dma_start(xl[:, :, :], stream(j - 1)).then_inc(xlF_loaded.sem, 16)
                copies(3)
                if f:
                    rows(7)
                if a_prep:
                    rows(0)

            for j in range(HEAD):
                iteration(j, **parts_of(j))
            with sp.Fori(HEAD, UNITS) as j:
                iteration(j, **ALL)
            for j in range(UNITS, LAST):
                iteration(j, **parts_of(j))
            sp.wait_ge(resF_stored.sem, resF_stored.at(UNITS - 1, 1))

        @block.tensor
        def _(pe):
            for s in (m0_filled, m1_filled, s1_filled, s2_filled, y_filled):
                pe.sem_inc(s.sem, s.first)
            pe.wait_ge(consts_loaded.sem, 16 * NSET)
            pe.wait_ge(dve_init.sem, dve_init.per)
            pe.wait_ge(consts_cast.sem, consts_cast.per)

            def iteration(j, a, f, f_end, a_prep, f_prep):
                def skip(use):
                    pe.wait_ge(*free_for(j, use))
                    pe.sem_inc(is_full(use), 1)
                    pe.sem_inc(is_free(use), 1)

                def pass1(slot, b):
                    group, n = (slot + AHEAD) % NS, BEFORE1[slot] + b + 1
                    t = S1[(n - 1) % len(S1)]
                    if not (a if slot < 2 else f if slot < 6 else a_prep):
                        if b == 0:
                            pe.wait_ge(s1_drained.sem, s1_drained.at(j, n - 1))
                            pe.sem_inc(s1_filled.sem, N_BANKS[group])
                            pe.sem_inc(s1_drained.sem, N_BANKS[group])
                        return
                    if group == 0 and b == 0:
                        pe.wait_ge(scattered.sem, scattered.at(j, 2 * NSP))
                    if group == SA and b == 0:
                        pe.wait_ge(cast_done.sem, cast_done.at(j, 2 * PAIRS, 2))
                    pe.wait_ge(s1_drained.sem, s1_drained.at(j, n - len(S1)))
                    if group < SA:
                        for h, qt, col in BANKS_A1[b]:
                            hh, keys = GA * group + h, (qt + 1) * P
                            nc.tensor.matmul(t[:, col:col + keys], Qs[0:ROWS_P1, hh, qt * P:keys],
                                             Ks[0:ROWS_P1, hh, 0:keys], start=True, stop=False)
                            last = nc.tensor.matmul(t[:, col + qt * P:col + keys], identb[:, :], maskb[:, :],
                                                    start=False, stop=True)
                        last.then_inc(s1_filled.sem, 1)
                    else:
                        h, qt = divmod(b, NT)
                        lo, pair = DF * h, group - SA
                        nc.tensor.matmul(t[:, :], Qb[lo:lo + DF, pair, qt * P:qt * P + P], Kb[lo:lo + DF, pair, :],
                                         start=True, stop=True).then_inc(s1_filled.sem, 1)

                def pass2(slot, b):
                    n = BEFORE2[slot] + b + 1
                    t = S2[(n - 1) % len(S2)]
                    if not (a if slot < SA else f):
                        if b == 0:
                            pe.wait_ge(exps_done.sem, exps_done.at(j, n - 1))
                            pe.sem_inc(s2_filled.sem, N_BANKS[slot])
                            pe.sem_inc(exps_done.sem, N_BANKS[slot])
                        return
                    if b == 0 and slot < SA:
                        pe.wait_ge(rowsA_in.sem, rowsA_in.at(j, 2 * slot + 2, 1))
                    if b == 0 and slot >= SA:
                        pe.wait_ge(copies_in.sem, copies_in.at(j, 4 * (slot - SA + 1), 2))
                        pe.wait_ge(low_ready.sem, low_ready.at(j, 2 * (slot - SA + 1), 2))
                        pe.wait_ge(rowsF_in.sem, rowsF_in.at(j, slot - SA + 1, 2))
                    pe.wait_ge(exps_done.sem, exps_done.at(j, n - len(S2)))
                    if slot < SA:
                        for h, kt, col in BANKS_A2[b]:
                            hh = GA * slot + h
                            last = nc.tensor.matmul(t[:, col:col + T - kt * P], Ks[0:ROWS_P2, hh, kt * P:kt * P + P],
                                                    Qs[0:ROWS_P2, hh, kt * P:T], start=True, stop=True)
                        last.then_inc(s2_filled.sem, 1)
                    else:
                        h, kt = divmod(b, NT)
                        buf = (slot - SA) % 2
                        nc.tensor.matmul(t[:, :], XK[:, buf, h, kt * P:kt * P + P], XQ[:, buf, h, :],
                                         start=True, stop=False)
                        nc.tensor.matmul(t[:, :], KL[:, buf, h, kt * P:kt * P + P], QM[:, buf, h, :],
                                         start=False, stop=True).then_inc(s2_filled.sem, 1)

                def has_values(slot):
                    return f_end if slot == 0 else a if slot <= SA else f

                def values(slot, kt):
                    group = (slot - 1) % NS
                    if not has_values(slot):
                        if kt == 0:
                            pe.wait_ge(y_copied.sem, y_copied.at(j, slot))
                            pe.sem_inc(y_filled.sem, 1)
                            pe.sem_inc(y_copied.sem, 1)
                        return
                    if kt == 0:
                        pe.wait_ge(y_copied.sem, y_copied.at(j, slot))
                    if group < SA:
                        if kt == 0:
                            pe.wait_ge(masked.sem, masked.at(j, NA_B * (group + 1), 1))
                            if group == 0:
                                pe.wait_ge(*drained(j, "A v", 1))
                        for h in range(GA):
                            b, col = next((b, c) for b in range(NA_B) for hh, t, c in BANKS_A2[b] if (hh, t) == (h, kt))
                            last = nc.tensor.matmul(Y[32 * h:32 * h + DA + 1, kt * P:T], Vs[:, kt, GA * group + h, :],
                                                    PT[:, group % 2, b, col:col + T - kt * P],
                                                    start=(kt == 0), stop=(kt == NT - 1), tile_position=(0, 32 * h))
                    else:
                        if kt == 0:
                            pe.wait_ge(exps_done.sem, exps_done.at(j, BEFORE2[slot]))
                        if group == SA:
                            pe.wait_ge(v_acc.sem, v_acc.at(j, (E - 1) * (kt + 1), 2))
                        for h in range(GF):
                            last = nc.tensor.matmul(Y[DF * h:DF * h + DF, :], Vf[:, kt, GF * (group - SA) + h, :],
                                                    PT[:, group % 2, NT * h + kt, :],
                                                    start=(kt == 0), stop=(kt == NT - 1))
                    if kt == NT - 1:
                        last.then_inc(y_filled.sem, 1)

                def rows(group):
                    use = f"rows{group}"
                    if not (a_prep if group == 0 else a if group < SA else f):
                        return skip(use)
                    pe.wait_ge(*free_for(j, use))
                    t = bank(use)
                    if group < SA:
                        pe.wait_ge(nmb_ready.sem, nmb_ready.at(j, group + 1, 1 if group else 0))
                        nc.tensor.transpose(t[:, :].bitcast(BF)[0:2 * GA * NT, 0:P],
                                            nmb[:, :, :, :].rearrange("p j h t -> p (j h t)"),
                                            identb[:, :]).then_inc(is_full(use), 1)
                    else:
                        g = group - SA
                        pe.wait_ge(s1_drained.sem, s1_drained.at(j, BEFORE1[group - AHEAD + 1]))
                        nc.tensor.transpose(t[0:GF * NT, 0:P], nmaxF[:, GF * g:GF * g + GF, :].rearrange("p h t -> p (h t)"),
                                            ident[:, :]).then_inc(is_full(use), 1)

                def value_transposes(slot):
                    use = f"YT{(slot - 1) % NS}"
                    if not has_values(slot):
                        return skip(use)
                    pe.wait_ge(y_copied.sem, y_copied.at(j, slot + 1))
                    pe.wait_ge(*free_for(j, use))
                    t = bank(use)
                    for i in range(NT):
                        last = nc.tensor.transpose(t[:, i * P:(i + 1) * P], ySB[:, i * P:(i + 1) * P], ident[:, :])
                    last.then_inc(is_full(use), 1)

                def denominators(slot):
                    g = (slot - 1) % NS - SA
                    use = f"den{g}"
                    if not has_values(slot):
                        return skip(use)
                    pe.wait_ge(*free_for(j, use))
                    t = bank(use)
                    for kt in range(NT):
                        for h in range(GF):
                            lo = 32 * (2 * h + kt % 2)
                            last = nc.tensor.matmul(t[lo:lo + 32, :], ones[:, :], PT[:, (SA + g) % 2, NT * h + kt, :],
                                                    start=(kt < 2), stop=(kt >= 2), tile_position=(0, lo))
                    last.then_inc(is_full(use), 1)

                def denominator_transposes(slot):
                    g = (slot - 2) % NS - SA
                    use = f"denT{g}"
                    if not (f_end if slot < 2 else f):
                        return skip(use)
                    pe.wait_ge(*drained(j, f"den{g}", 0 if slot else 1))
                    pe.wait_ge(*free_for(j, use))
                    apart(pe)
                    t = bank(use)
                    for i in range(NT):
                        last = nc.tensor.transpose(t[:, i * P:(i + 1) * P], dSB[:, i * P:(i + 1) * P], ident[:, :])
                    last.then_inc(is_full(use), 1)

                def xn_transposes(use, has):
                    if not has:
                        return skip(use)
                    if use == "A xnT":
                        pe.wait_ge(xnA_ready.sem, xnA_ready.at(j, 1))
                    else:
                        pe.wait_ge(xnF_ready.sem, xnF_ready.at(j, 1, 1))
                    pe.wait_ge(*free_for(j, use))
                    t = bank(use)
                    for i in range(NT):
                        last = nc.tensor.transpose(t[:, i * P:(i + 1) * P], xn[:, i, :], ident[:, :])
                    last.then_inc(is_full(use), 1)

                def a_project(use):
                    if not a_prep:
                        return skip(use)
                    if use == "A q":
                        pe.wait_ge(wa_loaded.sem, wa_loaded.at(j, 4))
                        pe.wait_ge(*drained(j, "A xnT"))
                    pe.wait_ge(*free_for(j, use))
                    t = bank(use)
                    w = ("A q", "A qp", "A k", "A kp").index(use)
                    nc.tensor.matmul(t[:, :], wa_s[:, w, :], xnT[:, :], start=True, stop=True).then_inc(is_full(use), 1)

                def a_project_values():
                    if not a_prep:
                        return skip("A v")
                    pe.wait_ge(*free_for(j, "A v"))
                    t = bank("A v")
                    for i in range(NT):
                        last = nc.tensor.matmul(t[:, i * C:(i + 1) * C], xnT[:, i * P:(i + 1) * P], wa_s[:, 4, :],
                                                start=True, stop=True)
                    last.then_inc(is_full("A v"), 1)

                def a_y_transposes():
                    if not a:
                        return skip("A yNT")
                    pe.wait_ge(*drained(j, f"YT{SA - 1}"))
                    pe.wait_ge(*free_for(j, "A yNT"))
                    t = bank("A yNT")
                    for i in range(NT):
                        last = nc.tensor.transpose(t[:, i * P:(i + 1) * P], yN[:, i, :], ident[:, :])
                    last.then_inc(is_full("A yNT"), 1)

                def a_output():
                    if not a:
                        return skip("A out")
                    pe.wait_ge(xrA_loaded.sem, xrA_loaded.at(j, 3, 1))
                    pe.wait_ge(*drained(j, "A yNT"))
                    pe.wait_ge(*free_for(j, "A out"))
                    t = bank("A out")
                    for i in range(NT):
                        last = nc.tensor.matmul(t[:, i * C:(i + 1) * C], yT[:, i * P:(i + 1) * P], wp_s[:, :],
                                                start=True, stop=True)
                    last.then_inc(is_full("A out"), 1)

                def f_project(p):
                    for i, use in enumerate((f"F q{p}", f"F k{p}")):
                        if not f_prep:
                            skip(use)
                            continue
                        if p == 0 and i == 0:
                            pe.wait_ge(*drained(j, "F xnT"))
                        pe.wait_ge(*free_for(j, use))
                        t = bank(use)
                        w0 = i * HF * DF + p * P
                        nc.tensor.matmul(t[:, :], wqk_s[:, w0:w0 + P], xnT[:, :], start=True,
                                         stop=True).then_inc(is_full(use), 1)

                def f_gates(i):
                    use = f"F gate{i}"
                    if not f_prep:
                        return skip(use)
                    pe.wait_ge(*free_for(j, use))
                    t = bank(use)
                    nc.tensor.matmul(t[:, 0:NG + NX], xnT[:, i * P:(i + 1) * P], wgv_s[:, :],
                                     start=True, stop=True).then_inc(is_full(use), 1)

                def z_transposes(c):
                    use = f"ZT{c}"
                    if not f_end:
                        return skip(use)
                    if c == 0:
                        pe.wait_ge(z_acc.sem, z_acc.at(j, HF - 1, 3))
                    lo, hi = ZCH[c]
                    pe.wait_ge(*free_for(j, use))
                    apart(pe)
                    t = bank(use)
                    for i in range(NT):
                        zi = Z[:, i, :, :].rearrange("p e d -> p (e d)")
                        last = nc.tensor.transpose(t[0:hi - lo, i * P:(i + 1) * P], zi[:, lo:hi], ident[:, :])
                    last.then_inc(is_full(use), 1)

                def f_output():
                    if not f_end:
                        return skip("F out")
                    pe.wait_ge(*drained(j, "ZT2"))
                    pe.wait_ge(*drained(j, "ZT1"))
                    pe.wait_ge(*free_for(j, "F out"))
                    t = bank("F out")
                    for i in range(NT):
                        for c, (lo, hi) in enumerate(ZCH):
                            last = nc.tensor.matmul(t[:, i * C:(i + 1) * C], ZT[0:hi - lo, c, i * P:(i + 1) * P],
                                                    wo_s[0:hi - lo, c, :], start=(c == 0), stop=(c == 2))
                    last.then_inc(is_full("F out"), 1)

                for slot in range(NS):
                    for b in range(STEPS):
                        if b < N_BANKS[slot]:
                            pass2(slot, b)
                        if b < N_BANKS[(slot + AHEAD) % NS]:
                            pass1(slot, b)
                        if b % 2 == 1 and b < 2 * NT:
                            values(slot, b // 2)
                        at = (slot, b)
                        if b == 0 and slot in (0, 1, 6, 7):
                            denominator_transposes(slot)
                        if at == (7, 2):
                            f_project(1)
                        if b == 3:
                            rows((slot + 1) % NS)
                        if at == (2, 4):
                            xn_transposes("A xnT", a_prep)
                        if at == (2, 6):
                            a_project("A q")
                        if at == (2, 7):
                            a_project("A qp")
                        if at == (3, 4):
                            a_project("A k")
                            a_project("A kp")
                        if at == (5, 1):
                            a_project_values()
                        if at == (5, 4):
                            a_y_transposes()
                        if at == (5, 6):
                            a_output()
                        if at == (6, 5):
                            xn_transposes("F xnT", f_prep)
                        if at in ((6, 8), (7, 4), (7, 5)):
                            f_project((0, 2, 3)[((6, 8), (7, 4), (7, 5)).index(at)])
                        if at == (7, 6):
                            f_gates(0)
                            f_gates(1)
                        if b == 7 and slot in (0, 5, 6, 7):
                            denominators(slot)
                        if at == (7, 8):
                            f_gates(2)
                            f_gates(3)
                        if at == (1, 6):
                            z_transposes(0)
                            z_transposes(1)
                        if at == (1, 7):
                            z_transposes(2)
                        if at == (1, 8):
                            f_output()
                        if b == 9:
                            value_transposes(slot)

            for j in range(HEAD):
                iteration(j, **parts_of(j))
            with pe.Fori(HEAD, UNITS) as j:
                iteration(j, **ALL)
            for j in range(UNITS, LAST):
                iteration(j, **parts_of(j))

        @block.scalar
        def _(act):
            for s in (exps_done, y_copied, part0_ready, part1_ready, sig_e, hi_ready):
                act.sem_inc(s.sem, s.first)
            act.wait_ge(consts_loaded.sem, 16 * NSET)
            nc.scalar.activation(identb[:, :], ident[:, :], ACT.Copy).then_inc(consts_cast.sem, 1)
            nc.scalar.activation(maskb[:, :], maskf, ACT.Copy).then_inc(consts_cast.sem, 1)

            def iteration(j, a, f, f_end, a_prep, f_prep):
                def drain(use, dst, src):
                    act.wait_ge(*filled(j, use))
                    nc.scalar.activation(dst, src, ACT.Copy).then_inc(is_free(use), 1)

                def exps(slot, b):
                    n = BEFORE2[slot] + b + 1
                    if b == 0:
                        act.wait_ge(y_filled.sem, y_filled.at(j, slot))
                    act.wait_ge(s2_filled.sem, s2_filled.at(j, n))
                    nc.scalar.activation(PT[:, slot % 2, b, :], S2[(n - 1) % len(S2)][:, :], ACT.Exp,
                                         scale=SCALE_A if slot < SA else SCALE_F).then_inc(exps_done.sem, 1)

                def rows(group):
                    if not (a_prep if group == 0 else a if group < SA else f):
                        return
                    t = bank(f"rows{group}")
                    if group < SA:
                        act.wait_ge(rowsA_in.sem, rowsA_in.at(j, 2 * group, 1 if group else 0))
                        drain(f"rows{group}", mrowA[:, :], t[:, :].bitcast(BF)[0:2 * GA * NT, 0:P])
                    else:
                        act.wait_ge(rowsF_in.sem, rowsF_in.at(j, group - SA, 2))
                        drain(f"rows{group}", mrowF[:, :], t[0:GF * NT, 0:P])

                def part0(qk):
                    act.wait_ge(rot_ready.sem, rot_ready.at(j, qk + 1))
                    if qk == 0:
                        act.wait_ge(scattered.sem, scattered.at(j, 0))
                    nc.scalar.activation(parts[:, qk, 0, :], rot, ACT.Copy).then_inc(part0_ready.sem, 1)

                def part1(qk):
                    act.wait_ge(rest1_ready.sem, rest1_ready.at(j, qk + 1))
                    nc.scalar.activation(parts[:, qk, 1, :], rot2, ACT.Copy).then_inc(part1_ready.sem, 1)

                def f_stage(p):
                    act.wait_ge(low_ready.sem, low_ready.at(j, 2 * p + 2, 2))
                    for i, use in enumerate((f"F q{p}", f"F k{p}")):
                        drain(use, stage[:, i, p, :], bank(use)[:, :])

                def high_parts(g, qk):
                    if qk == 0:
                        act.wait_ge(s2_filled.sem, s2_filled.at(j, BEFORE2[g + 3]))
                    for h in range(GF):
                        own = slice(DF * h, DF * h + DF)
                        last = nc.scalar.activation((XQ, XK)[qk][own, g % 2, h, :], stage[own, qk, g, :], ACT.Copy)
                    last.then_inc(hi_ready.sem, 1)

                def f_gates(i):
                    use = f"F gate{i}"
                    if i == 0:
                        act.wait_ge(v_mult.sem, v_mult.at(j, v_mult.per, 2))
                    act.wait_ge(*filled(j, use))
                    nc.scalar.activation(gate[:, i, :, :].rearrange("p g e -> p (g e)"), bank(use)[:, 0:NG], ACT.Copy)
                    nc.scalar.activation(xv[:, i, :], bank(use)[:, NG:NG + NX], ACT.Copy).then_inc(is_free(use), 1)

                for slot in range(NS):
                    for b in range(STEPS):
                        if b < N_BANKS[slot] and (a if slot < SA else f):
                            exps(slot, b)
                        at = (slot, b)
                        if b == 8 and (f_end if slot == 0 else a if slot <= SA else f):
                            act.wait_ge(y_filled.sem, y_filled.at(j, slot + 1))
                            nc.scalar.activation(ySB[:, :], Y[:, :], ACT.Copy).then_inc(y_copied.sem, 1)
                        if 3 <= slot < 7 and b < 2 and f:
                            high_parts(slot - 3, b)
                        if at == (7, 2) and f_prep:
                            f_stage(1)
                        if b == 3:
                            rows((slot + 1) % NS)
                        if b == 8 and (f_end if slot == 0 else f if slot > 4 else False):
                            use = f"den{(slot - 1) % NS - SA}"
                            drain(use, dSB[:, :], bank(use)[:, :])
                        if at == (2, 5) and a_prep:
                            act.wait_ge(*filled(j, "A v", 1))
                            act.wait_ge(*filled(j, "F gate3", 1))
                            drain("A xnT", xnT[:, :], bank("A xnT")[:, :])
                        if at in ((2, 9), (3, 8)) and a_prep:
                            part0(slot - 2)
                        if at in ((3, 1), (4, 0)) and a_prep:
                            part1(slot - 3)
                        if at == (5, 5) and a:
                            drain("A yNT", yT[:, :], bank("A yNT")[:, :])
                        if at == (6, 6) and f_prep:
                            act.wait_ge(*filled(j, "A v"))
                            drain("F xnT", xnT[:, :], bank("F xnT")[:, :])
                        if at in ((6, 8), (7, 4), (7, 5)) and f_prep:
                            f_stage((0, 2, 3)[((6, 8), (7, 4), (7, 5)).index(at)])
                        if at == (7, 6) and f_prep:
                            f_gates(0)
                            f_gates(1)
                        if at == (7, 8) and f_prep:
                            f_gates(2)
                            f_gates(3)
                        if slot == 1 and b in (6, 7) and f_end:
                            for c in ((0, 1), (2,))[b - 6]:
                                lo, hi = ZCH[c]
                                if c == 0:
                                    act.wait_ge(scattered.sem, scattered.at(j, 0))
                                drain(f"ZT{c}", ZT[0:hi - lo, c, :], bank(f"ZT{c}")[0:hi - lo, :])
                        if at == (7, 9) and f_prep:
                            act.wait_ge(*drained(j, "F gate2"))
                            act.wait_ge(*drained(j, "F gate3"))
                            nc.scalar.activation(wv_s[:, :, :, :].rearrange("p t h e -> p t (h e)"),
                                                 gate[:, :, 0:HF, :].rearrange("p t h e -> p t (h e)"),
                                                 ACT.Exp, scale=-1.0).then_inc(sig_e.sem, 1)

            for j in range(HEAD):
                iteration(j, **parts_of(j))
            with act.Fori(HEAD, UNITS) as j:
                iteration(j, **ALL)
            for j in range(UNITS, LAST):
                iteration(j, **parts_of(j))

        @block.vector
        def _(dve):
            for s in (m0_drained, m1_drained, s1_drained, resA_ready, resF_ready, varA_ready, varF_ready, xnA_ready,
                      xnF_ready, nmb_ready, cast_done, v_mult, z_mult, lnA_chain, lnF_chain, outA_chain, maxA_chain,
                      normA_chain, pick_chain, mix_chain, low_ready):
                dve.sem_inc(s.sem, s.first)
            nc.vector.memset(Qs[:, :, :], 0.0).then_inc(dve_init.sem, 1)
            nc.vector.memset(Ks[:, :, :], 0.0).then_inc(dve_init.sem, 1)
            nc.vector.memset(Y[:, :], 0.0).then_inc(dve_init.sem, 1)
            nc.vector.memset(Vs[:, :, :, :], 1.0).then_inc(dve_init.sem, 1)
            nc.vector.memset(KL[DF:DF + 1, :, :, :].bitcast(F32), 1.0).then_inc(dve_init.sem, 1)
            nc.vector.memset(ones[:, :], 1.0).then_inc(dve_init.sem, 1)
            nc.vector.memset(minus_half[:, :], -0.5).then_inc(dve_init.sem, 1)
            dve.wait_ge(dve_init.sem, 2)
            nc.vector.memset(Ks[ROWS_P1:ROWS_P2, :, :], 1.0).then_inc(dve_init.sem, 1)
            dve.wait_ge(dve_init.sem, dve_init.per)

            def iteration(j, a, f, f_end, a_prep, f_prep):
                def variances(chain, var_ready, lag):
                    for i in range(NT):
                        last = nc.vector.bn_stats(stats[:, i, :], xl[:, i, :])
                    last.then_inc(chain.sem, 1)
                    dve.wait_ge(chain.sem, chain.at(j, 1, lag))
                    apart(dve)
                    for i in range(NT):
                        last = nc.vector.bn_aggr(mv[:, i, :], stats[:, i, :])
                    last.then_inc(chain.sem, 1)
                    dve.wait_ge(chain.sem, chain.at(j, 2, lag))
                    nc.vector.tensor_scalar(var_eps[:, :], mv[:, :, 1], EPS, None, ALU.add).then_inc(var_ready.sem, 1)

                def normalise(rstd_ready, xn_ready, lag):
                    dve.wait_ge(rstd_ready.sem, rstd_ready.at(j, 1, lag))
                    for i in range(NT):
                        last = nc.vector.tensor_scalar(xn[:, i, :], xl[:, i, :], mv[:, i, 0:1], rstd[:, i:i + 1],
                                                       ALU.subtract, ALU.mult)
                    last.then_inc(xn_ready.sem, 1)

                def rotate(qk, half):
                    use = (("A q", "A qp"), ("A k", "A kp"))[qk][half]
                    if qk == 0 and half == 0:
                        dve.wait_ge(wa_loaded.sem, wa_loaded.at(j, 4))
                    if qk and half == 0:
                        dve.wait_ge(part2_ready.sem, part2_ready.at(j, 1))
                    dve.wait_ge(*filled(j, use))
                    nc.vector.scalar_tensor_tensor((rot, rot2)[half], bank(use)[:, :],
                                                   ba_s[:, 2 * qk + half:2 * qk + half + 1], tab_s[:, half, :],
                                                   ALU.add, ALU.mult).then_inc(is_free(use), 1)

                def a_values():
                    dve.wait_ge(y_filled.sem, y_filled.at(j, SA + 1))
                    dve.wait_ge(*filled(j, "A v"))
                    nc.vector.tensor_tensor(
                        Vs[:, :, :, 0:DA], bank("A v")[:, :].rearrange("p (t h d) -> p t h d", t=NT, h=HA),
                        bv_s[:, :].rearrange("p (h d) -> p h d", h=HA).unsqueeze(1).broadcast_to([P, NT, HA, DA]),
                        ALU.add).then_inc(is_free("A v"), 1)

                def maxima(slot, b):
                    group, n = (slot + AHEAD) % NS, BEFORE1[slot] + b + 1
                    dve.wait_ge(s1_filled.sem, s1_filled.at(j, n))
                    t = S1[(n - 1) % len(S1)]
                    if group < SA:
                        segs = BANKS_A1[b]
                        h0, qt0, _ = segs[0]
                        if len(segs) == 2 and segs[1][1] == qt0:
                            last = nc.vector.tensor_reduce(nmaxA[:, GA * group + h0:GA * group + h0 + 2, qt0],
                                                           t[:, :].rearrange("p (h k) -> p h k", h=2), AX.X, ALU.max,
                                                           negate=True)
                        else:
                            for h, qt, col in segs:
                                last = nc.vector.tensor_reduce(nmaxA[:, GA * group + h, qt:qt + 1],
                                                               t[:, col:col + (qt + 1) * P], AX.X, ALU.max, negate=True)
                        last.then_inc(s1_drained.sem, 1)
                    else:
                        h, qt = divmod(b, NT)
                        nc.vector.tensor_reduce(nmaxF[:, GF * (group - SA) + h, qt:qt + 1], t[:, :], AX.X, ALU.max,
                                                negate=True).then_inc(s1_drained.sem, 1)

                def split_maxima(group, lag):
                    slot = (group - AHEAD) % NS
                    n = BEFORE1[slot] + NA_B
                    dve.wait_ge(s1_drained.sem, s1_drained.at(j, n, 1 if group == 1 else 0))
                    before = (group - 1) % SA
                    dve.wait_ge(*filled(j, f"rows{before}", 1 if group == 1 else 0))
                    src = nmaxA[:, GA * group:GA * group + GA, :]
                    nc.vector.tensor_copy(nmb[:, 0, :, :], src).then_inc(maxA_chain.sem, 1)
                    dve.wait_ge(maxA_chain.sem, maxA_chain.at(j, group + 1, lag))
                    nc.vector.tensor_tensor(nmb[:, 1, :, :], src, nmb[:, 0, :, :], ALU.subtract).then_inc(nmb_ready.sem, 1)

                def a_norm(g):
                    dve.wait_ge(*filled(j, f"YT{g}"))
                    v = bank(f"YT{g}")[:, :].rearrange("p (t h r) -> p t h r", t=NT, h=GA)
                    nc.vector.reciprocal(recA[:, :, :], v[:, :, :, DA]).then_inc(normA_chain.sem, 1)
                    dve.wait_ge(normA_chain.sem, normA_chain.at(j, g + 1, 1))
                    nc.vector.tensor_tensor(
                        yN[:, :, GA * DA * g:GA * DA * (g + 1)].rearrange("p t (h d) -> p t h d", h=GA), v[:, :, :, 0:DA],
                        recA[:, :, :].unsqueeze(3).broadcast_to([P, NT, GA, DA]),
                        ALU.mult).then_inc(is_free(f"YT{g}"), 1)

                def a_output():
                    dve.wait_ge(xrA_loaded.sem, xrA_loaded.at(j, 3, 1))
                    dve.wait_ge(resF_stored.sem, resF_stored.at(j, 1, 3))
                    nc.vector.tensor_tensor(res[:, :, :], xr[:, :, :],
                                            bp_s[:, :].unsqueeze(1).broadcast_to([P, NT, C]),
                                            ALU.add).then_inc(outA_chain.sem, 1)
                    dve.wait_ge(outA_chain.sem, outA_chain.at(j, 1, 1))
                    dve.wait_ge(*filled(j, "A out"))
                    flat = res[:, :, :].rearrange("p t c -> p (t c)")
                    nc.vector.tensor_tensor(flat, bank("A out")[:, :], flat, ALU.add).then_inc(resA_ready.sem, 1)
                    dve.wait_ge(resA_ready.sem, resA_ready.at(j, 1, 1))
                    dve.sem_inc(is_free("A out"), 1)

                def low_part(g, qk):
                    dve.wait_ge(hi_ready.sem, hi_ready.at(j, 2 * g + qk + 1, 2))
                    for h in range(GF):
                        own = slice(DF * h, DF * h + DF)
                        to = slice(0, DF) if qk else slice(DF - DF * h, P - DF * h)
                        last = nc.vector.tensor_tensor((XQ, KL)[qk][to, g % 2, h, :], stage[own, qk, g, :],
                                                       (XQ, XK)[qk][own, g % 2, h, :], ALU.subtract)
                    last.then_inc(low_ready.sem, 1)

                def f_cast(p):
                    for i, dst in enumerate((Qb, Kb)):
                        dve.wait_ge(*drained(j, (f"F q{p}", f"F k{p}")[i]))
                        nc.vector.tensor_copy(dst[:, p, :], stage[:, i, p, :]).then_inc(cast_done.sem, 1)

                def f_compare():
                    dve.wait_ge(*drained(j, "F gate2", 1))
                    dve.wait_ge(*drained(j, "F gate3", 1))
                    gl = gate[:, :, :, :].rearrange("p t g e -> p (t g) e")
                    n_gl = NT * 2 * HF
                    for e in range(E):
                        last = nc.vector.tensor_tensor(cmp_[:, :, 0:e + 1, e], gl[:, :, e:e + 1].broadcast_to([P, n_gl, e + 1]),
                                                       gl[:, :, 0:e + 1], ALU.is_gt)
                        if e < E - 1:
                            last = nc.vector.tensor_tensor(cmp_[:, :, e + 1:E, e],
                                                           gl[:, :, e:e + 1].broadcast_to([P, n_gl, E - 1 - e]),
                                                           gl[:, :, e + 1:E], ALU.is_ge)
                    last.then_inc(pick_chain.sem, 1)

                def f_count():
                    dve.wait_ge(pick_chain.sem, pick_chain.at(j, 1, 2))
                    pk = pick[:, :, :, :].rearrange("p t g e -> p (t g) e")
                    nc.vector.tensor_reduce(pk, cmp_[:, :, :, :], AX.X, ALU.add).then_inc(pick_chain.sem, 1)

                def f_pick():
                    dve.wait_ge(pick_chain.sem, pick_chain.at(j, 2, 2))
                    pk = pick[:, :, :, :].rearrange("p t g e -> p (t g) e")
                    nc.vector.tensor_scalar(pk, pk, 1.5, None, ALU.is_lt).then_inc(pick_chain.sem, 1)

                def f_sigmoid(step):
                    wv2 = wv_s[:, :, :, :].rearrange("p t h e -> p (t h e)")
                    if step == 0:
                        dve.wait_ge(sig_e.sem, sig_e.at(j, 1, 2))
                        nc.vector.tensor_scalar(wv2, wv2, 1.0, None, ALU.add).then_inc(pick_chain.sem, 1)
                    if step == 1:
                        dve.wait_ge(pick_chain.sem, pick_chain.at(j, 4, 2))
                        nc.vector.reciprocal(wv2, wv2).then_inc(pick_chain.sem, 1)
                    if step == 2:
                        dve.wait_ge(pick_chain.sem, pick_chain.at(j, 5, 2))
                        nc.vector.tensor_tensor(wv_s[:, :, :, :].rearrange("p t h e -> p t (h e)"),
                                                wv_s[:, :, :, :].rearrange("p t h e -> p t (h e)"),
                                                pick[:, :, 0:HF, :].rearrange("p t h e -> p t (h e)"),
                                                ALU.mult).then_inc(pick_chain.sem, 1)

                def f_value_product(i, e):
                    if i == 0 and e == 0:
                        dve.wait_ge(pick_chain.sem, pick_chain.at(j, 6, 2))
                        dve.wait_ge(y_filled.sem, y_filled.at(j, 1))
                        dve.wait_ge(z_acc.sem, z_acc.at(j, HF - 1, 3))
                    n = i * (E - 1) + e
                    if e and n > VBUF:
                        dve.wait_ge(v_acc.sem, v_acc.at(j, n - VBUF, 2))
                    nc.vector.tensor_tensor(
                        vtmp[:, n % VBUF, :, :] if e else Vf[:, i, :, :],
                        xv[:, i:i + 1, e * DF:(e + 1) * DF].broadcast_to([P, HF, DF]),
                        wv_s[:, i, :, e:e + 1].broadcast_to([P, HF, DF]), ALU.mult).then_inc(v_mult.sem, 1)

                def f_mix_weights(slot):
                    g, lag = (slot - 2) % NS - SA, 3 if slot < 2 else 2
                    dve.wait_ge(*filled(j, f"denT{g}"))
                    v = bank(f"denT{g}")[:, :].rearrange("p (t h k r) -> p t h k r", t=NT, h=GF, k=2)
                    nc.vector.tensor_reduce(denF[:, :, :], v[:, :, :, :, 0], AX.X, ALU.add).then_inc(is_free(f"denT{g}"), 1)
                    dve.wait_ge(*drained(j, f"denT{g}"))
                    nc.vector.reciprocal(recF[:, :, :], denF[:, :, :]).then_inc(mix_chain.sem, 1)
                    dve.wait_ge(mix_chain.sem, mix_chain.at(j, 2 * g + 1, lag))
                    nc.vector.tensor_tensor(wz[:, :, :, :], pick[:, :, HF + GF * g:HF + GF * g + GF, :],
                                            recF[:, :, :].unsqueeze(3).broadcast_to([P, NT, GF, E]),
                                            ALU.mult).then_inc(mix_chain.sem, 1)

                def f_mix(g, h, lag):
                    if h == 0:
                        dve.wait_ge(mix_chain.sem, mix_chain.at(j, 2 * g + 2, lag))
                        dve.wait_ge(*filled(j, f"YT{SA + g}", 1 if g == SF - 2 else 0))
                    y = bank(f"YT{SA + g}")[:, :].rearrange("p (t h d) -> p t h d", t=NT, h=GF)
                    hh = GF * g + h
                    if hh == 1:
                        dve.wait_ge(v_acc.sem, v_acc.at(j, v_acc.per, lag))
                    if hh > 2:
                        dve.wait_ge(z_acc.sem, z_acc.at(j, hh - 2, lag))
                    nc.vector.tensor_tensor(ztmp[:, hh % 2, :, :, :] if hh else Z[:, :, :, :],
                                            y[:, :, h:h + 1, :].broadcast_to([P, NT, E, DF]),
                                            wz[:, :, h, :].unsqueeze(3).broadcast_to([P, NT, E, DF]),
                                            ALU.mult).then_inc(z_mult.sem, 1)
                    if h == GF - 1:
                        dve.wait_ge(z_mult.sem, z_mult.at(j, GF * g + GF, lag))
                        dve.sem_inc(is_free(f"YT{SA + g}"), 1)

                def f_output():
                    dve.wait_ge(xrF_loaded.sem, xrF_loaded.at(j, 1, 3))
                    dve.wait_ge(resA_stored.sem, resA_stored.at(j, 1, 2))
                    dve.wait_ge(*filled(j, "F out"))
                    nc.vector.tensor_tensor(res[:, :, :].rearrange("p t c -> p (t c)"), bank("F out")[:, :],
                                            xr[:, :, :].rearrange("p t c -> p (t c)"), ALU.add).then_inc(resF_ready.sem, 1)
                    dve.wait_ge(resF_ready.sem, resF_ready.at(j, 1, 3))
                    dve.sem_inc(is_free("F out"), 1)

                for slot in range(NS):
                    nxt = (slot + 1) % NS
                    if nxt < SA and (a if nxt else a_prep):
                        split_maxima(nxt, 1 if nxt else 0)
                    for b in range(STEPS):
                        if b < N_BANKS[(slot + AHEAD) % NS] and (a if slot < 2 else f if slot < 6 else a_prep):
                            maxima(slot, b)
                        at = (slot, b)
                        if b in (0, 2) and slot in (0, 1, 6, 7) and (f if slot > 1 else f_end):
                            if b == 0:
                                f_mix_weights(slot)
                            f_mix((slot - 2) % NS - SA, b // 2, 3 if slot < 2 else 2)
                        if b in (1, 3) and 3 <= slot < 7 and f:
                            low_part(slot - 3, b // 2)
                        if at == (1, 6) and a_prep:
                            dve.wait_ge(xlA_loaded.sem, xlA_loaded.at(j, 1))
                            variances(lnA_chain, varA_ready, 0)
                        if at == (1, 9) and a_prep:
                            normalise(rstdA_ready, xnA_ready, 0)
                        if at in ((2, 6), (2, 7), (3, 5), (3, 6)) and a_prep:
                            rotate(*divmod(((2, 6), (2, 7), (3, 5), (3, 6)).index(at), 2))
                        if at == (5, 2) and a_prep:
                            a_values()
                        if at == (5, 7) and a:
                            a_output()
                        if at == (0, 3) and f:
                            f_compare()
                        if at == (1, 3) and f:
                            f_count()
                        if at == (1, 4) and f:
                            f_pick()
                            f_sigmoid(0)
                        if at == (1, 5) and f:
                            f_sigmoid(1)
                        if at == (1, 9) and f:
                            f_sigmoid(2)
                        if at in V_STEPS and f:
                            f_value_product(*divmod(V_STEPS.index(at), E))
                        if at == (1, 8) and f_end:
                            f_output()
                        if at == (6, 2) and f_prep:
                            dve.wait_ge(xlF_loaded.sem, xlF_loaded.at(j, 1, 1))
                            variances(lnF_chain, varF_ready, 1)
                        if at == (6, 4) and f_prep:
                            normalise(rstdF_ready, xnF_ready, 1)
                        if at in ((7, 2), (7, 5), (7, 6), (7, 7)) and f_prep:
                            f_cast(((7, 2), (7, 5), (7, 6), (7, 7)).index(at))
                        if b == 9 and 1 <= slot <= SA and a:
                            a_norm(slot - 1)

            for j in range(HEAD):
                iteration(j, **parts_of(j))
            with dve.Fori(HEAD, UNITS) as j:
                iteration(j, **ALL)
            for j in range(UNITS, LAST):
                iteration(j, **parts_of(j))

        @block.gpsimd
        def _(pool):
            for s in (rstdA_ready, rstdF_ready, rot_ready, rest1_ready, part2_ready, masked, v_acc, z_acc):
                pool.sem_inc(s.sem, s.first)
            pool.wait_ge(dve_init.sem, dve_init.per)

            def iteration(j, a, f, f_end, a_prep, f_prep):
                def mask(slot, b):
                    pool.wait_ge(exps_done.sem, exps_done.at(j, BEFORE2[slot] + b + 1))
                    apart(pool)
                    for h, kt, col in BANKS_A2[b]:
                        v = PT[:, slot % 2, b, col:col + P]
                        last = nc.gpsimd.affine_select(out=v, in_=v, compare_op=ALU.is_ge, fill=0.0, base=0,
                                                       pattern=[[1, P]], channel_multiplier=-1)
                    last.then_inc(masked.sem, 1)

                def rot_sum(qk):
                    for use in (("A q", "A qp"), ("A k", "A kp"))[qk]:
                        pool.wait_ge(*drained(j, use))
                    nc.gpsimd.tensor_tensor(rot, rot, rot2, ALU.add).then_inc(rot_ready.sem, 1)

                def rest1(qk):
                    pool.wait_ge(part0_ready.sem, part0_ready.at(j, qk + 1))
                    nc.gpsimd.tensor_tensor(rot2, rot, parts[:, qk, 0, :], ALU.subtract).then_inc(rest1_ready.sem, 1)

                def part2(qk):
                    pool.wait_ge(part1_ready.sem, part1_ready.at(j, qk + 1))
                    nc.gpsimd.tensor_tensor(parts[:, qk, 2, :], rot2, parts[:, qk, 1, :],
                                            ALU.subtract).then_inc(part2_ready.sem, 1)

                def f_value_sum(i, e):
                    if e == 0:
                        return
                    n = i * (E - 1) + e
                    pool.wait_ge(v_mult.sem, v_mult.at(j, i * E + e + 1, 2))
                    if n > 1:
                        pool.wait_ge(v_acc.sem, v_acc.at(j, n - 1, 2))
                    nc.gpsimd.tensor_tensor(Vf[:, i, :, :], Vf[:, i, :, :], vtmp[:, n % VBUF, :, :],
                                            ALU.add).then_inc(v_acc.sem, 1)

                def f_mix(g, h, lag):
                    hh = GF * g + h
                    if hh:
                        pool.wait_ge(z_mult.sem, z_mult.at(j, hh + 1, lag))
                        if hh > 1:
                            pool.wait_ge(z_acc.sem, z_acc.at(j, hh - 1, lag))
                        nc.gpsimd.tensor_tensor(Z[:, :, :, :], Z[:, :, :, :], ztmp[:, hh % 2, :, :, :],
                                                ALU.add).then_inc(z_acc.sem, 1)

                for slot in range(NS):
                    for b in range(STEPS):
                        if slot < SA and a:
                            mask(slot, b)
                        at = (slot, b)
                        if b in (1, 3) and slot in (0, 1, 6, 7) and (f if slot > 1 else f_end):
                            f_mix((slot - 2) % NS - SA, b // 2, 3 if slot < 2 else 2)
                        if at == (1, 6) and a_prep:
                            pool.wait_ge(varA_ready.sem, varA_ready.at(j, 1))
                            nc.gpsimd.tensor_tensor(rstd[:, :], var_eps[:, :], minus_half[:, :],
                                                    ALU.pow).then_inc(rstdA_ready.sem, 1)
                        if at in ((2, 7), (3, 6)) and a_prep:
                            rot_sum(slot - 2)
                        if at in ((2, 9), (3, 8)) and a_prep:
                            rest1(slot - 2)
                        if at in ((3, 2), (4, 1)) and a_prep:
                            part2(slot - 3)
                        if at in V_STEPS and f:
                            f_value_sum(*divmod(V_STEPS.index(at), E))
                        if at == (6, 2) and f_prep:
                            pool.wait_ge(varF_ready.sem, varF_ready.at(j, 1, 1))
                            nc.gpsimd.tensor_tensor(rstd[:, :], var_eps[:, :], minus_half[:, :],
                                                    ALU.pow).then_inc(rstdF_ready.sem, 1)

            for j in range(HEAD):
                iteration(j, **parts_of(j))
            with pool.Fori(HEAD, UNITS) as j:
                iteration(j, **ALL)
            for j in range(UNITS, LAST):
                iteration(j, **parts_of(j))


def kernel(L0_attn_a_x, L0_attn_a_wq, L0_attn_a_bq, L0_attn_a_wk, L0_attn_a_bk, L0_attn_a_wv, L0_attn_a_bv, L0_attn_a_wp,
           L0_attn_a_bp, L0_attn_b_W_attn, L0_attn_b_b_attn, L0_attn_b_W_proj, L0_attn_b_b_proj, L0_ffn_Wq, L0_ffn_Wk,
           L0_ffn_Ws, L0_ffn_Wd, L0_ffn_Wv, L0_ffn_Wo):
    import concourse.bacc as bacc
    from concourse.bass_utils import run_bass_kernel_spmd

    x = np.ascontiguousarray(L0_attn_a_x)
    B, T, C = x.shape
    H, D = 16, C // 16
    plain = [h * D + d for d in range(D) for h in range(H)]
    swapped = [h * D + (d + D // 2) % D for d in range(D) for h in range(H)]

    def layout(wq, wk, wv, wp, bq, bk, bv, bp):
        w = np.stack([wq[:, plain], wq[:, swapped], wk[:, plain], wk[:, swapped], wv], 1)
        b = np.stack([bq[plain], bq[swapped], bk[plain], bk[swapped]], 1)
        return w, wp, b, np.broadcast_to(bv, (C, C)), np.broadcast_to(bp, (C, C))

    a = layout(*(np.asarray(w).T for w in (L0_attn_a_wq, L0_attn_a_wk, L0_attn_a_wv, L0_attn_a_wp)),
               *(np.asarray(b) for b in (L0_attn_a_bq, L0_attn_a_bk, L0_attn_a_bv, L0_attn_a_bp)))
    Wb, bb = np.asarray(L0_attn_b_W_attn), np.asarray(L0_attn_b_b_attn)
    b = layout(Wb[:, :C], Wb[:, C:2 * C], Wb[:, 2 * C:], np.asarray(L0_attn_b_W_proj), bb[:C], bb[C:2 * C], bb[2 * C:],
               np.asarray(L0_attn_b_b_proj))

    half = D // 2
    i = np.arange(half, dtype=np.float32)
    f32 = np.float32
    ang_a = np.arange(T, dtype=f32)[None] * (f32(1.0) / f32(10000.0) ** (f32(2.0) * i / f32(D)))[:, None]
    ang_b = np.arange(T, dtype=f32)[None] / (f32(1250.0) ** (f32(2.0) * i / f32(D)))[:, None]
    tabs = []
    for ang in (ang_a, ang_b):
        cos, sin = np.cos(ang), np.sin(ang)
        tabs.append(np.stack([np.repeat(np.concatenate([cos, cos]), H, 0), np.repeat(np.concatenate([-sin, sin]), H, 0)], 1))

    Wv, Wo = np.asarray(L0_ffn_Wv), np.asarray(L0_ffn_Wo)
    E, _, DH = Wv.shape
    HE = L0_ffn_Ws.shape[1]
    arrays = {
        "x": x,
        "wa": np.stack([a[0], b[0]]),
        "wp": np.stack([a[1], b[1]]),
        "ba": np.stack([a[2], b[2]]),
        "bv": np.stack([a[3], b[3]]),
        "bp": np.stack([a[4], b[4]]),
        "tab": np.stack(tabs).astype(np.float32),
        "wqk": np.concatenate([np.asarray(L0_ffn_Wq), np.asarray(L0_ffn_Wk)], 1),
        "wgv": np.concatenate([np.asarray(L0_ffn_Ws), np.asarray(L0_ffn_Wd), Wv.transpose(1, 0, 2).reshape(C, E * DH)], 1),
        "wo": Wo.reshape(E * DH, C),
        "ident": np.eye(128, dtype=np.float32),
        "mask": np.triu(np.full((128, 128), -1e30, np.float32), 1),
    }
    arrays = {n: np.ascontiguousarray(v) for n, v in arrays.items()}
    nc = bacc.Bacc("TRN2", target_bir_lowering=False, num_devices=1)
    args = [nc.dram_tensor(f"in_{n}", v.shape, mybir.dt.from_np(v.dtype), kind="ExternalInput").ap()
            for n, v in arrays.items()]
    args.append(nc.dram_tensor("out_x", (B, T, C), mybir.dt.float32, kind="ExternalOutput").ap())
    attention_and_mixture(nc, *args)
    r = run_bass_kernel_spmd(nc, [{f"in_{n}": v for n, v in arrays.items()}], core_ids=[0])
    return r.results[0]["out_x"]
```

```python
import numpy as np
import concourse.bass as bass
from concourse import mybir
from contextlib import ExitStack



def attention_and_mixture(nc, x, wa, wp, ba, bv, bp, tab, wqk, wgv, wo, ident_in, mask_in, out):
    F32, F32R, BF = mybir.dt.float32, mybir.dt.float32r, mybir.dt.bfloat16
    ALU, ACT, AX = mybir.AluOpType, mybir.ActivationFunctionType, mybir.AxisListType

    B, T, C = x.shape
    P = 128
    NT = T // P
    ROUNDS = wa.shape[0]
    UNITS = ROUNDS * B
    HEAD, LAST = 3, UNITS + 3
    EPS = 1e-5
    HA, DA = 16, C // 16
    GA = 4
    SA = HA // GA
    SCALE_A = float(1.0 / np.sqrt(np.float32(DA)))
    SPLITS_Q = (0, 1, 0, 1, 2, 0)
    SPLITS_K = (0, 0, 1, 1, 0, 2)
    NSP = len(SPLITS_Q)
    ROWS_P1 = 96
    ROWS_P2 = ROWS_P1 + 2
    HF, DF, E = 8, 64, wo.shape[0] // 64
    GF = 2
    SF = HF // GF
    SCALE_F = float(DF) ** -0.5
    PAIRS = HF // 2
    NG = 2 * HF * E
    NX = E * DF
    ZCH = [(0, 128), (128, 256), (256, NX)]

    BANKS_A1 = []
    BANKS_A2 = []
    for pair in range(GA // 2):
        h0, h1 = 2 * pair, 2 * pair + 1
        for h in (h0, h1):
            BANKS_A1 += [[(h, 3, 0)], [(h, 2, 0), (h, 0, 384)]]
            BANKS_A2 += [[(h, 0, 0)], [(h, 1, 0), (h, 3, 384)]]
        BANKS_A1.append([(h0, 1, 0), (h1, 1, 256)])
        BANKS_A2.append([(h0, 2, 0), (h1, 2, 256)])
    NA_B = len(BANKS_A1)
    NF_B = GF * NT

    ctx = ExitStack()
    with ctx:
        def sb(name, shape, dt=F32):
            return ctx.enter_context(nc.sbuf_tensor(name, shape, dt))

        def pb(name, dt=F32):
            return ctx.enter_context(nc.psum_tensor(name, [P, 512], dt))

        waits_passed = {e: ctx.enter_context(nc.semaphore(f"waits_passed_{n}")) for n, e in
                        (("sp", nc.sync), ("pool", nc.gpsimd), ("dve", nc.vector), ("pe", nc.tensor))}

        def apart(eng):
            eng.sem_inc(waits_passed[eng], 1)

        class Signal:

            def __init__(self, name, per, unit=1, times=UNITS):
                self.sem = ctx.enter_context(nc.semaphore(name))
                self.per, self.unit, self.times = per, unit, times
                self.first = per * unit

            def at(self, j, n, lag=0):
                value = j * self.first + ((1 - lag) * self.per + n) * self.unit
                return min(max(value, 0), (self.times + 1) * self.first) if isinstance(j, int) else value

        ident = sb("ident", [P, P])
        identb = sb("identb", [P, P], BF)
        maskb = sb("maskb", [P, P], BF)
        wa_s = sb("wa_s", [P, 5, C])
        wp_s = sb("wp_s", [P, C])
        bp_s = sb("bp_s", [P, C])
        ba_s = sb("ba_s", [P, 4])
        bv_s = sb("bv_s", [P, C])
        tab_s = sb("tab_s", [P, 2, T])
        xl = sb("xl", [P, NT, C])
        xr = sb("xr", [P, NT, C])
        xn = sb("xn", [P, NT, C])
        xnT = sb("xnT", [C, T])
        stats = sb("stats", [P, NT, 6])
        mv = sb("mv", [P, NT, 2])
        rstd = sb("rstd", [P, NT])
        var_eps = sb("var_eps", [P, NT])
        minus_half = sb("minus_half", [P, NT])
        parts = sb("parts", [P, 2, 3, T], BF)
        Qs = sb("Qs", [ROWS_P2, HA, T], BF)
        Ks = sb("Ks", [ROWS_P2, HA, T], BF)
        Vs = sb("Vs", [P, NT, HA, DA + 1])
        nmaxA = sb("nmaxA", [P, HA, NT])
        nmb = sb("nmb", [P, 2, GA, NT], BF)
        mrowA = sb("mrowA", [2 * GA * NT, P], BF)
        PT = sb("PT", [P, 2, NA_B, 512])
        ySB = sb("ySB", [P, T])
        recA = sb("recA", [P, NT, GA])
        yN = sb("yN", [P, NT, C])
        yT = sb("yT", [C, T])
        res = sb("res", [P, NT, C])
        wqk_s = sb("wqk_s", [P, 2 * HF * DF])
        wgv_s = sb("wgv_s", [P, NG + NX])
        wo_s = sb("wo_s", [P, 3, C])
        stage = sb("stage", [P, 2, PAIRS, T])
        maskf = stage[:, 0, 0, 0:P]
        Qb = sb("Qb", [P, PAIRS, T], BF)
        Kb = sb("Kb", [P, PAIRS, T], BF)
        XQ = sb("XQ", [P, 2, GF, T], F32R)
        XK = sb("XK", [P, 2, GF, T], F32R)
        QM = sb("QM", [DF + 1, 2, GF, T], F32R)
        KL = sb("KL", [DF + 1, 2, GF, T], F32R)
        gate = sb("gate", [P, NT, 2 * HF, E])
        xv = sb("xv", [P, NT, NX])
        beaten_by = sb("beaten_by", [P, NT, 2 * HF, E], BF)
        pick = sb("pick", [P, NT, HF, E])
        wv_s = sb("wv_s", [P, NT, HF, E])
        Vf = sb("Vf", [P, NT, HF, DF])
        nmaxF = sb("nmaxF", [P, HF, NT])
        mrowF = sb("mrowF", [GF * NT, P], F32R)
        rotated = sb("rotated", [P, 2, T])
        rot, rot2 = rotated[:, 0, :], rotated[:, 1, :]
        cmp_ = rotated[:, :, :].rearrange("p a t -> p (a t)").bitcast(BF)[:, 0:NT * 2 * HF * E * E].rearrange(
            "p (g a b) -> p g a b", a=E, b=E)
        ones = sb("ones", [P, 32])
        dSB = sb("dSB", [P, T])
        denF = sb("denF", [P, NT, GF])
        recF = sb("recF", [P, NT, GF])
        wz = sb("wz", [P, NT, GF, E])
        Z = sb("Z", [P, NT, E, DF])
        ztmp = sb("ztmp", [P, 2, NT, E, DF])
        VBUF = 4
        vtmp = ztmp[:, :, :, :, :].rearrange("p b t e d -> p (b t e d)")[:, 0:VBUF * HF * DF].rearrange(
            "p (j h d) -> p j h d", j=VBUF, h=HF)
        ZT = parts[:, :, :, :].rearrange("p q c t -> p (q c t)").bitcast(F32).rearrange("p (c t) -> p c t", c=3)

        S1 = [pb("S1a"), pb("S1b"), pb("S1c")]
        S2 = [pb("S2a"), pb("S2b")]
        Y = pb("Y")
        M0, M1 = pb("M0"), pb("M1")

        M0_USES = ["denT2", "rows1", "den3",
                   "denT3", "rows2", "ZT1", "F out",
                   "rows3", "A xnT", "A qp",
                   "rows4", "A kp",
                   "rows5",
                   "A yNT", "rows6", "den0",
                   "denT0", "F xnT", "rows7", "F gate1", "F gate3", "den1", "F k0", "F k1",
                   "denT1", "rows0", "F k2", "den2", "F k3"]
        M1_USES = ["YT6",
                   "YT7", "ZT0", "ZT2",
                   "YT0", "A q",
                   "YT1", "A k",
                   "YT2",
                   "YT3", "A v", "A out",
                   "YT4", "F gate0", "F gate2", "F q0", "F q1",
                   "YT5", "F q2", "F q3"]

        N_BANKS = [NA_B] * SA + [NF_B] * SF
        NS = SA + SF
        STEPS = NA_B
        F_STEPS = [(6, 8), (6, 9), (7, 6), (7, 8)]
        V_STEPS = [(s, b) for s, bs in ((1, (8, 9)), (2, (1, 3, 5, 8)), (3, (0, 2, 4, 7)), (4, (0, 1, 3, 4, 5, 6, 7)),
                                        (5, (0, 1, 2)))
                   for b in bs]
        N1 = sum(N_BANKS)
        AHEAD = 2
        BEFORE2 = [sum(N_BANKS[:s]) for s in range(NS)]
        BEFORE1 = [sum(N_BANKS[i % NS] for i in range(AHEAD, AHEAD + s)) for s in range(NS)]

        m0_filled = Signal("m0_filled", len(M0_USES), times=LAST)
        m0_drained = Signal("m0_drained", len(M0_USES), times=LAST)
        m1_filled = Signal("m1_filled", len(M1_USES), times=LAST)
        m1_drained = Signal("m1_drained", len(M1_USES), times=LAST)
        s1_filled = Signal("s1_filled", N1, times=LAST)
        s1_drained = Signal("s1_drained", N1, times=LAST)
        s2_filled = Signal("s2_filled", N1, times=LAST)
        exps_done = Signal("exps_done", N1, times=LAST)
        y_filled = Signal("y_filled", NS, times=LAST)
        y_copied = Signal("y_copied", NS, times=LAST)
        NSET = 6
        consts_loaded = Signal("consts_loaded", NSET, 16)
        x_copied = Signal("x_copied", B, 16)
        consts_cast = Signal("consts_cast", 2)
        dve_init = Signal("dve_init", 8)
        xlA_loaded = Signal("xlA_loaded", 1, 16)
        xrA_loaded = Signal("xrA_loaded", 3, 16)
        xrF_loaded = Signal("xrF_loaded", 1, 16)
        resA_stored = Signal("resA_stored", 1, 16)
        resF_stored = Signal("resF_stored", 1, 16)
        wa_loaded = Signal("wa_loaded", 4, 16)
        scattered = Signal("scattered", 2 * NSP, 16)
        rowsA_in = Signal("rowsA_in", 2 * SA, 16)
        rowsF_in = Signal("rowsF_in", SF, 16)
        kb_cast = Signal("kb_cast", PAIRS)
        hi_ready = Signal("hi_ready", 2 * SF)
        low_ready = Signal("low_ready", 2 * SF)
        copies_in = Signal("copies_in", 4 * SF, 16)
        resA_ready = Signal("resA_ready", 1)
        resF_ready = Signal("resF_ready", 1)
        varA_ready = Signal("varA_ready", 1)
        varF_ready = Signal("varF_ready", 1)
        rstdA_ready = Signal("rstdA_ready", 1)
        rstdF_ready = Signal("rstdF_ready", 1)
        xnA_ready = Signal("xnA_ready", 1)
        xnF_ready = Signal("xnF_ready", 1)
        rot_ready = Signal("rot_ready", 2)
        part0_ready = Signal("part0_ready", 2)
        rest1_ready = Signal("rest1_ready", 2)
        part1_ready = Signal("part1_ready", 2)
        part2_ready = Signal("part2_ready", 2)
        nmb_ready = Signal("nmb_ready", SA)
        masked = Signal("masked", SA * NA_B)
        sig_e = Signal("sig_e", 1)
        v_mult = Signal("v_mult", NT * E)
        v_acc = Signal("v_acc", NT * (E - 1))
        z_mult = Signal("z_mult", HF)
        z_acc = Signal("z_acc", HF - 1)
        lnA_chain = Signal("lnA_chain", 2)
        lnF_chain = Signal("lnF_chain", 2)
        outA_chain = Signal("outA_chain", 1)
        maxA_chain = Signal("maxA_chain", SA)
        normA_chain = Signal("normA_chain", SA)
        pick_chain = Signal("pick_chain", 7)
        mix_chain = Signal("mix_chain", 2 * SF)

        def bank(use):
            return M0 if use in M0_USES else M1

        def is_full(use):
            return (m0_filled if use in M0_USES else m1_filled).sem

        def is_free(use):
            return (m0_drained if use in M0_USES else m1_drained).sem

        def filled(k, use, lag=0):
            uses, signal = (M0_USES, m0_filled) if use in M0_USES else (M1_USES, m1_filled)
            return signal.sem, signal.at(k, uses.index(use) + 1, lag)

        def drained(k, use, lag=0):
            uses, signal = (M0_USES, m0_drained) if use in M0_USES else (M1_USES, m1_drained)
            return signal.sem, signal.at(k, uses.index(use) + 1, lag)

        def free_for(k, use, lag=0):
            uses, signal = (M0_USES, m0_drained) if use in M0_USES else (M1_USES, m1_drained)
            return signal.sem, signal.at(k, uses.index(use), lag)

        ALL = dict(a=True, f=True, f_end=True, a_prep=True, f_prep=True)

        def parts_of(j):
            return dict(a=0 <= j - 1 < UNITS, f=0 <= j - 2 < UNITS, f_end=0 <= j - 3 < UNITS, a_prep=0 <= j < UNITS,
                        f_prep=0 <= j - 1 < UNITS)

        block = ctx.enter_context(nc.Block())

        @block.sync
        def _(sp):
            for s in (xlA_loaded, xrA_loaded, xrF_loaded, resA_stored, resF_stored, wa_loaded, scattered,
                      rowsA_in, rowsF_in, copies_in):
                sp.sem_inc(s.sem, s.first)
            for b in range(B):
                sp.dma_start(out[b], x[b]).then_inc(x_copied.sem, 16)
            sp.dma_start(ident[:, :], ident_in).then_inc(consts_loaded.sem, 16)
            sp.dma_start(maskf, mask_in).then_inc(consts_loaded.sem, 16)
            sp.dma_start(wqk_s[:, :], wqk).then_inc(consts_loaded.sem, 16)
            sp.dma_start(wgv_s[:, :], wgv).then_inc(consts_loaded.sem, 16)
            sp.dma_start(wo_s[:, 0:2, :], wo[0:256, :].rearrange("(c p) n -> p c n", p=P)).then_inc(consts_loaded.sem, 16)
            sp.dma_start(wo_s[0:NX - 256, 2, :], wo[256:NX, :]).then_inc(consts_loaded.sem, 16)
            sp.wait_ge(x_copied.sem, 16 * B)
            sp.wait_ge(dve_init.sem, dve_init.per)

            def stream(u):
                return out[u % B].rearrange("(t p) c -> p t c", p=P)

            def iteration(j, a, f, f_end, a_prep, f_prep):
                def rows(group):
                    sp.wait_ge(*drained(j, f"rows{group}"))
                    apart(sp)
                    if group < SA:
                        for i in range(2):
                            sp.dma_start(Qs[ROWS_P1 + i:ROWS_P1 + i + 1, GA * group:GA * group + GA, :],
                                         mrowA[i * GA * NT:(i + 1) * GA * NT, :]).then_inc(rowsA_in.sem, 16)
                    else:
                        g = group - SA
                        sp.dma_start(QM[DF:DF + 1, g % 2, :, :].bitcast(F32),
                                     mrowF[:, :].bitcast(F32)).then_inc(rowsF_in.sem, 16)

                def copies(g):
                    if not (f if g else f_prep):
                        return
                    for qk, (src, dst) in enumerate(((XQ, QM), (XK, XK))):
                        sp.wait_ge(hi_ready.sem, hi_ready.at(j, 2 * g + qk + 1, 2 if g else 1))
                        apart(sp)
                        for h in range(GF):
                            own = slice(DF * h, DF * h + DF)
                            to = slice(DF - DF * h, P - DF * h) if qk else slice(0, DF)
                            sp.dma_start(dst[to, g % 2, h, :].bitcast(F32),
                                         src[own, g % 2, h, :].bitcast(F32)).then_inc(copies_in.sem, 16)

                if f_end:
                    sp.wait_ge(resA_ready.sem, resA_ready.at(j, 1, 2))
                    apart(sp)
                    sp.dma_start(xr[:, :, :], stream(j - 3)).then_inc(xrF_loaded.sem, 16)
                if a:
                    rows(1)
                if a_prep:
                    sp.wait_ge(xnA_ready.sem, xnA_ready.at(j, 1, 1))
                    apart(sp)
                    sp.wait_ge(resF_stored.sem, resF_stored.at(j, 1, 4))
                    apart(sp)
                    sp.dma_start(xl[:, :, :], stream(j)).then_inc(xlA_loaded.sem, 16)
                    sp.wait_ge(*drained(j, "A v", 1))
                    apart(sp)
                    for dst, src in ((wa_s, wa), (ba_s, ba), (bv_s, bv), (tab_s, tab)):
                        dst = dst[:, :] if len(dst.shape) == 2 else dst[:, :, :]
                        sp.dma_start(dst, src[j // B]).then_inc(wa_loaded.sem, 16)
                copies(1)
                if a:
                    rows(2)
                if f_end:
                    sp.wait_ge(resF_ready.sem, resF_ready.at(j, 1, 3))
                    apart(sp)
                    sp.dma_start(stream(j - 3), res[:, :, :]).then_inc(resF_stored.sem, 16)
                if a:
                    sp.wait_ge(resF_ready.sem, resF_ready.at(j, 1, 3))
                    apart(sp)
                    sp.wait_ge(resA_ready.sem, resA_ready.at(j, 1, 2))
                    apart(sp)
                    sp.dma_start(xr[:, :, :], stream(j - 1)).then_inc(xrA_loaded.sem, 16)
                    sp.dma_start(wp_s[:, :], wp[(j - 1) // B]).then_inc(xrA_loaded.sem, 16)
                    sp.dma_start(bp_s[:, :], bp[(j - 1) // B]).then_inc(xrA_loaded.sem, 16)
                    rows(3)
                if f:
                    rows(4)
                if f:
                    rows(5)
                if a_prep:
                    sp.wait_ge(s2_filled.sem, s2_filled.at(j, BEFORE2[SA]))
                    apart(sp)
                    for qk, (dst, order) in enumerate(((Qs, SPLITS_Q), (Ks, SPLITS_K))):
                        sp.wait_ge(part2_ready.sem, part2_ready.at(j, qk + 1))
                        apart(sp)
                        for r in range(NSP):
                            sp.dma_start(dst[DA * r:DA * r + DA, :, :],
                                         parts[:, qk, order[r], :]).then_inc(scattered.sem, 16)
                copies(2)
                if f:
                    rows(6)
                if a:
                    sp.wait_ge(resA_ready.sem, resA_ready.at(j, 1, 1))
                    apart(sp)
                    sp.dma_start(stream(j - 1), res[:, :, :]).then_inc(resA_stored.sem, 16)
                copies(3)
                if f:
                    rows(7)
                copies(0)
                if a_prep:
                    rows(0)

            for j in range(HEAD):
                iteration(j, **parts_of(j))
            with sp.Fori(HEAD, UNITS) as j:
                iteration(j, **ALL)
            for j in range(UNITS, LAST):
                iteration(j, **parts_of(j))
            sp.wait_ge(resF_stored.sem, resF_stored.at(UNITS - 1, 1))

        @block.tensor
        def _(pe):
            for s in (m0_filled, m1_filled, s1_filled, s2_filled, y_filled):
                pe.sem_inc(s.sem, s.first)
            pe.wait_ge(consts_loaded.sem, 16 * NSET)
            pe.wait_ge(dve_init.sem, dve_init.per)
            pe.wait_ge(consts_cast.sem, consts_cast.per)

            def iteration(j, a, f, f_end, a_prep, f_prep):
                def skip(use):
                    pe.wait_ge(*free_for(j, use))
                    pe.sem_inc(is_full(use), 1)
                    pe.sem_inc(is_free(use), 1)

                def pass1(slot, b):
                    group, n = (slot + AHEAD) % NS, BEFORE1[slot] + b + 1
                    t = S1[(n - 1) % len(S1)]
                    if not (a if slot < 2 else f if slot < 6 else a_prep):
                        if b == 0:
                            pe.wait_ge(s1_drained.sem, s1_drained.at(j, n - 1))
                            pe.sem_inc(s1_filled.sem, N_BANKS[group])
                            pe.sem_inc(s1_drained.sem, N_BANKS[group])
                        return
                    if group == 0 and b == 0:
                        pe.wait_ge(scattered.sem, scattered.at(j, 2 * NSP))
                    if group == SA and b == 0:
                        pe.wait_ge(*drained(j, "F q3", 1))
                        pe.wait_ge(kb_cast.sem, kb_cast.at(j, PAIRS, 2))
                    pe.wait_ge(s1_drained.sem, s1_drained.at(j, n - len(S1)))
                    if group < SA:
                        for h, qt, col in BANKS_A1[b]:
                            hh, keys = GA * group + h, (qt + 1) * P
                            nc.tensor.matmul(t[:, col:col + keys], Qs[0:ROWS_P1, hh, qt * P:keys],
                                             Ks[0:ROWS_P1, hh, 0:keys], start=True, stop=False)
                            last = nc.tensor.matmul(t[:, col + qt * P:col + keys], identb[:, :], maskb[:, :],
                                                    start=False, stop=True)
                        last.then_inc(s1_filled.sem, 1)
                    else:
                        h, qt = divmod(b, NT)
                        lo, pair = DF * h, group - SA
                        nc.tensor.matmul(t[:, :], Qb[lo:lo + DF, pair, qt * P:qt * P + P], Kb[lo:lo + DF, pair, :],
                                         start=True, stop=True).then_inc(s1_filled.sem, 1)

                def pass2(slot, b):
                    n = BEFORE2[slot] + b + 1
                    t = S2[(n - 1) % len(S2)]
                    if not (a if slot < SA else f):
                        if b == 0:
                            pe.wait_ge(exps_done.sem, exps_done.at(j, n - 1))
                            pe.sem_inc(s2_filled.sem, N_BANKS[slot])
                            pe.sem_inc(exps_done.sem, N_BANKS[slot])
                        return
                    if b == 0 and slot < SA:
                        pe.wait_ge(rowsA_in.sem, rowsA_in.at(j, 2 * slot + 2, 1))
                    if b == 0 and slot >= SA:
                        pe.wait_ge(copies_in.sem, copies_in.at(j, 4 * (slot - SA + 1), 2))
                        pe.wait_ge(low_ready.sem, low_ready.at(j, 2 * (slot - SA + 1), 2))
                        pe.wait_ge(rowsF_in.sem, rowsF_in.at(j, slot - SA + 1, 2))
                    pe.wait_ge(exps_done.sem, exps_done.at(j, n - len(S2)))
                    if slot < SA:
                        for h, kt, col in BANKS_A2[b]:
                            hh = GA * slot + h
                            last = nc.tensor.matmul(t[:, col:col + T - kt * P], Ks[0:ROWS_P2, hh, kt * P:kt * P + P],
                                                    Qs[0:ROWS_P2, hh, kt * P:T], start=True, stop=True)
                        last.then_inc(s2_filled.sem, 1)
                    else:
                        h, kt = divmod(b, NT)
                        buf = (slot - SA) % 2
                        nc.tensor.matmul(t[:, :], XK[:, buf, h, kt * P:kt * P + P], XQ[:, buf, h, :],
                                         start=True, stop=False)
                        nc.tensor.matmul(t[:, :], KL[:, buf, h, kt * P:kt * P + P], QM[:, buf, h, :],
                                         start=False, stop=True).then_inc(s2_filled.sem, 1)

                def has_values(slot):
                    return f_end if slot == 0 else a if slot <= SA else f

                def values(slot, kt):
                    group = (slot - 1) % NS
                    if not has_values(slot):
                        if kt == 0:
                            pe.wait_ge(y_copied.sem, y_copied.at(j, slot))
                            pe.sem_inc(y_filled.sem, 1)
                            pe.sem_inc(y_copied.sem, 1)
                        return
                    if kt == 0:
                        pe.wait_ge(y_copied.sem, y_copied.at(j, slot))
                    if group < SA:
                        through = max(b for b in range(NA_B) if any(t <= kt for _, t, _ in BANKS_A2[b]))
                        pe.wait_ge(masked.sem, masked.at(j, NA_B * group + through + 1, 1))
                        if kt == 0:
                            if group == 0:
                                pe.wait_ge(*drained(j, "A v", 1))
                        for h in range(GA):
                            b, col = next((b, c) for b in range(NA_B) for hh, t, c in BANKS_A2[b] if (hh, t) == (h, kt))
                            last = nc.tensor.matmul(Y[32 * h:32 * h + DA + 1, kt * P:T], Vs[:, kt, GA * group + h, :],
                                                    PT[:, group % 2, b, col:col + T - kt * P],
                                                    start=(kt == 0), stop=(kt == NT - 1), tile_position=(0, 32 * h))
                    else:
                        if kt == 0:
                            pe.wait_ge(exps_done.sem, exps_done.at(j, BEFORE2[slot]))
                        if group == SA:
                            pe.wait_ge(v_acc.sem, v_acc.at(j, (E - 1) * (kt + 1), 2))
                        for h in range(GF):
                            last = nc.tensor.matmul(Y[DF * h:DF * h + DF, :], Vf[:, kt, GF * (group - SA) + h, :],
                                                    PT[:, group % 2, NT * h + kt, :],
                                                    start=(kt == 0), stop=(kt == NT - 1))
                    if kt == NT - 1:
                        last.then_inc(y_filled.sem, 1)

                def rows(group):
                    use = f"rows{group}"
                    if not (a_prep if group == 0 else a if group < SA else f):
                        return skip(use)
                    pe.wait_ge(*free_for(j, use))
                    t = bank(use)
                    if group < SA:
                        pe.wait_ge(nmb_ready.sem, nmb_ready.at(j, group + 1, 1 if group else 0))
                        nc.tensor.transpose(t[:, :].bitcast(BF)[0:2 * GA * NT, 0:P],
                                            nmb[:, :, :, :].rearrange("p j h t -> p (j h t)"),
                                            identb[:, :]).then_inc(is_full(use), 1)
                    else:
                        g = group - SA
                        pe.wait_ge(s1_drained.sem, s1_drained.at(j, BEFORE1[group - AHEAD + 1]))
                        nc.tensor.transpose(t[0:GF * NT, 0:P], nmaxF[:, GF * g:GF * g + GF, :].rearrange("p h t -> p (h t)"),
                                            ident[:, :]).then_inc(is_full(use), 1)

                def value_transposes(slot):
                    use = f"YT{(slot - 2) % NS}"
                    if not (f_end if slot < 2 else a if slot < 2 + SA else f):
                        return skip(use)
                    pe.wait_ge(y_copied.sem, y_copied.at(j, slot))
                    pe.wait_ge(*free_for(j, use))
                    t = bank(use)
                    for i in range(NT):
                        last = nc.tensor.transpose(t[:, i * P:(i + 1) * P], ySB[:, i * P:(i + 1) * P], ident[:, :])
                    last.then_inc(is_full(use), 1)

                def denominators(slot):
                    g = (slot - 1) % NS - SA
                    use = f"den{g}"
                    if not has_values(slot):
                        return skip(use)
                    pe.wait_ge(*free_for(j, use))
                    t = bank(use)
                    for kt in range(NT):
                        for h in range(GF):
                            lo = 32 * (2 * h + kt % 2)
                            last = nc.tensor.matmul(t[lo:lo + 32, :], ones[:, :], PT[:, (SA + g) % 2, NT * h + kt, :],
                                                    start=(kt < 2), stop=(kt >= 2), tile_position=(0, lo))
                    last.then_inc(is_full(use), 1)

                def denominator_transposes(slot):
                    g = (slot - 2) % NS - SA
                    use = f"denT{g}"
                    if not (f_end if slot < 2 else f):
                        return skip(use)
                    pe.wait_ge(*drained(j, f"den{g}", 0 if slot else 1))
                    pe.wait_ge(*free_for(j, use))
                    apart(pe)
                    t = bank(use)
                    for i in range(NT):
                        last = nc.tensor.transpose(t[:, i * P:(i + 1) * P], dSB[:, i * P:(i + 1) * P], ident[:, :])
                    last.then_inc(is_full(use), 1)

                def xn_transposes(use, has):
                    if not has:
                        return skip(use)
                    if use == "A xnT":
                        pe.wait_ge(xnA_ready.sem, xnA_ready.at(j, 1))
                    else:
                        pe.wait_ge(xnF_ready.sem, xnF_ready.at(j, 1, 1))
                    pe.wait_ge(*free_for(j, use))
                    t = bank(use)
                    for i in range(NT):
                        last = nc.tensor.transpose(t[:, i * P:(i + 1) * P], xn[:, i, :], ident[:, :])
                    last.then_inc(is_full(use), 1)

                def a_project(use):
                    if not a_prep:
                        return skip(use)
                    if use == "A q":
                        pe.wait_ge(wa_loaded.sem, wa_loaded.at(j, 4))
                        pe.wait_ge(*drained(j, "A xnT"))
                    pe.wait_ge(*free_for(j, use))
                    t = bank(use)
                    w = ("A q", "A qp", "A k", "A kp").index(use)
                    nc.tensor.matmul(t[:, :], wa_s[:, w, :], xnT[:, :], start=True, stop=True).then_inc(is_full(use), 1)

                def a_project_values():
                    if not a_prep:
                        return skip("A v")
                    pe.wait_ge(*free_for(j, "A v"))
                    t = bank("A v")
                    for i in range(NT):
                        last = nc.tensor.matmul(t[:, i * C:(i + 1) * C], xnT[:, i * P:(i + 1) * P], wa_s[:, 4, :],
                                                start=True, stop=True)
                    last.then_inc(is_full("A v"), 1)

                def a_y_transposes():
                    if not a:
                        return skip("A yNT")
                    pe.wait_ge(*drained(j, f"YT{SA - 1}"))
                    pe.wait_ge(*free_for(j, "A yNT"))
                    t = bank("A yNT")
                    for i in range(NT):
                        last = nc.tensor.transpose(t[:, i * P:(i + 1) * P], yN[:, i, :], ident[:, :])
                    last.then_inc(is_full("A yNT"), 1)

                def a_output():
                    if not a:
                        return skip("A out")
                    pe.wait_ge(xrA_loaded.sem, xrA_loaded.at(j, 3, 1))
                    pe.wait_ge(*drained(j, "A yNT"))
                    pe.wait_ge(*free_for(j, "A out"))
                    t = bank("A out")
                    for i in range(NT):
                        last = nc.tensor.matmul(t[:, i * C:(i + 1) * C], yT[:, i * P:(i + 1) * P], wp_s[:, :],
                                                start=True, stop=True)
                    last.then_inc(is_full("A out"), 1)

                def f_project(p):
                    for i, use in enumerate((f"F q{p}", f"F k{p}")):
                        if not f_prep:
                            skip(use)
                            continue
                        pe.wait_ge(*free_for(j, use))
                        t = bank(use)
                        w0 = i * HF * DF + p * P
                        nc.tensor.matmul(t[:, :], wqk_s[:, w0:w0 + P], xnT[:, :], start=True,
                                         stop=True).then_inc(is_full(use), 1)

                def f_gates(i):
                    use = f"F gate{i}"
                    if not f_prep:
                        return skip(use)
                    pe.wait_ge(*free_for(j, use))
                    if i == 0:
                        pe.wait_ge(*drained(j, "F xnT"))
                    t = bank(use)
                    nc.tensor.matmul(t[:, 0:NG + NX], xnT[:, i * P:(i + 1) * P], wgv_s[:, :],
                                     start=True, stop=True).then_inc(is_full(use), 1)

                def z_transposes(c):
                    use = f"ZT{c}"
                    if not f_end:
                        return skip(use)
                    if c == 0:
                        pe.wait_ge(z_acc.sem, z_acc.at(j, HF - 1, 3))
                    lo, hi = ZCH[c]
                    pe.wait_ge(*free_for(j, use))
                    apart(pe)
                    t = bank(use)
                    for i in range(NT):
                        zi = Z[:, i, :, :].rearrange("p e d -> p (e d)")
                        last = nc.tensor.transpose(t[0:hi - lo, i * P:(i + 1) * P], zi[:, lo:hi], ident[:, :])
                    last.then_inc(is_full(use), 1)

                def f_output():
                    if not f_end:
                        return skip("F out")
                    pe.wait_ge(*drained(j, "ZT2"))
                    pe.wait_ge(*drained(j, "ZT1"))
                    pe.wait_ge(*free_for(j, "F out"))
                    t = bank("F out")
                    for i in range(NT):
                        for c, (lo, hi) in enumerate(ZCH):
                            last = nc.tensor.matmul(t[:, i * C:(i + 1) * C], ZT[0:hi - lo, c, i * P:(i + 1) * P],
                                                    wo_s[0:hi - lo, c, :], start=(c == 0), stop=(c == 2))
                    last.then_inc(is_full("F out"), 1)

                for slot in range(NS):
                    for b in range(STEPS):
                        if b < N_BANKS[slot]:
                            pass2(slot, b)
                        if b < N_BANKS[(slot + AHEAD) % NS]:
                            pass1(slot, b)
                        if b % 2 == 1 and b < 2 * NT:
                            values(slot, b // 2)
                        at = (slot, b)
                        if b == 0:
                            value_transposes(slot)
                            if slot in (0, 1, 6, 7):
                                denominator_transposes(slot)
                        if at == (2, 4):
                            xn_transposes("A xnT", a_prep)
                        if at == (2, 6):
                            a_project("A q")
                        if at == (2, 7):
                            a_project("A qp")
                        if at == (3, 4):
                            a_project("A k")
                            a_project("A kp")
                        if at == (5, 3):
                            a_project_values()
                        if at == (5, 2):
                            a_y_transposes()
                        if at == (5, 4):
                            a_output()
                        if at == (6, 1):
                            xn_transposes("F xnT", f_prep)
                        if b == 3:
                            rows((slot + 1) % NS)
                        if b == 7 and slot in (0, 5, 6, 7):
                            denominators(slot)
                        if at == (6, 5):
                            f_gates(0)
                            f_gates(1)
                        if at == (6, 6):
                            f_gates(2)
                            f_gates(3)
                        if at in F_STEPS:
                            f_project(F_STEPS.index(at))
                        if at == (1, 9):
                            z_transposes(0)
                            z_transposes(1)
                            z_transposes(2)
                        if at == (2, 1):
                            f_output()

            for j in range(HEAD):
                iteration(j, **parts_of(j))
            with pe.Fori(HEAD, UNITS) as j:
                iteration(j, **ALL)
            for j in range(UNITS, LAST):
                iteration(j, **parts_of(j))

        @block.scalar
        def _(act):
            for s in (exps_done, y_copied, part0_ready, part1_ready, sig_e, hi_ready):
                act.sem_inc(s.sem, s.first)
            act.wait_ge(consts_loaded.sem, 16 * NSET)
            nc.scalar.activation(identb[:, :], ident[:, :], ACT.Copy).then_inc(consts_cast.sem, 1)
            nc.scalar.activation(maskb[:, :], maskf, ACT.Copy).then_inc(consts_cast.sem, 1)

            def iteration(j, a, f, f_end, a_prep, f_prep):
                def drain(use, dst, src):
                    act.wait_ge(*filled(j, use))
                    nc.scalar.activation(dst, src, ACT.Copy).then_inc(is_free(use), 1)

                def exps(slot, b):
                    n = BEFORE2[slot] + b + 1
                    if b == 0:
                        act.wait_ge(y_filled.sem, y_filled.at(j, slot))
                    act.wait_ge(s2_filled.sem, s2_filled.at(j, n))
                    nc.scalar.activation(PT[:, slot % 2, b, :], S2[(n - 1) % len(S2)][:, :], ACT.Exp,
                                         scale=SCALE_A if slot < SA else SCALE_F).then_inc(exps_done.sem, 1)

                def rows(group):
                    if not (a_prep if group == 0 else a if group < SA else f):
                        return
                    t = bank(f"rows{group}")
                    if group < SA:
                        act.wait_ge(rowsA_in.sem, rowsA_in.at(j, 2 * group, 1 if group else 0))
                        drain(f"rows{group}", mrowA[:, :], t[:, :].bitcast(BF)[0:2 * GA * NT, 0:P])
                    else:
                        act.wait_ge(rowsF_in.sem, rowsF_in.at(j, group - SA, 2))
                        drain(f"rows{group}", mrowF[:, :], t[0:GF * NT, 0:P])

                def part0(qk):
                    act.wait_ge(rot_ready.sem, rot_ready.at(j, qk + 1))
                    if qk == 0:
                        act.wait_ge(scattered.sem, scattered.at(j, 0))
                    nc.scalar.activation(parts[:, qk, 0, :], rot, ACT.Copy).then_inc(part0_ready.sem, 1)

                def part1(qk):
                    act.wait_ge(rest1_ready.sem, rest1_ready.at(j, qk + 1))
                    nc.scalar.activation(parts[:, qk, 1, :], rot2, ACT.Copy).then_inc(part1_ready.sem, 1)

                def f_stage(p):
                    act.wait_ge(low_ready.sem, low_ready.at(j, 2 * p + 2, 2))
                    for i, use in enumerate((f"F q{p}", f"F k{p}")):
                        act.wait_ge(*filled(j, use))
                        last = nc.scalar.activation(stage[:, i, p, :], bank(use)[:, :], ACT.Copy)
                        if i == 0:
                            last = nc.scalar.activation(Qb[:, p, :], bank(use)[:, :], ACT.Copy)
                        last.then_inc(is_free(use), 1)

                def high_parts(g, qk):
                    if qk == 0:
                        act.wait_ge(s2_filled.sem, s2_filled.at(j, BEFORE2[(7, 0, 5, 6)[g]]))
                    for h in range(GF):
                        own = slice(DF * h, DF * h + DF)
                        last = nc.scalar.activation((XQ, XK)[qk][own, g % 2, h, :], stage[own, qk, g, :], ACT.Copy)
                    last.then_inc(hi_ready.sem, 1)

                def f_gates(i):
                    use = f"F gate{i}"
                    if i == 0:
                        act.wait_ge(v_mult.sem, v_mult.at(j, v_mult.per, 2))
                    act.wait_ge(*filled(j, use))
                    nc.scalar.activation(gate[:, i, :, :].rearrange("p g e -> p (g e)"), bank(use)[:, 0:NG], ACT.Copy)
                    nc.scalar.activation(xv[:, i, :], bank(use)[:, NG:NG + NX], ACT.Copy).then_inc(is_free(use), 1)

                for slot in range(NS):
                    for b in range(STEPS):
                        if b < N_BANKS[slot] and (a if slot < SA else f):
                            exps(slot, b)
                        at = (slot, b)
                        if b == 8 and (f_end if slot == 0 else a if slot <= SA else f):
                            act.wait_ge(y_filled.sem, y_filled.at(j, slot + 1))
                            nc.scalar.activation(ySB[:, :], Y[:, :], ACT.Copy).then_inc(y_copied.sem, 1)
                        if slot in (5, 6) and b < 2 and f:
                            high_parts(slot - 3, b)
                        if at in ((0, 8), (0, 9)) and f:
                            high_parts(1, b - 8)
                        if at in ((7, 1), (7, 2)) and f_prep:
                            high_parts(0, b - 1)
                        if at == (5, 2) and a:
                            drain("A yNT", yT[:, :], bank("A yNT")[:, :])
                        if b == 3:
                            rows((slot + 1) % NS)
                        if b == 8 and (f_end if slot == 0 else f if slot > 4 else False):
                            use = f"den{(slot - 1) % NS - SA}"
                            drain(use, dSB[:, :], bank(use)[:, :])
                        if at == (2, 5) and a_prep:
                            act.wait_ge(*filled(j, "A v", 1))
                            act.wait_ge(*filled(j, "F k3", 1))
                            drain("A xnT", xnT[:, :], bank("A xnT")[:, :])
                        if at in ((2, 9), (3, 9)) and a_prep:
                            part0(slot - 2)
                        if at in ((3, 3), (4, 3)) and a_prep:
                            part1(slot - 3)
                        if at == (6, 1) and f_prep:
                            act.wait_ge(*filled(j, "A v"))
                            drain("F xnT", xnT[:, :], bank("F xnT")[:, :])
                        if at in F_STEPS and f_prep:
                            f_stage(F_STEPS.index(at))
                        if at == (6, 5) and f_prep:
                            f_gates(0)
                            f_gates(1)
                        if at == (6, 6) and f_prep:
                            f_gates(2)
                            f_gates(3)
                        if at == (1, 9) and f_end:
                            for c in range(3):
                                lo, hi = ZCH[c]
                                if c == 0:
                                    act.wait_ge(scattered.sem, scattered.at(j, 0))
                                drain(f"ZT{c}", ZT[0:hi - lo, c, :], bank(f"ZT{c}")[0:hi - lo, :])
                        if at == (6, 7) and f_prep:
                            act.wait_ge(*drained(j, "F gate2"))
                            act.wait_ge(*drained(j, "F gate3"))
                            nc.scalar.activation(wv_s[:, :, :, :].rearrange("p t h e -> p t (h e)"),
                                                 gate[:, :, 0:HF, :].rearrange("p t h e -> p t (h e)"),
                                                 ACT.Exp, scale=-1.0).then_inc(sig_e.sem, 1)

            for j in range(HEAD):
                iteration(j, **parts_of(j))
            with act.Fori(HEAD, UNITS) as j:
                iteration(j, **ALL)
            for j in range(UNITS, LAST):
                iteration(j, **parts_of(j))

        @block.vector
        def _(dve):
            for s in (m0_drained, m1_drained, s1_drained, resA_ready, resF_ready, varA_ready, varF_ready, xnA_ready,
                      xnF_ready, rot_ready, nmb_ready, v_mult, z_mult, lnA_chain, lnF_chain, maxA_chain,
                      normA_chain, pick_chain, mix_chain, low_ready, kb_cast):
                dve.sem_inc(s.sem, s.first)
            nc.vector.memset(Qs[:, :, :], 0.0).then_inc(dve_init.sem, 1)
            nc.vector.memset(Ks[:, :, :], 0.0).then_inc(dve_init.sem, 1)
            nc.vector.memset(Y[:, :], 0.0).then_inc(dve_init.sem, 1)
            nc.vector.memset(Vs[:, :, :, :], 1.0).then_inc(dve_init.sem, 1)
            nc.vector.memset(KL[DF:DF + 1, :, :, :].bitcast(F32), 1.0).then_inc(dve_init.sem, 1)
            nc.vector.memset(ones[:, :], 1.0).then_inc(dve_init.sem, 1)
            nc.vector.memset(minus_half[:, :], -0.5).then_inc(dve_init.sem, 1)
            dve.wait_ge(dve_init.sem, 2)
            nc.vector.memset(Ks[ROWS_P1:ROWS_P2, :, :], 1.0).then_inc(dve_init.sem, 1)
            dve.wait_ge(dve_init.sem, dve_init.per)

            def iteration(j, a, f, f_end, a_prep, f_prep):
                def variances(src, chain, var_ready, lag):
                    for i in range(NT):
                        last = nc.vector.bn_stats(stats[:, i, :], src[:, i, :])
                    last.then_inc(chain.sem, 1)
                    dve.wait_ge(chain.sem, chain.at(j, 1, lag))
                    apart(dve)
                    for i in range(NT):
                        last = nc.vector.bn_aggr(mv[:, i, :], stats[:, i, :])
                    last.then_inc(chain.sem, 1)
                    dve.wait_ge(chain.sem, chain.at(j, 2, lag))
                    nc.vector.tensor_scalar(var_eps[:, :], mv[:, :, 1], EPS, None, ALU.add).then_inc(var_ready.sem, 1)

                def normalise(src, rstd_ready, xn_ready, lag):
                    dve.wait_ge(rstd_ready.sem, rstd_ready.at(j, 1, lag))
                    for i in range(NT):
                        last = nc.vector.tensor_scalar(xn[:, i, :], src[:, i, :], mv[:, i, 0:1], rstd[:, i:i + 1],
                                                       ALU.subtract, ALU.mult)
                    last.then_inc(xn_ready.sem, 1)

                def rotate(qk, half):
                    use = (("A q", "A qp"), ("A k", "A kp"))[qk][half]
                    if qk == 0 and half == 0:
                        dve.wait_ge(wa_loaded.sem, wa_loaded.at(j, 4))
                    if qk and half == 0:
                        dve.wait_ge(part2_ready.sem, part2_ready.at(j, 1))
                    dve.wait_ge(*filled(j, use))
                    nc.vector.scalar_tensor_tensor((rot, rot2)[half], bank(use)[:, :],
                                                   ba_s[:, 2 * qk + half:2 * qk + half + 1], tab_s[:, half, :],
                                                   ALU.add, ALU.mult).then_inc(is_free(use), 1)
                    if half:
                        for use in (("A q", "A qp"), ("A k", "A kp"))[qk]:
                            dve.wait_ge(*drained(j, use))
                        nc.vector.tensor_tensor(rot, rot, rot2, ALU.add).then_inc(rot_ready.sem, 1)

                def a_values():
                    dve.wait_ge(y_filled.sem, y_filled.at(j, SA + 1))
                    dve.wait_ge(*filled(j, "A v"))
                    nc.vector.tensor_tensor(
                        Vs[:, :, :, 0:DA], bank("A v")[:, :].rearrange("p (t h d) -> p t h d", t=NT, h=HA),
                        bv_s[:, :].rearrange("p (h d) -> p h d", h=HA).unsqueeze(1).broadcast_to([P, NT, HA, DA]),
                        ALU.add).then_inc(is_free("A v"), 1)

                def maxima(slot, b):
                    group, n = (slot + AHEAD) % NS, BEFORE1[slot] + b + 1
                    dve.wait_ge(s1_filled.sem, s1_filled.at(j, n))
                    t = S1[(n - 1) % len(S1)]
                    if group < SA:
                        segs = BANKS_A1[b]
                        h0, qt0, _ = segs[0]
                        if len(segs) == 2 and segs[1][1] == qt0:
                            last = nc.vector.tensor_reduce(nmaxA[:, GA * group + h0:GA * group + h0 + 2, qt0],
                                                           t[:, :].rearrange("p (h k) -> p h k", h=2), AX.X, ALU.max,
                                                           negate=True)
                        else:
                            for h, qt, col in segs:
                                last = nc.vector.tensor_reduce(nmaxA[:, GA * group + h, qt:qt + 1],
                                                               t[:, col:col + (qt + 1) * P], AX.X, ALU.max, negate=True)
                        last.then_inc(s1_drained.sem, 1)
                    else:
                        h, qt = divmod(b, NT)
                        nc.vector.tensor_reduce(nmaxF[:, GF * (group - SA) + h, qt:qt + 1], t[:, :], AX.X, ALU.max,
                                                negate=True).then_inc(s1_drained.sem, 1)

                def split_maxima(group, lag):
                    slot = (group - AHEAD) % NS
                    n = BEFORE1[slot] + NA_B
                    dve.wait_ge(s1_drained.sem, s1_drained.at(j, n, 1 if group == 1 else 0))
                    before = (group - 1) % SA
                    dve.wait_ge(*filled(j, f"rows{before}", 1 if group == 1 else 0))
                    src = nmaxA[:, GA * group:GA * group + GA, :]
                    nc.vector.tensor_copy(nmb[:, 0, :, :], src).then_inc(maxA_chain.sem, 1)
                    dve.wait_ge(maxA_chain.sem, maxA_chain.at(j, group + 1, lag))
                    nc.vector.tensor_tensor(nmb[:, 1, :, :], src, nmb[:, 0, :, :], ALU.subtract).then_inc(nmb_ready.sem, 1)

                def a_norm(g):
                    dve.wait_ge(*filled(j, f"YT{g}"))
                    v = bank(f"YT{g}")[:, :].rearrange("p (t h r) -> p t h r", t=NT, h=GA)
                    nc.vector.reciprocal(recA[:, :, :], v[:, :, :, DA]).then_inc(normA_chain.sem, 1)
                    dve.wait_ge(normA_chain.sem, normA_chain.at(j, g + 1, 1))
                    nc.vector.tensor_tensor(
                        yN[:, :, GA * DA * g:GA * DA * (g + 1)].rearrange("p t (h d) -> p t h d", h=GA), v[:, :, :, 0:DA],
                        recA[:, :, :].unsqueeze(3).broadcast_to([P, NT, GA, DA]),
                        ALU.mult).then_inc(is_free(f"YT{g}"), 1)

                def a_output():
                    dve.wait_ge(outA_chain.sem, outA_chain.at(j, 1, 1))
                    dve.wait_ge(*filled(j, "A out"))
                    flat = res[:, :, :].rearrange("p t c -> p (t c)")
                    nc.vector.tensor_tensor(flat, bank("A out")[:, :], flat, ALU.add).then_inc(resA_ready.sem, 1)
                    dve.wait_ge(resA_ready.sem, resA_ready.at(j, 1, 1))
                    dve.sem_inc(is_free("A out"), 1)

                def low_part(g, qk):
                    dve.wait_ge(hi_ready.sem, hi_ready.at(j, 2 * g + qk + 1, 2 if g else 1))
                    for h in range(GF):
                        own = slice(DF * h, DF * h + DF)
                        to = slice(0, DF) if qk else slice(DF - DF * h, P - DF * h)
                        last = nc.vector.tensor_tensor((XQ, KL)[qk][to, g % 2, h, :], stage[own, qk, g, :],
                                                       (XQ, XK)[qk][own, g % 2, h, :], ALU.subtract)
                    last.then_inc(low_ready.sem, 1)

                def f_cast(p):
                    dve.wait_ge(*drained(j, f"F k{p}"))
                    nc.vector.tensor_copy(Kb[:, p, :], stage[:, 1, p, :]).then_inc(kb_cast.sem, 1)

                def f_compare(e):
                    if e == 0:
                        dve.wait_ge(*drained(j, "F gate2"))
                        dve.wait_ge(*drained(j, "F gate3"))
                    gl = gate[:, :, :, :].rearrange("p t g e -> p (t g) e")
                    n_gl = NT * 2 * HF
                    last = nc.vector.tensor_tensor(cmp_[:, :, 0:e + 1, e], gl[:, :, e:e + 1].broadcast_to([P, n_gl, e + 1]),
                                                   gl[:, :, 0:e + 1], ALU.is_gt)
                    if e < E - 1:
                        last = nc.vector.tensor_tensor(cmp_[:, :, e + 1:E, e],
                                                       gl[:, :, e:e + 1].broadcast_to([P, n_gl, E - 1 - e]),
                                                       gl[:, :, e + 1:E], ALU.is_ge)
                    else:
                        last.then_inc(pick_chain.sem, 1)

                def f_count(half):
                    dve.wait_ge(pick_chain.sem, pick_chain.at(j, 1, 1))
                    n = NT * HF
                    by = beaten_by[:, :, :, :].rearrange("p t g e -> p (t g) e")
                    with nc.allow_low_precision(reason="counts of at most 4 are exact in bfloat16"):
                        nc.vector.tensor_reduce(by[:, n * half:n * half + n, :], cmp_[:, n * half:n * half + n, :, :],
                                                AX.X, ALU.add).then_inc(pick_chain.sem, 1)

                def f_sigmoid(step):
                    wv2 = wv_s[:, :, :, :].rearrange("p t h e -> p (t h e)")
                    if step == 0:
                        dve.wait_ge(sig_e.sem, sig_e.at(j, 1, 1))
                        nc.vector.tensor_scalar(wv2, wv2, 1.0, None, ALU.add).then_inc(pick_chain.sem, 1)
                    if step == 1:
                        dve.wait_ge(pick_chain.sem, pick_chain.at(j, 4, 1))
                        nc.vector.reciprocal(wv2, wv2).then_inc(pick_chain.sem, 1)
                    if step == 2:
                        dve.wait_ge(pick_chain.sem, pick_chain.at(j, 5, 1))
                        nc.vector.scalar_tensor_tensor(wv_s[:, :, :, :].rearrange("p t h e -> p t (h e)"),
                                                       beaten_by[:, :, 0:HF, :].rearrange("p t h e -> p t (h e)"), 1.5,
                                                       wv_s[:, :, :, :].rearrange("p t h e -> p t (h e)"),
                                                       ALU.is_lt, ALU.mult).then_inc(pick_chain.sem, 1)

                def f_pick():
                    dve.wait_ge(pick_chain.sem, pick_chain.at(j, 6, 2))
                    nc.vector.tensor_scalar(pick[:, :, :, :].rearrange("p t h e -> p t (h e)"),
                                            beaten_by[:, :, HF:2 * HF, :].rearrange("p t h e -> p t (h e)"), 1.5, None,
                                            ALU.is_lt).then_inc(pick_chain.sem, 1)

                def f_value_product(i, e):
                    if i == 0 and e == 0:
                        dve.wait_ge(pick_chain.sem, pick_chain.at(j, 7, 2))
                        dve.wait_ge(y_filled.sem, y_filled.at(j, 1))
                    if i == 0 and e == 1:
                        dve.wait_ge(z_acc.sem, z_acc.at(j, HF - 1, 3))
                    n = i * (E - 1) + e
                    if e and n > VBUF:
                        dve.wait_ge(v_acc.sem, v_acc.at(j, n - VBUF, 2))
                    nc.vector.tensor_tensor(
                        vtmp[:, n % VBUF, :, :] if e else Vf[:, i, :, :],
                        xv[:, i:i + 1, e * DF:(e + 1) * DF].broadcast_to([P, HF, DF]),
                        wv_s[:, i, :, e:e + 1].broadcast_to([P, HF, DF]), ALU.mult).then_inc(v_mult.sem, 1)

                def f_mix_weights(slot):
                    g, lag = (slot - 2) % NS - SA, 3 if slot < 2 else 2
                    dve.wait_ge(*filled(j, f"denT{g}"))
                    v = bank(f"denT{g}")[:, :].rearrange("p (t h k r) -> p t h k r", t=NT, h=GF, k=2)
                    nc.vector.tensor_reduce(denF[:, :, :], v[:, :, :, :, 0], AX.X, ALU.add).then_inc(is_free(f"denT{g}"), 1)
                    dve.wait_ge(*drained(j, f"denT{g}"))
                    nc.vector.reciprocal(recF[:, :, :], denF[:, :, :]).then_inc(mix_chain.sem, 1)
                    dve.wait_ge(mix_chain.sem, mix_chain.at(j, 2 * g + 1, lag))
                    nc.vector.tensor_tensor(wz[:, :, :, :], pick[:, :, GF * g:GF * g + GF, :],
                                            recF[:, :, :].unsqueeze(3).broadcast_to([P, NT, GF, E]),
                                            ALU.mult).then_inc(mix_chain.sem, 1)

                def f_mix(g, h, lag):
                    if h == 0:
                        dve.wait_ge(mix_chain.sem, mix_chain.at(j, 2 * g + 2, lag))
                        dve.wait_ge(*filled(j, f"YT{SA + g}"))
                    y = bank(f"YT{SA + g}")[:, :].rearrange("p (t h d) -> p t h d", t=NT, h=GF)
                    hh = GF * g + h
                    if hh == 1:
                        dve.wait_ge(v_acc.sem, v_acc.at(j, v_acc.per, lag))
                    if hh > 2:
                        dve.wait_ge(z_acc.sem, z_acc.at(j, hh - 2, lag))
                    nc.vector.tensor_tensor(ztmp[:, hh % 2, :, :, :] if hh else Z[:, :, :, :],
                                            y[:, :, h:h + 1, :].broadcast_to([P, NT, E, DF]),
                                            wz[:, :, h, :].unsqueeze(3).broadcast_to([P, NT, E, DF]),
                                            ALU.mult).then_inc(z_mult.sem, 1)
                    if h == GF - 1:
                        dve.wait_ge(z_mult.sem, z_mult.at(j, GF * g + GF, lag))
                        dve.sem_inc(is_free(f"YT{SA + g}"), 1)

                def f_output():
                    dve.wait_ge(xrF_loaded.sem, xrF_loaded.at(j, 1, 3))
                    dve.wait_ge(resA_stored.sem, resA_stored.at(j, 1, 2))
                    dve.wait_ge(*filled(j, "F out"))
                    nc.vector.tensor_tensor(res[:, :, :].rearrange("p t c -> p (t c)"), bank("F out")[:, :],
                                            xr[:, :, :].rearrange("p t c -> p (t c)"), ALU.add).then_inc(resF_ready.sem, 1)
                    dve.wait_ge(resF_ready.sem, resF_ready.at(j, 1, 3))
                    dve.sem_inc(is_free("F out"), 1)

                for slot in range(NS):
                    nxt = (slot + 1) % NS
                    if nxt < SA and (a if nxt else a_prep):
                        split_maxima(nxt, 1 if nxt else 0)
                    for b in range(STEPS):
                        if b < N_BANKS[(slot + AHEAD) % NS] and (a if slot < 2 else f if slot < 6 else a_prep):
                            maxima(slot, b)
                        at = (slot, b)
                        if b in (1, 3) and slot in (0, 1, 6, 7) and (f if slot > 1 else f_end):
                            if b == 1:
                                f_mix_weights(slot)
                            f_mix((slot - 2) % NS - SA, b // 2, 3 if slot < 2 else 2)
                        if at in ((5, 4), (5, 6), (6, 1), (6, 3)) and f:
                            low_part(slot - 3, ((5, 4), (5, 6), (6, 1), (6, 3)).index(at) % 2)
                        if at in ((1, 0), (1, 2)) and f:
                            low_part(1, b // 2)
                        if at in ((7, 5), (7, 6)) and f_prep:
                            low_part(0, b - 5)
                        if at == (1, 6) and a_prep:
                            dve.wait_ge(xlA_loaded.sem, xlA_loaded.at(j, 1))
                            variances(xl, lnA_chain, varA_ready, 0)
                        if at in ((2, 6), (2, 7), (3, 5), (3, 6)) and a_prep:
                            rotate(*divmod(((2, 6), (2, 7), (3, 5), (3, 6)).index(at), 2))
                        if at == (1, 9) and a_prep:
                            normalise(xl, rstdA_ready, xnA_ready, 0)
                        if at == (5, 9) and f_prep:
                            normalise(res, rstdF_ready, xnF_ready, 1)
                        if at == (5, 3) and a_prep:
                            a_values()
                        if at == (5, 5) and a:
                            a_output()
                        if at in ((6, 7), (6, 8)) and f_prep:
                            for e in ((0, 1), (2, 3, 4))[b - 7]:
                                f_compare(e)
                        if at in ((6, 9), (7, 0)) and f_prep:
                            f_count(slot - 6)
                        if at in ((7, 1), (7, 2), (7, 4)) and f_prep:
                            f_sigmoid((1, 2, 4).index(b))
                        if at in ((6, 9), (7, 3), (7, 8), (7, 9)) and f_prep:
                            f_cast(((6, 9), (7, 3), (7, 8), (7, 9)).index(at))
                        if at == (1, 5) and f:
                            f_pick()
                        if at in V_STEPS and f:
                            f_value_product(*divmod(V_STEPS.index(at), E))
                        if at == (2, 1) and f_end:
                            f_output()
                        if at == (5, 7) and f_prep:
                            variances(res, lnF_chain, varF_ready, 1)
                        if b == 0 and 2 <= slot < 2 + SA and a:
                            a_norm(slot - 2)

            for j in range(HEAD):
                iteration(j, **parts_of(j))
            with dve.Fori(HEAD, UNITS) as j:
                iteration(j, **ALL)
            for j in range(UNITS, LAST):
                iteration(j, **parts_of(j))

        @block.gpsimd
        def _(pool):
            for s in (rstdA_ready, rstdF_ready, outA_chain, rest1_ready, part2_ready, masked, v_acc, z_acc):
                pool.sem_inc(s.sem, s.first)
            pool.wait_ge(dve_init.sem, dve_init.per)

            def iteration(j, a, f, f_end, a_prep, f_prep):
                def mask(slot, b):
                    pool.wait_ge(exps_done.sem, exps_done.at(j, BEFORE2[slot] + b + 1))
                    apart(pool)
                    tiles = PT[:, slot % 2, b, :].rearrange("p (k c) -> p k c", c=P)
                    if len(BANKS_A2[b]) == 2:
                        v, pattern = tiles[:, 0::BANKS_A2[b][1][2] // P, :], [[0, 2], [1, P]]
                    else:
                        v, pattern = tiles[:, 0, :], [[1, P]]
                    last = nc.gpsimd.affine_select(out=v, in_=v, compare_op=ALU.is_ge, fill=0.0, base=0,
                                                   pattern=pattern, channel_multiplier=-1)
                    last.then_inc(masked.sem, 1)

                def deviations(var_ready, rstd_ready, lag):
                    pool.wait_ge(var_ready.sem, var_ready.at(j, 1, lag))
                    nc.gpsimd.tensor_tensor(rstd[:, :], var_eps[:, :], minus_half[:, :], ALU.pow).then_inc(rstd_ready.sem, 1)

                def rest1(qk):
                    pool.wait_ge(part0_ready.sem, part0_ready.at(j, qk + 1))
                    nc.gpsimd.tensor_tensor(rot2, rot, parts[:, qk, 0, :], ALU.subtract).then_inc(rest1_ready.sem, 1)

                def part2(qk):
                    pool.wait_ge(part1_ready.sem, part1_ready.at(j, qk + 1))
                    nc.gpsimd.tensor_tensor(parts[:, qk, 2, :], rot2, parts[:, qk, 1, :],
                                            ALU.subtract).then_inc(part2_ready.sem, 1)

                def f_value_sum(i, e):
                    if e == 0:
                        return
                    n = i * (E - 1) + e
                    pool.wait_ge(v_mult.sem, v_mult.at(j, i * E + e + 1, 2))
                    if n > 1:
                        pool.wait_ge(v_acc.sem, v_acc.at(j, n - 1, 2))
                    nc.gpsimd.tensor_tensor(Vf[:, i, :, :], Vf[:, i, :, :], vtmp[:, n % VBUF, :, :],
                                            ALU.add).then_inc(v_acc.sem, 1)

                def f_mix(g, h, lag):
                    hh = GF * g + h
                    if hh:
                        pool.wait_ge(z_mult.sem, z_mult.at(j, hh + 1, lag))
                        if hh > 1:
                            pool.wait_ge(z_acc.sem, z_acc.at(j, hh - 1, lag))
                        nc.gpsimd.tensor_tensor(Z[:, :, :, :], Z[:, :, :, :], ztmp[:, hh % 2, :, :, :],
                                                ALU.add).then_inc(z_acc.sem, 1)

                for slot in range(NS):
                    for b in range(STEPS):
                        if slot < SA and a:
                            mask(slot, b)
                        at = (slot, b)
                        if at == (1, 6) and a_prep:
                            deviations(varA_ready, rstdA_ready, 0)
                        if at in ((2, 9), (3, 9)) and a_prep:
                            rest1(slot - 2)
                        if at in ((3, 3), (4, 3)) and a_prep:
                            part2(slot - 3)
                        if at == (4, 8) and a:
                            pool.wait_ge(xrA_loaded.sem, xrA_loaded.at(j, 3, 1))
                            pool.wait_ge(resF_stored.sem, resF_stored.at(j, 1, 3))
                            nc.gpsimd.tensor_tensor(res[:, :, :], xr[:, :, :],
                                                    bp_s[:, :].unsqueeze(1).broadcast_to([P, NT, C]),
                                                    ALU.add).then_inc(outA_chain.sem, 1)
                        if at in V_STEPS and f:
                            f_value_sum(*divmod(V_STEPS.index(at), E))
                        if at == (5, 7) and f_prep:
                            deviations(varF_ready, rstdF_ready, 1)
                        if b in (2, 4) and slot in (0, 1, 6, 7) and (f if slot > 1 else f_end):
                            f_mix((slot - 2) % NS - SA, b // 2 - 1, 3 if slot < 2 else 2)

            for j in range(HEAD):
                iteration(j, **parts_of(j))
            with pool.Fori(HEAD, UNITS) as j:
                iteration(j, **ALL)
            for j in range(UNITS, LAST):
                iteration(j, **parts_of(j))


def kernel(L0_attn_a_x, L0_attn_a_wq, L0_attn_a_bq, L0_attn_a_wk, L0_attn_a_bk, L0_attn_a_wv, L0_attn_a_bv, L0_attn_a_wp,
           L0_attn_a_bp, L0_attn_b_W_attn, L0_attn_b_b_attn, L0_attn_b_W_proj, L0_attn_b_b_proj, L0_ffn_Wq, L0_ffn_Wk,
           L0_ffn_Ws, L0_ffn_Wd, L0_ffn_Wv, L0_ffn_Wo):
    import concourse.bacc as bacc
    from concourse.bass_utils import run_bass_kernel_spmd

    x = np.ascontiguousarray(L0_attn_a_x)
    B, T, C = x.shape
    H, D = 16, C // 16
    plain = [h * D + d for d in range(D) for h in range(H)]
    swapped = [h * D + (d + D // 2) % D for d in range(D) for h in range(H)]

    def layout(wq, wk, wv, wp, bq, bk, bv, bp):
        w = np.stack([wq[:, plain], wq[:, swapped], wk[:, plain], wk[:, swapped], wv], 1)
        b = np.stack([bq[plain], bq[swapped], bk[plain], bk[swapped]], 1)
        return w, wp, b, np.broadcast_to(bv, (C, C)), np.broadcast_to(bp, (C, C))

    a = layout(*(np.asarray(w).T for w in (L0_attn_a_wq, L0_attn_a_wk, L0_attn_a_wv, L0_attn_a_wp)),
               *(np.asarray(b) for b in (L0_attn_a_bq, L0_attn_a_bk, L0_attn_a_bv, L0_attn_a_bp)))
    Wb, bb = np.asarray(L0_attn_b_W_attn), np.asarray(L0_attn_b_b_attn)
    b = layout(Wb[:, :C], Wb[:, C:2 * C], Wb[:, 2 * C:], np.asarray(L0_attn_b_W_proj), bb[:C], bb[C:2 * C], bb[2 * C:],
               np.asarray(L0_attn_b_b_proj))

    half = D // 2
    i = np.arange(half, dtype=np.float32)
    f32 = np.float32
    ang_a = np.arange(T, dtype=f32)[None] * (f32(1.0) / f32(10000.0) ** (f32(2.0) * i / f32(D)))[:, None]
    ang_b = np.arange(T, dtype=f32)[None] / (f32(1250.0) ** (f32(2.0) * i / f32(D)))[:, None]
    tabs = []
    for ang in (ang_a, ang_b):
        cos, sin = np.cos(ang), np.sin(ang)
        tabs.append(np.stack([np.repeat(np.concatenate([cos, cos]), H, 0), np.repeat(np.concatenate([-sin, sin]), H, 0)], 1))

    Wv, Wo = np.asarray(L0_ffn_Wv), np.asarray(L0_ffn_Wo)
    E, _, DH = Wv.shape
    HE = L0_ffn_Ws.shape[1]
    arrays = {
        "x": x,
        "wa": np.stack([a[0], b[0]]),
        "wp": np.stack([a[1], b[1]]),
        "ba": np.stack([a[2], b[2]]),
        "bv": np.stack([a[3], b[3]]),
        "bp": np.stack([a[4], b[4]]),
        "tab": np.stack(tabs).astype(np.float32),
        "wqk": np.concatenate([np.asarray(L0_ffn_Wq), np.asarray(L0_ffn_Wk)], 1),
        "wgv": np.concatenate([np.asarray(L0_ffn_Ws), np.asarray(L0_ffn_Wd), Wv.transpose(1, 0, 2).reshape(C, E * DH)], 1),
        "wo": Wo.reshape(E * DH, C),
        "ident": np.eye(128, dtype=np.float32),
        "mask": np.triu(np.full((128, 128), -1e30, np.float32), 1),
    }
    arrays = {n: np.ascontiguousarray(v) for n, v in arrays.items()}
    nc = bacc.Bacc("TRN2", target_bir_lowering=False, num_devices=1)
    args = [nc.dram_tensor(f"in_{n}", v.shape, mybir.dt.from_np(v.dtype), kind="ExternalInput").ap()
            for n, v in arrays.items()]
    args.append(nc.dram_tensor("out_x", (B, T, C), mybir.dt.float32, kind="ExternalOutput").ap())
    attention_and_mixture(nc, *args)
    r = run_bass_kernel_spmd(nc, [{f"in_{n}": v for n, v in arrays.items()}], core_ids=[0])
    return r.results[0]["out_x"]
```
